# Optimizing a Trainium2 kernel written in Bass

```python
import numpy as np
import jax
import jax.numpy as jnp

def _softmax(x, axis=-1):
    return jax.nn.softmax(x, axis=axis)

def _gelu(x):
    return jax.nn.gelu(x, approximate=True)

def _silu(x):
    return jax.nn.silu(x)

def _sigmoid(x):
    return jax.nn.sigmoid(x)

def _layernorm(x, axis=-1, eps=1e-05):
    m = jnp.mean(x, axis=axis, keepdims=True)
    v = jnp.var(x, axis=axis, keepdims=True)
    return (x - m) / jnp.sqrt(v + eps)

def _scatter_add(tgt, idx, src, axis=0):
    return tgt.at[idx].add(src)

def _segment_sum(src, seg, n):
    return jax.ops.segment_sum(src, seg, n)
kernel_name = 'mk_xattn_ffn_d1_seqx_r2_d08bfd'

def setup_inputs(seed: int=0):
    np.random.seed(seed)
    _w = jnp.asarray

    def _rec_inputs():
        import jax
        import jax.numpy as jnp
        _rk = jax.random.key(seed)
        x = -0.0002928 + 1 * jax.random.normal(jax.random.fold_in(_rk, 1), (4, 1024, 512), jnp.float32)
        _lenS = 1024 - jax.random.randint(jax.random.fold_in(_rk, 7), (4,), 0, max(1, 1024 // 4) + 1, jnp.int32)
        _lenS2 = 2048 - jax.random.randint(jax.random.fold_in(_rk, 8), (4,), 0, max(1, 2048 // 4) + 1, jnp.int32)
        _ctx_1024P = jax.random.normal(jax.random.fold_in(_rk, 11), (4, 16, 512), jnp.float32)
        _ctx_1024c = jax.random.dirichlet(jax.random.fold_in(_rk, 511), 0.3 * jnp.ones((16,), jnp.float32), (4, 2048))
        _ctx_1024t = jnp.einsum('bsk,bkd->bsd', _ctx_1024c, _ctx_1024P)
        _ctx_1024t = _ctx_1024t * jax.lax.rsqrt(jnp.mean(jnp.square(_ctx_1024t)) + 1e-12) * 0.953939
        ctx_1024 = -1.39393e-06 + 0.999914 * (_ctx_1024t + 0.3 * jax.random.normal(jax.random.fold_in(_rk, 611), (4, 2048, 512), jnp.float32))
        _validS = jnp.arange(1024)[None, :] < _lenS[:, None]
        _validS2 = jnp.arange(2048)[None, :] < _lenS2[:, None]
        _causal = jnp.tril(jnp.ones((1024, 1024), dtype=bool))
        mask_BxSxS2_bf1 = jnp.ones((4, 1024, 2048), dtype=bool)
        return (x, ctx_1024, mask_BxSxS2_bf1)
    x, ctx_1024, mask_BxSxS2_bf1 = _rec_inputs()

    def _L0_xattn_setup():
        import jax, jax.numpy as jnp
        import numpy as np
        DIM = 512
        HEAD_DIM = 64
        NUM_HEADS = DIM // HEAD_DIM
        SCALE = HEAD_DIM ** (-0.5)
        key = jax.random.key(seed)
        k_x, k_ctx, k_wq, k_wkv, k_wo = jax.random.split(key, 5)
        B, N, M = (2, 1024, 1024)
        x = jax.random.normal(k_x, (B, N, DIM), dtype=jnp.float32)
        context = jax.random.normal(k_ctx, (B, M, DIM), dtype=jnp.float32)
        mask = jnp.ones((B, N, M), dtype=bool)
        s = DIM ** (-0.5)
        Wq = jax.random.normal(k_wq, (DIM, DIM), dtype=jnp.float32) * s
        Wkv = jax.random.normal(k_wkv, (DIM, 2 * DIM), dtype=jnp.float32) * s
        Wo = jax.random.normal(k_wo, (DIM, DIM), dtype=jnp.float32) * s
        return {'x': x, 'context': context, 'mask': mask, 'Wq': Wq, 'Wkv': Wkv, 'Wo': Wo}
    _L0_xattn_all = _L0_xattn_setup()
    _L0_xattn_in = {k: v for k, v in _L0_xattn_all.items() if k in ('Wq', 'Wkv', 'Wo')}
    del _L0_xattn_all

    def _L0_ffn_setup():
        import jax, jax.numpy as jnp
        import numpy as np
        NUM_HEAVY = 512
        N_ITERS = 50
        FETCH_K_RATIO = 9.0 / 8.0
        EPS = 1.0

        def rmsnorm(x, gamma):
            scale = gamma.shape[0] ** 0.5
            normed = x / jnp.maximum(jnp.linalg.norm(x, axis=-1, keepdims=True), 1e-12)
            return normed * scale * gamma

        def feedforward(x, gamma, w1, b1, w2, b2):
            h = rmsnorm(x, gamma)
            h = jax.nn.gelu(h @ w1.T + b1, approximate=False)
            return h @ w2.T + b2

        def coor_descent(s, n_iters, k, eps):
            logk = jnp.log(jnp.asarray(k, s.dtype))
            a0 = jnp.zeros_like(s[..., :1])
            b0 = -s

            def body(carry, _):
                a, b = carry
                a = eps * (logk - jax.nn.logsumexp((s + b) / eps, axis=-1, keepdims=True))
                b = -jax.nn.relu(s + a)
                return ((a, b), None)
            (a, b), _ = jax.lax.scan(body, (a0, b0), None, length=n_iters)
            return jnp.exp((s + a + b) / eps)
        key = jax.random.key(seed)
        ks = jax.random.split(key, 12)
        b, n, dim = (8, 4096, 512)
        d_light, d_heavy = (int(dim * 0.5), dim * 4)

        def lin(k, dout, din):
            bound = 1.0 / np.sqrt(din)
            k1, k2 = jax.random.split(k)
            w = jax.random.uniform(k1, (dout, din), jnp.float32, -bound, bound)
            bb = jax.random.uniform(k2, (dout,), jnp.float32, -bound, bound)
            return (w, bb)
        x = jax.random.normal(ks[0], (b, n, dim), jnp.float32)
        routing_token = jax.random.normal(ks[1], (dim,), jnp.float32)
        w1_l, b1_l = lin(ks[2], d_light, dim)
        w2_l, b2_l = lin(ks[3], dim, d_light)
        w1_h, b1_h = lin(ks[4], d_heavy, dim)
        w2_h, b2_h = lin(ks[5], dim, d_heavy)
        return dict(x=x, routing_token=routing_token, gamma_l=jnp.ones((dim,), jnp.float32), w1_l=w1_l, b1_l=b1_l, w2_l=w2_l, b2_l=b2_l, gamma_h=jnp.ones((dim,), jnp.float32), w1_h=w1_h, b1_h=b1_h, w2_h=w2_h, b2_h=b2_h)
    _L0_ffn_all = _L0_ffn_setup()
    _L0_ffn_in = {k: v for k, v in _L0_ffn_all.items() if k in ('routing_token', 'gamma_l', 'w1_l', 'b1_l', 'w2_l', 'b2_l', 'gamma_h', 'w1_h', 'b1_h', 'w2_h', 'b2_h')}
    del _L0_ffn_all
    return {'x': x, 'ctx_1024': ctx_1024, 'mask_BxSxS2_bf1': mask_BxSxS2_bf1, 'L0_xattn_Wq': _L0_xattn_in['Wq'], 'L0_xattn_Wkv': _L0_xattn_in['Wkv'], 'L0_xattn_Wo': _L0_xattn_in['Wo'], 'L0_ffn_routing_token': _L0_ffn_in['routing_token'], 'L0_ffn_gamma_l': _L0_ffn_in['gamma_l'], 'L0_ffn_w1_l': _L0_ffn_in['w1_l'], 'L0_ffn_b1_l': _L0_ffn_in['b1_l'], 'L0_ffn_w2_l': _L0_ffn_in['w2_l'], 'L0_ffn_b2_l': _L0_ffn_in['b2_l'], 'L0_ffn_gamma_h': _L0_ffn_in['gamma_h'], 'L0_ffn_w1_h': _L0_ffn_in['w1_h'], 'L0_ffn_b1_h': _L0_ffn_in['b1_h'], 'L0_ffn_w2_h': _L0_ffn_in['w2_h'], 'L0_ffn_b2_h': _L0_ffn_in['b2_h']}

def reference(x, ctx_1024, mask_BxSxS2_bf1, L0_xattn_Wq, L0_xattn_Wkv, L0_xattn_Wo, L0_ffn_routing_token, L0_ffn_gamma_l, L0_ffn_w1_l, L0_ffn_b1_l, L0_ffn_w2_l, L0_ffn_b2_l, L0_ffn_gamma_h, L0_ffn_w1_h, L0_ffn_b1_h, L0_ffn_w2_h, L0_ffn_b2_h):
    import jax
    import jax.numpy as jnp

    def _L0_xattn_ref(x, context, mask, Wq, Wkv, Wo):
        import jax, jax.numpy as jnp
        import numpy as np
        DIM = 512
        HEAD_DIM = 64
        NUM_HEADS = DIM // HEAD_DIM
        SCALE = HEAD_DIM ** (-0.5)
        B, N, C = x.shape
        M = context.shape[1]
        H, D = (NUM_HEADS, HEAD_DIM)
        q = (x @ Wq).reshape(B, N, H, D).transpose(0, 2, 1, 3)
        kv = (context @ Wkv).reshape(B, M, 2, H, D).transpose(2, 0, 3, 1, 4)
        k, v = (kv[0], kv[1])
        attn = jnp.einsum('bhnd,bhmd->bhnm', q, k) * SCALE
        attn = jnp.where(mask[:, None, :, :], attn, -jnp.inf)
        attn = jax.nn.softmax(attn, axis=-1)
        out = jnp.einsum('bhnm,bhmd->bhnd', attn, v)
        out = out.transpose(0, 2, 1, 3).reshape(B, N, C)
        return out @ Wo

    def _L0_ffn_ref(x, routing_token, gamma_l, w1_l, b1_l, w2_l, b2_l, gamma_h, w1_h, b1_h, w2_h, b2_h):
        import jax, jax.numpy as jnp
        import numpy as np
        NUM_HEAVY = 512
        N_ITERS = 50
        FETCH_K_RATIO = 9.0 / 8.0
        EPS = 1.0

        def rmsnorm(x, gamma):
            scale = gamma.shape[0] ** 0.5
            normed = x / jnp.maximum(jnp.linalg.norm(x, axis=-1, keepdims=True), 1e-12)
            return normed * scale * gamma

        def feedforward(x, gamma, w1, b1, w2, b2):
            h = rmsnorm(x, gamma)
            h = jax.nn.gelu(h @ w1.T + b1, approximate=False)
            return h @ w2.T + b2

        def coor_descent(s, n_iters, k, eps):
            logk = jnp.log(jnp.asarray(k, s.dtype))
            a0 = jnp.zeros_like(s[..., :1])
            b0 = -s

            def body(carry, _):
                a, b = carry
                a = eps * (logk - jax.nn.logsumexp((s + b) / eps, axis=-1, keepdims=True))
                b = -jax.nn.relu(s + a)
                return ((a, b), None)
            (a, b), _ = jax.lax.scan(body, (a0, b0), None, length=n_iters)
            return jnp.exp((s + a + b) / eps)
        b, n, dim = x.shape
        light_out = feedforward(x, gamma_l, w1_l, b1_l, w2_l, b2_l)
        s = jnp.einsum('bnd,d->bn', x, routing_token)
        effective_k = min(NUM_HEAVY * FETCH_K_RATIO, n)
        scores = coor_descent(s, N_ITERS, effective_k, EPS)
        selected_scores, selected_indices = jax.lax.top_k(scores, NUM_HEAVY)
        selected_scores = selected_scores + jax.lax.stop_gradient(1.0 - selected_scores)
        routed = jnp.take_along_axis(x, selected_indices[..., None], axis=1)
        routed_out = feedforward(routed, gamma_h, w1_h, b1_h, w2_h, b2_h)
        routed_out = routed_out * selected_scores[..., None]
        batch_range = jnp.arange(b)[:, None]
        heavy_out = jnp.zeros_like(x).at[batch_range, selected_indices].set(routed_out)
        return light_out + heavy_out
    x = x + _L0_xattn_ref(_layernorm(x, axis=-1), ctx_1024, mask_BxSxS2_bf1, L0_xattn_Wq, L0_xattn_Wkv, L0_xattn_Wo)
    x = x + _L0_ffn_ref(_layernorm(x, axis=-1), L0_ffn_routing_token, L0_ffn_gamma_l, L0_ffn_w1_l, L0_ffn_b1_l, L0_ffn_w2_l, L0_ffn_b2_l, L0_ffn_gamma_h, L0_ffn_w1_h, L0_ffn_b1_h, L0_ffn_w2_h, L0_ffn_b2_h)
    return x

_drawn_inputs = setup_inputs


def setup_inputs(seed=0):
    import zlib

    import numpy as np

    out = dict(_drawn_inputs(seed))
    spreads = {'L0_ffn_gamma_l': (1.0, 0.2), 'L0_ffn_gamma_h': (1.0, 0.6)}
    factors = {'L0_ffn_b1_l': 6.972, 'L0_ffn_b1_h': 8.0, 'L0_ffn_b2_h': 7.536}
    for name, (base, spread) in spreads.items():
        noise = np.random.default_rng([zlib.crc32(name.encode()), seed]).standard_normal(out[name].shape)
        drawn = base * np.exp(spread * noise) if base else spread * noise
        out[name] = jnp.asarray(drawn.astype(out[name].dtype))
    for name, factor in factors.items():
        out[name] = (out[name] * factor).astype(out[name].dtype)
    return out
```

```python
from contextlib import ExitStack

import concourse.bass as bass
import numpy as np
from concourse import mybir

F32 = mybir.dt.float32
F32R = mybir.dt.float32r
BF16 = mybir.dt.bfloat16
U8 = mybir.dt.uint8
I32 = mybir.dt.int32
ALU = mybir.AluOpType
ACT = mybir.ActivationFunctionType
AX = mybir.AxisListType

P = 128
B, N, M, D = 4, 1024, 2048, 512
H, HD = 8, 64
KT = D // P
HALF = 4
HALVES = H // HALF
HC = HALF * HD
CH = 512
SCALE = HD ** -0.5
EPS = 1e-5
ITERS = 50
CHOSEN = 512
EFFECTIVE_K = min(CHOSEN * 9.0 / 8.0, N)
TOK = B * N
FL = 256
FH = 2048
BIG = 3.4028235e38


def f32(ap):
    return ap.bitcast(F32)


def rows_by_tile(ap, k):
    return ap.rearrange("(k p) n -> p k n", k=k)


def free_from_the_start(eng, *rings):
    for sem, slots in rings:
        eng.sem_inc(sem, slots)


def wait_alone(eng, passed, sem, value):
    eng.wait_ge(sem, value)
    eng.sem_inc(passed, 1)


def products(pe, out, pairs, last=True):
    for n, (w, m) in enumerate(pairs):
        ins = pe.matmul(out, w, m, start=(n == 0), stop=last and n == len(pairs) - 1,
                        skip_group_check=True)
    return ins


def prepare(nc, x, wq, wkv, xnT, w_split, consts):
    eps, ident = consts["eps"], consts["ident"]
    with ExitStack() as ctx:
        sb = lambda name, shape, dt=F32: ctx.enter_context(nc.sbuf_tensor(name, shape, dt))
        sem = lambda name: ctx.enter_context(nc.semaphore(name))
        xin = sb("a_xin", [P, 2, 4, D])
        xn = sb("a_xn", [P, 2, 4, D])
        xt = sb("a_xt", [P, 2, KT, CH])
        stats = sb("a_stats", [P, 4, 6])
        mv = sb("a_mv", [P, 4, 2])
        sd = sb("a_sd", [P, 4])
        rstd = sb("a_rstd", [P, 4])
        wraw = sb("a_wraw", [P, HALVES, KT, 3, HC])
        whi = sb("a_whi", [P, HALVES, KT, 3, HC], F32R)
        wlo = sb("a_wlo", [P, HALVES, KT, 3, HC], F32R)
        ps = ctx.enter_context(nc.psum_tensor("a_ps", [P, 8, CH], F32))

        x_loaded = [sem(f"a_x_loaded{i}") for i in range(2)]
        w_loaded = sem("a_w_loaded")
        w_hi = sem("a_w_hi")
        w_lo = sem("a_w_lo")
        w_stored = sem("a_w_stored")
        passed = sem("a_passed")
        stats_done = sem("a_stats_done")
        mv_done = sem("a_mv_done")
        sd_done = sem("a_sd_done")
        rstd_done = sem("a_rstd_done")
        normed = sem("a_normed")
        turned = sem("a_turned")
        copied = sem("a_copied")
        xt_stored = [sem(f"a_xt_stored{i}") for i in range(2)]
        ident_zero = sem("a_ident_zero")
        ident_ready = sem("a_ident_ready")
        eps_ready = sem("a_eps_ready")

        x_rows = x.rearrange("b n d -> (b n) d")
        block = ctx.enter_context(nc.Block())

        @block.gpsimd
        def _(pool):
            free_from_the_start(pool, (normed, 2), (turned, 2 * KT), (copied, 2 * KT),
                                (xt_stored[0], 16), (xt_stored[1], 16))
            pool.memset(ident[:, :], 0.0).then_inc(ident_zero, 1)
            pool.memset(eps[:, :], EPS).then_inc(eps_ready, 1)
            pool.wait_ge(ident_zero, 1)
            pool.affine_select(out=ident[:, :], in_=ident[:, :], compare_op=ALU.not_equal, fill=1.0,
                               base=0, pattern=[[-1, P]], channel_multiplier=1).then_inc(ident_ready, 1)

        @block.sync
        def _(sp):
            for h in range(HALVES):
                for n, w in enumerate((wq[:, h * HC:(h + 1) * HC], wkv[:, h * HC:(h + 1) * HC],
                                       wkv[:, D + h * HC:D + (h + 1) * HC])):
                    sp.dma_start(wraw[:, h, :, n, :], rows_by_tile(w, KT)).then_inc(w_loaded, 16)
            with sp.Fori(0, TOK // CH // 2) as i:
                for u in range(2):
                    c = i * 2 + u
                    sp.wait_ge(normed, c + 1)
                    sp.dma_start(xin[:, u, :, :], x_rows[bass.ds(c * CH, CH), :].rearrange(
                        "(t p) d -> p t d", p=P)).then_inc(x_loaded[u], 16)
                for u in range(2):
                    c = i * 2 + u
                    wait_alone(sp, passed, copied, 2 * KT + c * KT + KT)
                    sp.dma_start(rows_by_tile(xnT[:, bass.ds(c * CH, CH)], KT),
                                 xt[:, u, :, :]).then_inc(xt_stored[u], 16)
            sp.wait_ge(w_lo, HALVES)
            for h in range(HALVES):
                sp.dma_start(w_split[h, 0], f32(whi[:, h].rearrange("p k a n -> p (k a n)"))).then_inc(w_stored, 16)
                sp.dma_start(w_split[h, 1], f32(wlo[:, h].rearrange("p k a n -> p (k a n)"))).then_inc(w_stored, 16)
            sp.wait_ge(w_stored, 16 * 2 * HALVES)
            for u in range(2):
                sp.wait_ge(xt_stored[u], 16 + 16 * (TOK // CH // 2))

        @block.vector
        def _(dve):
            with dve.Fori(0, TOK // CH // 2) as i:
                for u in range(2):
                    c = i * 2 + u
                    dve.wait_ge(x_loaded[u], (i + 1) * 16)
                    for t in range(4):
                        last = dve.bn_stats(out=stats[:, t, :], in_=xin[:, u, t, :])
                    last.then_inc(stats_done, 1)
                    wait_alone(dve, passed, stats_done, c + 1)
                    for t in range(4):
                        last = dve.bn_aggr(out=mv[:, t, :], in_=stats[:, t, :])
                    last.then_inc(mv_done, 1)
                    dve.wait_ge(sd_done, c + 1)
                    dve.reciprocal(rstd[:, :], sd[:, :]).then_inc(rstd_done, 1)
                    dve.wait_ge(rstd_done, c + 1)
                    dve.wait_ge(turned, c * KT + KT)
                    for t in range(4):
                        last = dve.tensor_scalar(xn[:, u, t, :], xin[:, u, t, :], mv[:, t, 0:1],
                                                 rstd[:, t:t + 1], ALU.subtract, ALU.mult)
                    last.then_inc(normed, 1)
            dve.wait_ge(w_hi, HALVES)
            for h in range(HALVES):
                dve.tensor_tensor(wlo[:, h], wraw[:, h], f32(whi[:, h]), ALU.subtract).then_inc(w_lo, 1)

        @block.tensor
        def _(pe):
            pe.wait_ge(ident_ready, 1)
            with pe.Fori(0, TOK // CH // 2) as i:
                for u in range(2):
                    c = i * 2 + u
                    pe.wait_ge(normed, 2 + c + 1)
                    for k in range(KT):
                        if k == 0:
                            pe.wait_ge(copied, c * KT + KT)
                        for t in range(4):
                            last = pe.transpose(ps[:, 4 * u + k, t * P:(t + 1) * P],
                                                xn[:, u, t, k * P:(k + 1) * P], ident[:, :])
                        last.then_inc(turned, 1)

        @block.scalar
        def _(act):
            act.wait_ge(eps_ready, 1)
            act.wait_ge(w_loaded, 16 * 3 * HALVES)
            for h in range(HALVES):
                act.activation(whi[:, h], wraw[:, h], ACT.Copy).then_inc(w_hi, 1)
            with act.Fori(0, TOK // CH // 2) as i:
                for u in range(2):
                    c = i * 2 + u
                    act.wait_ge(mv_done, c + 1)
                    act.activation(sd[:, :], mv[:, :, 1], ACT.Sqrt, bias=eps[:, :]).then_inc(sd_done, 1)
                    for k in range(KT):
                        act.wait_ge(turned, 2 * KT + c * KT + k + 1)
                        if k == 0:
                            act.wait_ge(xt_stored[u], i * 16 + 16)
                        act.activation(xt[:, u, k, :], ps[:, 4 * u + k, :], ACT.Copy).then_inc(copied, 1)


NB = 256
BLOCKS = N // NB * HALF
NT = NB // P
STEPS = M // P // 2
CTX_CHUNKS, X_CHUNKS = M // CH, N // CH
CHUNKS = CTX_CHUNKS + X_CHUNKS
TILES = 4 * CTX_CHUNKS + 2 * X_CHUNKS
G = BLOCKS * STEPS
QK_AT = {0: 0, 1: 1, 3: 2, 4: 3}
MAX_AT = {1: 0, 2: 1, 4: 2, 5: 3}
EXP_AT = {3: 0, 5: 1, 6: 2, 7: 3}
LAG = 2
RING = 4


def tiles_to(c):
    return 4 * min(c, CTX_CHUNKS) + 2 * max(c - CTX_CHUNKS, 0)


def attend(nc, ctxT, mask, xnT, w_split, attT, r_row, consts):
    ident = consts["ident"]
    with ExitStack() as ctx:
        def sb(name, shape, dt=F32, stack=ctx):
            return stack.enter_context(nc.sbuf_tensor(name, shape, dt))

        def sem(name):
            return ctx.enter_context(nc.semaphore("b_" + name))

        ks = sb("b_ks", [P, HALF, M], F32R)
        vs = sb("b_vs", [P, M // P, HALF, P], F32R)
        qhi = sb("b_qhi", [P, HALF, N], F32R)
        qlo = sb("b_qlo", [P, HALF, N], F32R)
        pthi = sb("b_pthi", [P, RING, 2 * NB], F32R)
        ptlo = sb("b_ptlo", [P, RING, 2 * NB], F32R)
        whi = sb("b_whi", [P, KT, 3, HC], F32R)
        wlo = sb("b_wlo", [P, KT, 3, HC], F32R)
        raw = sb("b_raw", [P, KT, CH])
        mask_in = sb("b_mask_in", [P, NT, M], U8)
        mask_add = sb("b_mask_add", [P, 2 * NT, M], BF16)
        lowest = sb("b_lowest", [P, 2 * NT, 2])
        sums = sb("b_sums", [P, 2 * NT, 2])
        total = sb("b_total", [P, NT])
        recip = sb("b_recip", [P, 2, NT])
        o_both = sb("b_o_both", [HD, 2, 2, NB])
        r_all = sb("b_r_all", [HD, 2, NB])
        o_sum = sb("b_o_sum", [HD, 2, NB])
        o_out = sb("b_o_out", [HD, 2, NB])
        with ExitStack() as first:
            probs = sb("b_probs", [P, 2 * NT, M], F32, first)
        with ExitStack() as second:
            xhi = sb("b_xhi", [P, 2, KT, CH], F32R, second)
            xlo = sb("b_xlo", [P, 2, KT, CH], F32R, second)
        ps = ctx.enter_context(nc.psum_tensor("b_ps", [P, 8, CH], F32))
        SB, TB, OB = 0, 4, 6

        const_ready = sem("const_ready")
        passed = sem("passed")
        w_loaded, raw_loaded = sem("w_loaded"), sem("raw_loaded")
        x_hi, x_lo = sem("x_hi"), sem("x_lo")
        tile_done = sem("tile_done")
        tile_hi, tile_lo = sem("tile_hi"), sem("tile_lo")
        scored = sem("scored")
        maxed = sem("maxed")
        exped = sem("exped")
        turned = sem("turned")
        pt_hi, pt_lo = sem("pt_hi"), sem("pt_lo")
        pv_done = sem("pv_done")
        totalled, inverted = sem("totalled"), sem("inverted")
        r_out = [sem(f"r_out{i}") for i in range(2)]
        r_in = [sem(f"r_in{i}") for i in range(2)]
        o_copied = sem("o_copied")
        o_summed = sem("o_summed")
        o_scaled = sem("o_scaled")
        o_stored = [sem(f"o_stored{i}") for i in range(2)]
        mask_loaded = [sem(f"mask_loaded{i}") for i in range(NT)]
        mask_made = sem("mask_made")
        block = ctx.enter_context(nc.Block())

        QK = 4 * BLOCKS

        def split_hi(act, it, c, tile):
            for n in range(4 if c < CTX_CHUNKS else 2):
                act.wait_ge(tile_done, 4 + it * TILES + tile + 1)
                bank = ps[:, SB + tile % 4, :]
                if c < CTX_CHUNKS and n < 2:
                    for a in range(2):
                        last = act.activation(ks[0:HD, 2 * n + a, c * CH:(c + 1) * CH],
                                              bank[a * HD:(a + 1) * HD, :], ACT.Copy)
                elif c < CTX_CHUNKS:
                    t = 4 * c + 2 * (n - 2)
                    last = act.activation(vs[:, t:t + 2, :, 0:HD],
                                          bank.rearrange("p (t h d) -> p t h d", t=2, h=HALF), ACT.Copy)
                else:
                    for a in range(2):
                        for twice in range(2):
                            col = (c - CTX_CHUNKS) * CH
                            last = act.activation(qhi[twice * HD:(twice + 1) * HD, 2 * n + a, col:col + CH],
                                                  bank[a * HD:(a + 1) * HD, :], ACT.Copy)
                last.then_inc(tile_hi, 1)
                tile += 1
            return tile

        def split_lo(dve, it, c, tile):
            for n in range(4 if c < CTX_CHUNKS else 2):
                dve.wait_ge(tile_hi, 4 + it * TILES + tile + 1)
                bank = ps[:, SB + tile % 4, :]
                if c < CTX_CHUNKS and n < 2:
                    for a in range(2):
                        cols = slice(c * CH, (c + 1) * CH)
                        last = dve.tensor_tensor(ks[HD:P, 2 * n + a, cols], bank[a * HD:(a + 1) * HD, :],
                                                 f32(ks[0:HD, 2 * n + a, cols]), ALU.subtract)
                elif c < CTX_CHUNKS:
                    t = 4 * c + 2 * (n - 2)
                    last = dve.tensor_tensor(vs[:, t:t + 2, :, HD:P],
                                             bank.rearrange("p (t h d) -> p t h d", t=2, h=HALF),
                                             f32(vs[:, t:t + 2, :, 0:HD]), ALU.subtract)
                else:
                    for a in range(2):
                        for twice in range(2):
                            cols = slice((c - CTX_CHUNKS) * CH, (c - CTX_CHUNKS + 1) * CH)
                            last = dve.tensor_tensor(qlo[twice * HD:(twice + 1) * HD, 2 * n + a, cols],
                                                     bank[a * HD:(a + 1) * HD, :],
                                                     f32(qhi[0:HD, 2 * n + a, cols]), ALU.subtract)
                last.then_inc(tile_lo, 1)
                tile += 1
            return tile

        @block.sync
        def _(sp):
            def load_chunk(b, it, c):
                sp.wait_ge(x_lo, it * CHUNKS + c + 1)
                if c < CTX_CHUNKS:
                    src = ctxT[bass.ds(b, 1), :, c * CH:(c + 1) * CH].rearrange("a (k p) m -> p (a k) m", p=P)
                else:
                    src = rows_by_tile(xnT[:, bass.ds(b * N + (c - CTX_CHUNKS) * CH, CH)], KT)
                sp.dma_start(raw[:, :, :], src).then_inc(raw_loaded, 16)

            def load_mask(b, it, nb, nt):
                wait_alone(sp, passed, mask_made, it * NT * 4 + (nb - 1) * NT + nt + 1 + NT)
                row = nb * NB + nt * P
                sp.dma_start(mask_in[:, nt, :], mask[bass.ds(b, 1), row:row + P, :].rearrange(
                    "a p m -> p (a m)")).then_inc(mask_loaded[nt], 16)

            with sp.Fori(0, B) as b:
                with sp.Fori(0, HALVES) as half:
                    it = b * HALVES + half
                    sp.wait_ge(tile_done, 4 + it * TILES)
                    sp.dma_start(f32(whi[:, :, :, :].rearrange("p k a n -> p (k a n)")),
                                 w_split[bass.ds(half, 1), 0].rearrange("a p n -> p (a n)")).then_inc(w_loaded, 16)
                    sp.dma_start(f32(wlo[:, :, :, :].rearrange("p k a n -> p (k a n)")),
                                 w_split[bass.ds(half, 1), 1].rearrange("a p n -> p (a n)")).then_inc(w_loaded, 16)
                    load_chunk(b, it, 0)
                    for nt in range(NT):
                        load_mask(b, it, 0, nt)
                    for c in range(1, CHUNKS):
                        load_chunk(b, it, c)
                    for j in range(BLOCKS):
                        if j // HALF < 3 and j % HALF < NT:
                            load_mask(b, it, j // HALF + 1, j % HALF)
                        sp.wait_ge(inverted, it * BLOCKS + j + 1)
                        sp.dma_start(r_row[j % 2].rearrange("(p t) -> p t", p=P),
                                     recip[:, j % 2, :]).then_inc(r_out[j % 2], 16)
                        sp.wait_ge(r_out[j % 2], 16 + it * 8 * 16 + j // 2 * 16 + 16)
                        sp.wait_ge(o_scaled, it * BLOCKS + j + 1)
                        sp.dma_start(r_all[:, j % 2, :], r_row[j % 2:j % 2 + 1, :].partition_broadcast(HD)
                                     ).then_inc(r_in[j % 2], 16)

        @block.gpsimd
        def _(pool):
            free_from_the_start(pool, (x_lo, 1), (tile_done, 4), (tile_hi, 4), (tile_lo, 4), (maxed, 2),
                                (turned, 2), (pt_hi, 2), (pt_lo, 2), (pv_done, RING), (o_copied, 2),
                                (o_scaled, 2), (mask_made, NT), (r_out[0], 16), (r_out[1], 16))
            pool.sem_inc(const_ready, 1)

            def make_mask(it, nb, nt):
                pool.wait_ge(mask_loaded[nt], it * 4 * 16 + nb * 16 + 16)
                wait_alone(pool, passed, maxed, 2 + it * QK + max(nb - 1, 0) * HALF * 4)
                pool.tensor_scalar(mask_add[:, nb % 2 * NT + nt, :], mask_in[:, nt, :], -1.0, BIG,
                                   ALU.add, ALU.mult).then_inc(mask_made, 1)

            with pool.Fori(0, B) as b:
                with pool.Fori(0, HALVES) as half:
                    it = b * HALVES + half
                    for nt in range(NT):
                        make_mask(it, 0, nt)
                    for j in range(BLOCKS):
                        nb, h, s = j // HALF, j % HALF, j % 2
                        pool.wait_ge(o_copied, 2 + it * BLOCKS + j + 1)
                        pool.tensor_tensor(o_sum[:, s, :], o_both[:, s, 0, :], o_both[:, s, 1, :],
                                           ALU.add).then_inc(o_summed, 1)
                        pool.wait_ge(r_in[s], it * 8 * 16 + j // 2 * 16 + 16)
                        if j >= 2:
                            pool.wait_ge(o_stored[s], it * 8 * 16 + j // 2 * 16)
                        pool.wait_ge(o_summed, it * BLOCKS + j + 1)
                        pool.tensor_tensor(o_out[:, s, :].rearrange("d (t p) -> d t p", t=NT),
                                           o_sum[:, s, :].rearrange("d (t p) -> d t p", t=NT),
                                           r_all[:, s, :].rearrange("d (p t) -> d t p", t=NT),
                                           ALU.mult).then_inc(o_scaled, 1)
                        wait_alone(pool, passed, o_scaled, 2 + it * BLOCKS + j + 1)
                        pool.dma_start(attT[bass.ds(half * HC + h * HD, HD), bass.ds(b * N + nb * NB, NB)],
                                       o_out[:, s, :]).then_inc(o_stored[s], 16)
                        if nb < 3 and h < NT:
                            make_mask(it, nb + 1, h)
                    for s in range(2):
                        pool.wait_ge(o_stored[s], it * 8 * 16 + 8 * 16)

        @block.scalar
        def _(act):
            act.wait_ge(const_ready, 1)

            def exp(it, j, e):
                nt, c = e // 2, e % 2
                s = j % 2 * NT + nt
                if c == 0:
                    act.wait_ge(maxed, 2 + it * QK + 4 * j + 2 * nt + 2)
                piece = probs[:, s, c * 1024:(c + 1) * 1024]
                act.activation(piece, piece, ACT.Exp, bias=lowest[:, s, 1:2], scale=-1.0,
                               accum_out=sums[:, s, c:c + 1]).then_inc(exped, 1)

            def copy_out(it, j):
                act.wait_ge(pv_done, RING + it * G + STEPS * (j + 1))
                act.wait_ge(o_scaled, it * BLOCKS + j + 1)
                for part in range(2):
                    last = act.activation(o_both[:, j % 2, part, :],
                                          ps[part * HD:(part + 1) * HD, OB + j % 2, 0:NB], ACT.Copy)
                last.then_inc(o_copied, 1)

            with act.Fori(0, B) as b:
                with act.Fori(0, HALVES) as half:
                    it = b * HALVES + half
                    act.wait_ge(turned, 2 + it * G)
                    tile = 0
                    for c in range(CHUNKS):
                        act.wait_ge(raw_loaded, (it * CHUNKS + c + 1) * 16)
                        act.wait_ge(tile_done, 4 + it * TILES + (tiles_to(c - 1) if c >= 1 else -2))
                        act.activation(xhi[:, c % 2], raw[:, :, :], ACT.Copy).then_inc(x_hi, 1)
                        if c >= 1:
                            tile = split_hi(act, it, c - 1, tile)
                    tile = split_hi(act, it, CHUNKS - 1, tile)
                    for e in range(4):
                        exp(it, 0, e)
                    for g in range(G):
                        j, d = g // STEPS, g % STEPS
                        act.wait_ge(turned, 2 + it * G + g + 1)
                        act.wait_ge(pv_done, it * G + g + 1)
                        act.activation(pthi[:, g % RING, :], ps[:, TB + g % 2, :], ACT.Copy).then_inc(pt_hi, 1)
                        if d in EXP_AT and j + 1 < BLOCKS:
                            exp(it, j + 1, EXP_AT[d])
                        if d == LAG and j >= 1:
                            copy_out(it, j - 1)
                    copy_out(it, BLOCKS - 1)

        @block.vector
        def _(dve):
            def mask_and_max(it, j, k):
                nb, h, nt, c = j // HALF, j % HALF, k // 2, k % 2
                s = j % 2 * NT + nt
                if h == 0 and c == 0:
                    dve.wait_ge(mask_made, NT + it * NT * 4 + nb * NT + nt + 1)
                if c == 1:
                    dve.wait_ge(maxed, 2 + it * QK + 4 * j + k)
                wait_alone(dve, passed, scored, it * QK + 4 * j + k + 1)
                dve.tensor_tensor_reduce(
                    out=probs[:, s, c * 1024:(c + 1) * 1024],
                    in0=ps[:, SB + 2 * (k % 2):SB + 2 * (k % 2) + 2, :].rearrange("p a n -> p (a n)"),
                    in1=mask_add[:, nb % 2 * NT + nt, c * 1024:(c + 1) * 1024], scale=-SCALE,
                    scalar=BIG if c == 0 else lowest[:, s, 0:1], op0=ALU.add, op1=ALU.min,
                    accum_out=lowest[:, s, c:c + 1]).then_inc(maxed, 1)

            def invert(it, j):
                s = j % 2 * NT
                dve.wait_ge(exped, it * QK + 4 * j + 4)
                dve.tensor_tensor(total[:, :], sums[:, s:s + NT, 0], sums[:, s:s + NT, 1],
                                  ALU.add).then_inc(totalled, 1)
                dve.wait_ge(totalled, it * BLOCKS + j + 1)
                dve.wait_ge(r_out[j % 2], 16 + it * 8 * 16 + j // 2 * 16)
                dve.reciprocal(recip[:, j % 2, :], total[:, :]).then_inc(inverted, 1)

            with dve.Fori(0, B) as b:
                with dve.Fori(0, HALVES) as half:
                    it = b * HALVES + half
                    tile = 0
                    for c in range(CHUNKS):
                        dve.wait_ge(x_hi, it * CHUNKS + c + 1)
                        dve.tensor_tensor(xlo[:, c % 2], raw[:, :, :], f32(xhi[:, c % 2]),
                                          ALU.subtract).then_inc(x_lo, 1)
                        if c >= 1:
                            tile = split_lo(dve, it, c - 1, tile)
                    tile = split_lo(dve, it, CHUNKS - 1, tile)
                    for k in range(4):
                        mask_and_max(it, 0, k)
                    for g in range(G):
                        j, d = g // STEPS, g % STEPS
                        dve.wait_ge(pt_hi, 2 + it * G + g + 1)
                        dve.tensor_tensor(ptlo[:, g % RING, :], ps[:, TB + g % 2, :],
                                          f32(pthi[:, g % RING, :]), ALU.subtract).then_inc(pt_lo, 1)
                        if d in MAX_AT and j + 1 < BLOCKS:
                            mask_and_max(it, j + 1, MAX_AT[d])
                        if d == 3:
                            invert(it, j)

        @block.tensor
        def _(pe):
            def project(it, c, tile):
                s = c % 2
                parts = ((whi, xhi), (wlo, xhi), (whi, xlo))
                pe.wait_ge(x_lo, 1 + it * CHUNKS + c + 1)
                for n in range(4 if c < CTX_CHUNKS else 2):
                    pe.wait_ge(tile_lo, it * TILES + tile + 1)
                    bank = ps[:, SB + tile % 4, :]
                    if n < 2:
                        a = 1 if c < CTX_CHUNKS else 0
                        last = products(pe, bank, [(w[:, k, a, n * P:(n + 1) * P], x[:, s, k, :])
                                                   for w, x in parts for k in range(KT)])
                    else:
                        for t in range(2):
                            col = (2 * (n - 2) + t) * P
                            last = products(pe, bank[:, t * HC:(t + 1) * HC],
                                            [(x[:, s, k, col:col + P], w[:, k, 2, :])
                                             for w, x in parts for k in range(KT)])
                    last.then_inc(tile_done, 1)
                    tile += 1
                return tile

            def score(it, j, k):
                nb, h, nt, c = j // HALF, j % HALF, k // 2, k % 2
                pe.wait_ge(maxed, it * QK + 4 * j + k + 1)
                row = nb * NB + nt * P
                for q in (qhi, qlo):
                    for m in range(2):
                        col = (2 * c + m) * CH
                        last = pe.matmul(ps[:, SB + 2 * (k % 2) + m, :], q[:, h, row:row + P],
                                         ks[:, h, col:col + CH], start=q is qhi, stop=q is qlo,
                                         skip_group_check=True)
                last.then_inc(scored, 1)

            with pe.Fori(0, B) as b:
                with pe.Fori(0, HALVES) as half:
                    it = b * HALVES + half
                    pe.wait_ge(w_loaded, it * 32 + 32)
                    tile = 0
                    for c in range(CHUNKS):
                        tile = project(it, c, tile)
                    pe.wait_ge(tile_lo, 4 + it * TILES + TILES)
                    for k in range(4):
                        score(it, 0, k)
                    for g in range(G + LAG):
                        j, d = g // STEPS, g % STEPS
                        if g < G:
                            if d == 0:
                                pe.wait_ge(exped, it * QK + 4 * j + 3)
                            if d == STEPS // 2:
                                pe.wait_ge(exped, it * QK + 4 * j + 4)
                            pe.wait_ge(pt_lo, it * G + g + 1)
                            for m in range(2):
                                for nt in range(NT):
                                    col = (2 * d + m) * P
                                    last = pe.transpose(
                                        ps[:, TB + g % 2, m * NB + nt * P:m * NB + (nt + 1) * P],
                                        probs[:, j % 2 * NT + nt, col:col + P], ident[:, :])
                            last.then_inc(turned, 1)
                            if d in QK_AT and j + 1 < BLOCKS:
                                score(it, j + 1, QK_AT[d])
                        if g >= LAG:
                            v = g - LAG
                            j, d = v // STEPS, v % STEPS
                            pe.wait_ge(pt_lo, 2 + it * G + v + 1)
                            if d == 0:
                                pe.wait_ge(o_copied, it * BLOCKS + j + 1)
                            for m in range(2):
                                for pt in (pthi, ptlo):
                                    last = pe.matmul(ps[:, OB + j % 2, 0:NB], vs[:, 2 * d + m, j % HALF, :],
                                                     pt[:, v % RING, m * NB:(m + 1) * NB],
                                                     start=(d == 0 and m == 0 and pt is pthi),
                                                     stop=(d == STEPS - 1 and m == 1 and pt is ptlo),
                                                     skip_group_check=True)
                            last.then_inc(pv_done, 1)


LCHUNKS = TOK // CH
TILE = CH // P
ML = FL // P
MID = KT + ML


def light(nc, x, attT, wo, rt, gamma, w1, b1, w2, b2, z_rows, out, scores, consts):
    ident, eps = consts["ident"], consts["eps"]
    with ExitStack() as ctx:
        sb = lambda name, shape, dt=F32: ctx.enter_context(nc.sbuf_tensor("c_" + name, shape, dt))
        sem = lambda name: ctx.enter_context(nc.semaphore("c_" + name))
        wo_raw, wo_hi, wo_lo = (sb("wo" + n, [P, KT, D], dt) for n, dt in (("", F32), ("hi", F32R), ("lo", F32R)))
        w1_raw, w1_hi, w1_lo = (sb("w1" + n, [P, KT, FL], dt) for n, dt in (("", F32), ("hi", F32R), ("lo", F32R)))
        w2_raw, w2_hi, w2_lo = (sb("w2" + n, [P, ML, D], dt) for n, dt in (("", F32), ("hi", F32R), ("lo", F32R)))
        rt_all = sb("rt", [P, D])
        b2_all = sb("b2", [P, D])
        gamma_col = sb("gamma", [P, KT])
        b1_col = sb("b1", [P, ML])
        o_raw = sb("o_raw", [P, 2, KT, CH])
        o_hi, o_lo = sb("o_hi", [P, KT, CH], F32R), sb("o_lo", [P, KT, CH], F32R)
        x_in = sb("x_in", [P, 2, TILE, D])
        x1 = sb("x1", [P, 2, TILE, D])
        stats, mv = sb("stats", [P, TILE, 6]), sb("mv", [P, TILE, 2])
        sd, rstd = sb("sd", [P, TILE]), sb("rstd", [P, TILE])
        sq, nrm, nrm_min, rn = (sb(n, [P, TILE]) for n in ("sq", "nrm", "nrm_min", "rn"))
        s4 = sb("s4", [P, TILE])
        junk = sb("junk", [P, D])
        xn = sb("xn", [P, TILE, D])
        z = sb("z", [P, 2, TILE, D])
        z_hi, z_lo = sb("z_hi", [P, KT, CH], F32R), sb("z_lo", [P, KT, CH], F32R)
        g = sb("g", [P, ML, CH])
        g_hi, g_lo = sb("g_hi", [P, ML, CH], F32R), sb("g_lo", [P, ML, CH], F32R)
        y = sb("y", [P, TILE, D])
        ps = ctx.enter_context(nc.psum_tensor("c_ps", [P, 8, CH], F32))
        XB, MB, YB = 0, 4, 6

        passed = sem("passed")
        w_loaded, w_hi, w_lo = sem("w_loaded"), sem("w_hi"), sem("w_lo")
        o_loaded = [sem(f"o_loaded{u}") for u in range(2)]
        x_loaded = [sem(f"x_loaded{u}") for u in range(2)]
        o_is_hi, o_is_lo = sem("o_is_hi"), sem("o_is_lo")
        projected = sem("projected")
        x1_done, stats_done, mv_done, sd_done, rstd_done, xn_done = (
            sem(n) for n in ("x1_done", "stats_done", "mv_done", "sd_done", "rstd_done", "xn_done"))
        sq_done, junked, nrm_done, min_done, rn_done, z_done = (
            sem(n) for n in ("sq_done", "junked", "nrm_done", "min_done", "rn_done", "z_done"))
        z_stored = [sem(f"z_stored{u}") for u in range(2)]
        mid_done = sem("mid_done")
        z_is_hi, z_is_lo = sem("z_is_hi"), sem("z_is_lo")
        g_done, g_is_hi, g_is_lo = sem("g_done"), sem("g_is_hi"), sem("g_is_lo")
        b2_added = sem("b2_added")
        y_done, out_done = sem("y_done"), sem("out_done")
        out_stored = sem("out_stored")
        block = ctx.enter_context(nc.Block())
        x_rows = x.rearrange("b n d -> (b n) d")
        out_rows = out.rearrange("b n d -> (b n) d")
        weights = ((wo_raw, wo_hi, wo_lo), (w1_raw, w1_hi, w1_lo), (w2_raw, w2_hi, w2_lo))

        def steps(norm, split, last):
            pass

        def by_rows(ap, i, k):
            return ap[bass.ds((i * 2 + k) * CH, CH), :].rearrange("(t p) d -> p t d", p=P)

        @block.gpsimd
        def _(pool):
            free_from_the_start(pool, (projected, TILE), (x1_done, TILE), (mid_done, MID), (z_is_lo, KT),
                                (g_done, ML), (g_is_lo, ML), (y_done, TILE), (out_done, 2),
                                (z_stored[0], 16), (z_stored[1], 16), (out_stored, 16), (o_is_lo, 2))

            def add_b2(i, k):
                wait_alone(pool, passed, xn_done, i * 2 + k + 1)
                pool.tensor_tensor(x1[:, k % 2], x1[:, k % 2],
                                   b2_all[:, :].unsqueeze(1).broadcast_to([P, TILE, D]), ALU.add).then_inc(b2_added, 1)

            pool.wait_ge(w_loaded, 16 * 7)
            add_b2(0, 0)
            with pool.Fori(0, LCHUNKS // 2 - 1) as i:
                for k in range(2):
                    add_b2(i, k + 1)
            add_b2(0, LCHUNKS - 1)

        @block.sync
        def _(sp):
            def load(i, k):
                c, u = i * 2 + k, k % 2
                wait_alone(sp, passed, o_is_lo, c + 1)
                sp.dma_start(o_raw[:, u], rows_by_tile(attT[:, bass.ds(c * CH, CH)], KT)).then_inc(o_loaded[u], 16)
                if k >= 2:
                    wait_alone(sp, passed, x1_done, TILE + (c - 1) * TILE)
                sp.dma_start(x_in[:, u], by_rows(x_rows, i, k)).then_inc(x_loaded[u], 16)

            def store_z(i, k):
                c, u = i * 2 + k, k % 2
                wait_alone(sp, passed, z_done, c + 1)
                sp.dma_start(by_rows(z_rows, i, k), z[:, u]).then_inc(z_stored[u], 16)

            def store_out(i, k):
                c = i * 2 + k
                wait_alone(sp, passed, out_done, 2 + (c + 1) * TILE)
                sp.dma_start(by_rows(out_rows, i, k), y[:, :, :]).then_inc(out_stored, 16)

            for raw, w, kt in ((wo_raw, wo, KT), (w1_raw, w1, KT), (w2_raw, w2, ML)):
                sp.dma_start(raw[:, :, :], rows_by_tile(w, kt)).then_inc(w_loaded, 16)
            for all_, row in ((rt_all, rt), (b2_all, b2)):
                sp.dma_start(all_[:, :], row.rearrange("(a d) -> a d", a=1).partition_broadcast(P)
                             ).then_inc(w_loaded, 16)
            sp.dma_start(gamma_col[:, :], gamma).then_inc(w_loaded, 16)
            sp.dma_start(b1_col[:, :], b1).then_inc(w_loaded, 16)
            load(0, 0)
            load(0, 1)
            store_z(0, 0)
            with sp.Fori(0, LCHUNKS // 2 - 1) as i:
                for k in range(2):
                    load(i, k + 2)
                    store_z(i, k + 1)
                    store_out(i, k)
            store_z(0, LCHUNKS - 1)
            for k in (LCHUNKS - 2, LCHUNKS - 1):
                store_out(0, k)
            sp.wait_ge(out_stored, 16 + 16 * LCHUNKS)
            for u in range(2):
                sp.wait_ge(z_stored[u], 16 + 16 * LCHUNKS // 2)

        def in_order(eng, norm, light, split):
            split(0, 0)
            norm(0, 0)
            split(0, 1)
            with eng.Fori(0, LCHUNKS // 2 - 1) as i:
                for k in range(2):
                    norm(i, k + 1)
                    light(i, k)
                    split(i, k + 2)
            norm(0, LCHUNKS - 1)
            light(0, LCHUNKS - 2)
            light(0, LCHUNKS - 1)

        @block.scalar
        def _(act):
            act.wait_ge(w_loaded, 16 * 7)
            for raw, hi, lo in weights:
                act.activation(hi[:, :, :], raw[:, :, :], ACT.Copy).then_inc(w_hi, 1)

            def split(i, k):
                c, u = i * 2 + k, k % 2
                act.wait_ge(o_loaded[u], (i + k // 2 + 1) * 16)
                act.wait_ge(projected, TILE + c * TILE)
                act.activation(o_hi[:, :, :], o_raw[:, u], ACT.Copy).then_inc(o_is_hi, 1)

            def norm(i, k):
                c = i * 2 + k
                act.wait_ge(mv_done, c + 1)
                act.activation(sd[:, :], mv[:, :, 1], ACT.Sqrt, bias=eps[:, :]).then_inc(sd_done, 1)
                act.wait_ge(sq_done, c + 1)
                act.activation(nrm[:, :], sq[:, :], ACT.Sqrt).then_inc(nrm_done, 1)

            def light_branch(i, k):
                c = i * 2 + k
                for n in range(KT):
                    act.wait_ge(mid_done, MID + c * MID + n + 1)
                    act.activation(z_hi[:, n, :], ps[:, MB + n % 2, :], ACT.Copy,
                                   scale=gamma_col[:, n:n + 1]).then_inc(z_is_hi, 1)
                for m in range(ML):
                    act.wait_ge(mid_done, MID + c * MID + KT + m + 1)
                    act.wait_ge(g_is_lo, c * ML + ML)
                    act.activation(g[:, m, :], ps[:, MB + m % 2, :], ACT.Gelu,
                                   bias=b1_col[:, m:m + 1]).then_inc(g_done, 1)

            in_order(act, norm, light_branch, split)

        @block.vector
        def _(dve):
            for n, (raw, hi, lo) in enumerate(weights):
                dve.wait_ge(w_hi, n + 1)
                dve.tensor_tensor(lo[:, :, :], raw[:, :, :], f32(hi[:, :, :]), ALU.subtract).then_inc(w_lo, 1)

            def split(i, k):
                c, u = i * 2 + k, k % 2
                dve.wait_ge(o_is_hi, c + 1)
                dve.tensor_tensor(o_lo[:, :, :], o_raw[:, u], f32(o_hi[:, :, :]), ALU.subtract).then_inc(o_is_lo, 1)

            def norm(i, k):
                c, u = i * 2 + k, k % 2
                dve.wait_ge(x_loaded[u], (i + k // 2 + 1) * 16)
                for t in range(TILE):
                    dve.wait_ge(projected, TILE + c * TILE + t + 1)
                    dve.tensor_tensor(x1[:, u, t, :], ps[:, XB + t, :], x_in[:, u, t, :],
                                      ALU.add).then_inc(x1_done, 1)
                for t in range(TILE):
                    wait_alone(dve, passed, x1_done, TILE + c * TILE + t + 1)
                    last = dve.bn_stats(out=stats[:, t, :], in_=x1[:, u, t, :])
                last.then_inc(stats_done, 1)
                wait_alone(dve, passed, stats_done, c + 1)
                for t in range(TILE):
                    last = dve.bn_aggr(out=mv[:, t, :], in_=stats[:, t, :])
                last.then_inc(mv_done, 1)
                dve.wait_ge(sd_done, c + 1)
                dve.reciprocal(rstd[:, :], sd[:, :]).then_inc(rstd_done, 1)
                dve.wait_ge(rstd_done, c + 1)
                for t in range(TILE):
                    last = dve.tensor_scalar(xn[:, t, :], x1[:, u, t, :], mv[:, t, 0:1], rstd[:, t:t + 1],
                                             ALU.subtract, ALU.mult)
                last.then_inc(xn_done, 1)
                for t in range(TILE):
                    wait_alone(dve, passed, xn_done, c + 1)
                    if t == 0:
                        wait_alone(dve, passed, junked, c * 2 * TILE + 1)
                    for a, (other, total) in enumerate(((rt_all[:, :], s4), (xn[:, t, :], sq))):
                        if t + a > 0:
                            wait_alone(dve, passed, junked, 1 + (c * TILE + t) * 2 + a)
                        last = dve.tensor_tensor_reduce(out=junk[:, :], in0=xn[:, t, :], in1=other, scale=1.0,
                                                        scalar=0.0, op0=ALU.mult, op1=ALU.add,
                                                        accum_out=total[:, t:t + 1]).then_inc(junked, 1)
                dve.wait_ge(junked, 1 + (c + 1) * TILE * 2)
                dve.tensor_copy(scores[:, bass.ds(c * TILE, TILE)], s4[:, :]).then_inc(sq_done, 1)
                dve.wait_ge(nrm_done, c + 1)
                dve.tensor_scalar(nrm_min[:, :], nrm[:, :], 1e-12, None, ALU.max).then_inc(min_done, 1)
                dve.wait_ge(min_done, c + 1)
                dve.reciprocal(rn[:, :], nrm_min[:, :]).then_inc(rn_done, 1)
                dve.wait_ge(rn_done, c + 1)
                dve.wait_ge(z_stored[u], (i + k // 2 + 1) * 16)
                for t in range(TILE):
                    last = dve.tensor_scalar(z[:, u, t, :], xn[:, t, :], rn[:, t:t + 1], float(D) ** 0.5,
                                             ALU.mult, ALU.mult)
                last.then_inc(z_done, 1)

            def light_branch(i, k):
                c, u = i * 2 + k, k % 2
                for n in range(KT):
                    dve.wait_ge(z_is_hi, c * KT + n + 1)
                    dve.scalar_tensor_tensor(out=z_lo[:, n, :], in0=ps[:, MB + n % 2, :],
                                             scalar=gamma_col[:, n:n + 1], in1=f32(z_hi[:, n, :]),
                                             op0=ALU.mult, op1=ALU.subtract).then_inc(z_is_lo, 1)
                for m in range(ML):
                    dve.wait_ge(g_done, ML + c * ML + m + 1)
                    dve.wait_ge(y_done, TILE + c * TILE)
                    dve.tensor_copy(g_hi[:, m, :], g[:, m, :]).then_inc(g_is_hi, 1)
                    dve.wait_ge(g_is_hi, c * ML + m + 1)
                    dve.tensor_tensor(g_lo[:, m, :], g[:, m, :], f32(g_hi[:, m, :]),
                                      ALU.subtract).then_inc(g_is_lo, 1)
                dve.wait_ge(b2_added, c + 1)
                dve.wait_ge(out_stored, (c + 1) * 16)
                for t in range(TILE):
                    dve.wait_ge(y_done, TILE + c * TILE + t + 1)
                    dve.tensor_tensor(y[:, t, :], ps[:, YB + t % 2, :], x1[:, u, t, :],
                                      ALU.add).then_inc(out_done, 1)

            dve.memset(junk[:, :], 0.0).then_inc(junked, 1)
            in_order(dve, norm, light_branch, split)

        @block.tensor
        def _(pe):
            pe.wait_ge(w_lo, 3)

            def project(i, k):
                c = i * 2 + k
                pe.wait_ge(o_is_lo, 2 + c + 1)
                for t in range(TILE):
                    pe.wait_ge(x1_done, c * TILE + t + 1)
                    products(pe, ps[:, XB + t, :],
                             [(o[:, n, t * P:(t + 1) * P], w[:, n, :])
                              for o, w in ((o_hi, wo_hi), (o_lo, wo_hi), (o_hi, wo_lo))
                              for n in range(KT)]).then_inc(projected, 1)

            def light_branch(i, k):
                c, u = i * 2 + k, k % 2
                pe.wait_ge(z_done, c + 1)
                for n in range(KT):
                    if n < 2:
                        pe.wait_ge(g_done, c * ML + n + 1)
                    else:
                        pe.wait_ge(z_is_lo, KT + c * KT + n - 1)
                    for t in range(TILE):
                        last = pe.transpose(ps[:, MB + n % 2, t * P:(t + 1) * P],
                                            z[:, u, t, n * P:(n + 1) * P], ident[:, :])
                    last.then_inc(mid_done, 1)
                pe.wait_ge(z_is_lo, KT + c * KT + KT)
                for m in range(ML):
                    products(pe, ps[:, MB + m % 2, :],
                             [(w[:, n, m * P:(m + 1) * P], zz[:, n, :])
                              for w, zz in ((w1_hi, z_hi), (w1_lo, z_hi), (w1_hi, z_lo))
                              for n in range(KT)]).then_inc(mid_done, 1)
                pe.wait_ge(g_is_lo, ML + c * ML + ML)
                for t in range(TILE):
                    pe.wait_ge(out_done, c * TILE + t + 1)
                    products(pe, ps[:, YB + t % 2, :],
                             [(gg[:, m, t * P:(t + 1) * P], w[:, m, :])
                              for gg, w in ((g_hi, w2_hi), (g_lo, w2_hi), (g_hi, w2_lo))
                              for m in range(ML)]).then_inc(y_done, 1)

            in_order(pe, project, light_branch, lambda i, k: None)


NT_B = N // P


def route(nc, scores, score_row, slots, consts):
    cols = B * NT_B
    with ExitStack() as ctx:
        sb = lambda name, shape, dt=F32: ctx.enter_context(nc.sbuf_tensor("d_" + name, shape, dt))
        sem = lambda name: ctx.enter_context(nc.semaphore("d_" + name))
        ones = sb("ones", [P, P])
        before = sb("before", [P, P])
        top1, top = sb("top1", [P, B]), sb("top", [P, B])
        neg_a = sb("neg_a", [P, B])
        shift = sb("shift", [P, B])
        zc, zs, e = (sb(n, [P, cols]) for n in ("zc", "zs", "e"))
        part, lg = sb("part", [P, B]), sb("lg", [P, B])
        sa = sb("sa", [P, cols])
        sel = sb("sel", [P, cols])
        one_minus = sb("one_minus", [P, cols])
        pay = sb("pay", [P, cols, 2])
        row = sb("row", [P, B, N])
        junk = sb("junk", [P, 3, N])
        counts = sb("counts", [P, 3, cols])
        rank1, rank = sb("rank1", [P, cols]), sb("rank", [P, cols])
        place = sb("place", [P, cols], I32)
        ps = ctx.enter_context(nc.psum_tensor("d_ps", [P, CH], F32))
        by_batch = lambda t: t[:, :].rearrange("p (b t) -> p b t", b=B)
        each = lambda t: t[:, :].unsqueeze(2).broadcast_to([P, B, NT_B])

        passed = sem("passed")
        ones_ready, before_zero, before_ready, ids_ready = (
            sem(n) for n in ("ones_ready", "before_zero", "before_ready", "ids_ready"))
        top_part, top_ready, start_ready = sem("top_part"), sem("top_ready"), sem("start_ready")
        cut, shifted, exped, parted, summed, logged, stepped = (
            sem(n) for n in ("cut", "shifted", "exped", "parted", "summed", "logged", "stepped"))
        sa_done, sa_min, sel_done, minus_done, weight_done = (
            sem(n) for n in ("sa_done", "sa_min", "sel_done", "minus_done", "weight_done"))
        row_out, row_in = sem("row_out"), sem("row_in")
        counted, rank1_done, rank_done, placed = (
            sem(n) for n in ("counted", "rank1_done", "rank_done", "placed"))
        scattered = sem("scattered")
        block = ctx.enter_context(nc.Block())
        LOOPS = ITERS - 1
        FIRST_NEG_A = float(np.log(np.float32(N)) - np.log(np.float32(EFFECTIVE_K)))
        LOG_K = float(np.log(np.float32(EFFECTIVE_K)))

        @block.gpsimd
        def _(pool):
            pool.memset(ones[:, :], 1.0).then_inc(ones_ready, 1)
            pool.memset(before[:, :], 1.0).then_inc(before_zero, 1)
            pool.wait_ge(before_zero, 1)
            pool.affine_select(out=before[:, :], in_=before[:, :], compare_op=ALU.is_gt, fill=0.0, base=0,
                               pattern=[[-1, P]], channel_multiplier=1).then_inc(before_ready, 1)
            pool.iota(pay[:, :, 0].bitcast(I32), pattern=[[P, cols]], base=0,
                      channel_multiplier=1).then_inc(ids_ready, 1)
            pool.wait_ge(top_part, 1)
            pool.partition_all_reduce(top[:, :], top1[:, :], P, bass.bass_isa.ReduceOp.max).then_inc(top_ready, 1)
            pool.wait_ge(placed, 1)
            pool.wait_ge(weight_done, 1)
            pool.wait_ge(ids_ready, 1)
            for n in range(cols):
                pool.indirect_dma_start(out=slots, out_offset=bass.IndirectOffsetOnAxis(place[:, n:n + 1], 0),
                                        in_=pay[:, n, :], in_offset=None).then_inc(scattered, 16)
            pool.wait_ge(scattered, 16 * cols)

        @block.scalar
        def _(act):
            with act.Fori(0, LOOPS) as i:
                act.wait_ge(shifted, i + 1)
                act.activation(e[:, :], zs[:, :], ACT.Exp).then_inc(exped, 1)
                act.wait_ge(summed, i + 1)
                act.activation(lg[:, :], ps[:, 0:B], ACT.Ln).then_inc(logged, 1)
            act.wait_ge(sa_min, 1)
            act.activation(sel[:, :], sa[:, :], ACT.Exp).then_inc(sel_done, 1)

        @block.tensor
        def _(pe):
            pe.wait_ge(ones_ready, 1)
            with pe.Fori(0, LOOPS) as i:
                pe.wait_ge(parted, i + 1)
                pe.matmul(ps[:, 0:B], ones[:, :], part[:, :], start=True, stop=True).then_inc(summed, 1)

        @block.sync
        def _(sp):
            sp.wait_ge(sel_done, 1)
            with nc.allow_non_contiguous_dma(reason="a column of scores to a row"):
                sp.dma_start(score_row.rearrange("(n p) -> p n", p=P), sel[:, :]).then_inc(row_out, 16)
            sp.wait_ge(row_out, 16)
            sp.dma_start(row[:, :, :].rearrange("p b n -> p (b n)"),
                         score_row.rearrange("(a n) -> a n", a=1).partition_broadcast(P)).then_inc(row_in, 16)

        @block.vector
        def _(dve):
            dve.tensor_reduce(top1[:, :], by_batch(scores), AX.X, ALU.max).then_inc(top_part, 1)
            dve.memset(neg_a[:, :], FIRST_NEG_A).then_inc(stepped, 1)
            dve.wait_ge(top_ready, 1)
            with dve.Fori(0, LOOPS) as i:
                dve.wait_ge(stepped, i + 1)
                dve.tensor_tensor(by_batch(zc), by_batch(scores), each(neg_a), ALU.min).then_inc(cut, 1)
                dve.tensor_tensor(shift[:, :], top[:, :], neg_a[:, :], ALU.min).then_inc(cut, 1)
                dve.wait_ge(cut, 2 * i + 2)
                dve.tensor_tensor(by_batch(zs), by_batch(zc), each(shift), ALU.subtract).then_inc(shifted, 1)
                dve.wait_ge(exped, i + 1)
                dve.tensor_reduce(part[:, :], by_batch(e), AX.X, ALU.add).then_inc(parted, 1)
                dve.wait_ge(logged, i + 1)
                wait_alone(dve, passed, logged, i + 1)
                dve.scalar_tensor_tensor(out=neg_a[:, :], in0=lg[:, :], scalar=-LOG_K, in1=shift[:, :],
                                         op0=ALU.add, op1=ALU.add).then_inc(stepped, 1)
            dve.wait_ge(stepped, LOOPS + 1)
            dve.tensor_tensor(by_batch(zc), by_batch(scores), each(neg_a), ALU.subtract).then_inc(sa_done, 1)
            dve.wait_ge(sa_done, 1)
            dve.tensor_scalar(sa[:, :], zc[:, :], 0.0, None, ALU.min).then_inc(sa_min, 1)
            dve.wait_ge(sel_done, 1)
            dve.tensor_scalar(one_minus[:, :], sel[:, :], -1.0, 1.0, ALU.mult, ALU.add).then_inc(minus_done, 1)
            dve.wait_ge(minus_done, 1)
            dve.tensor_tensor(pay[:, :, 1], sel[:, :], one_minus[:, :], ALU.add).then_inc(weight_done, 1)
            dve.wait_ge(row_in, 16)
            dve.wait_ge(before_ready, 1)
            dve.memset(counts[:, :, :], 0.0).then_inc(counted, 1)
            dve.wait_ge(counted, 1)
            done = 1
            for n in range(cols):
                b, t = n // NT_B, n % NT_B
                own = slice(t * P, (t + 1) * P)
                mine = sel[:, n:n + 1]
                if n:
                    dve.wait_ge(counted, done)
                if t:
                    dve.tensor_scalar(junk[:, 0, 0:t * P], row[:, b, 0:t * P], mine, None, ALU.is_ge, ALU.add,
                                      accum_out=counts[:, 0, n:n + 1]).then_inc(counted, 1)
                    done += 1
                dve.tensor_scalar(junk[:, 1, t * P:N], row[:, b, t * P:N], mine, None, ALU.is_gt, ALU.add,
                                  accum_out=counts[:, 1, n:n + 1]).then_inc(counted, 1)
                dve.scalar_tensor_tensor(out=junk[:, 2, 0:P], in0=row[:, b, own], scalar=mine,
                                         in1=before[:, :], op0=ALU.is_equal, op1=ALU.mult,
                                         accum_out=counts[:, 2, n:n + 1]).then_inc(counted, 1)
                done += 2
            dve.wait_ge(counted, done)
            dve.tensor_tensor(rank1[:, :], counts[:, 0, :], counts[:, 1, :], ALU.add).then_inc(rank1_done, 1)
            dve.wait_ge(rank1_done, 1)
            dve.tensor_tensor(rank[:, :], rank1[:, :], counts[:, 2, :], ALU.add).then_inc(rank_done, 1)
            dve.wait_ge(rank_done, 1)
            for b in range(B):
                own = slice(b * NT_B, (b + 1) * NT_B)
                last = dve.tensor_scalar(place[:, own], rank[:, own], float(b * N), None, ALU.add)
            last.then_inc(placed, 1)


ST = CHOSEN // P
MH = FH // P
USES = KT + MH
GR = 3


def heavy(nc, z_rows, slots, gamma, w1, b1, w2, b2, out, consts):
    ident = consts["ident"]
    with ExitStack() as ctx:
        def sb(name, shape, dt=F32, stack=ctx):
            return stack.enter_context(nc.sbuf_tensor("e_" + name, shape, dt))

        sem = lambda name: ctx.enter_context(nc.semaphore("e_" + name))
        w1_hi, w1_lo = sb("w1_hi", [P, KT, FH], F32R), sb("w1_lo", [P, KT, FH], F32R)
        w2_hi, w2_lo = sb("w2_hi", [P, MH, D], F32R), sb("w2_lo", [P, MH, D], F32R)
        gamma_col, b1_col = sb("gamma", [P, KT]), sb("b1", [P, MH])
        b2_all = sb("b2", [P, D])
        slot = sb("slot", [P, ST, 2])
        z = sb("z", [P, ST, D])
        z_hi, z_lo = sb("z_hi", [P, KT, CH], F32R), sb("z_lo", [P, KT, CH], F32R)
        g = sb("g", [P, 2, CH])
        g_hi, g_lo = sb("g_hi", [P, GR, CH], F32R), sb("g_lo", [P, GR, CH], F32R)
        with ExitStack() as first:
            raw = sb("raw", [P, 2, 4, CH], F32, first)
        with ExitStack() as second:
            base = sb("base", [P, ST, D], F32, second)
            y = sb("y", [P, ST, D], F32, second)
        ps = ctx.enter_context(nc.psum_tensor("e_ps", [P, 8, CH], F32))
        YB, MB = 0, 4

        passed = sem("passed")
        w_loaded = [sem(f"w_loaded{u}") for u in range(2)]
        small_loaded = sem("small_loaded")
        w_hi, w_lo = sem("w_hi"), sem("w_lo")
        slot_loaded, z_loaded, base_loaded = sem("slot_loaded"), sem("z_loaded"), sem("base_loaded")
        mid_done = sem("mid_done")
        z_is_hi, z_is_lo = sem("z_is_hi"), sem("z_is_lo")
        g_done, g_is_hi, g_is_lo = sem("g_done"), sem("g_is_hi"), sem("g_is_lo")
        used = sem("used")
        b2_added, y_done, y_stored = sem("b2_added"), sem("y_done"), sem("y_stored")
        block = ctx.enter_context(nc.Block())
        out_rows = out.rearrange("b n d -> (b n) d")
        PIECES = 8

        def piece(n, big_1, big_2):
            return big_1[:, n, :] if n < KT else big_2[:, (n - KT) * 4:(n - KT) * 4 + 4, :].rearrange(
                "p k d -> p (k d)")

        @block.sync
        def _(sp):
            sp.dma_start(gamma_col[:, :], gamma).then_inc(small_loaded, 16)
            sp.dma_start(b1_col[:, :], b1).then_inc(small_loaded, 16)
            sp.dma_start(b2_all[:, :], b2.rearrange("(a d) -> a d", a=1).partition_broadcast(P)
                         ).then_inc(small_loaded, 16)
            for n in range(PIECES):
                if n >= 2:
                    sp.wait_ge(w_lo, n - 1)
                if n < KT:
                    src, dst = w1[n * P:(n + 1) * P, :], raw[:, n % 2].rearrange("p k d -> p (k d)")
                else:
                    src, dst = rows_by_tile(w2[(n - KT) * CH:(n - KT + 1) * CH, :], 4), raw[:, n % 2]
                sp.dma_start(dst, src).then_inc(w_loaded[n % 2], 16)
            with sp.Fori(0, B) as b:
                sp.wait_ge(y_done, b * ST + 1)
                sp.dma_start(slot[:, :, :], slots[bass.ds(b * N, CHOSEN), :].rearrange(
                    "(t p) a -> p t a", p=P)).then_inc(slot_loaded, 16)
                wait_alone(sp, passed, y_stored, b * ST * 16 + ST * 16)

        @block.gpsimd
        def _(pool):
            free_from_the_start(pool, (mid_done, 0 + USES), (g_done, 2), (g_is_lo, 2), (used, GR),
                                (y_done, 1), (z_is_lo, 2), (b2_added, ST))
            pool.wait_ge(w_lo, PIECES)
            with pool.Fori(0, B) as b:
                wait_alone(pool, passed, slot_loaded, b * 16 + 16)
                for t in range(ST):
                    pool.indirect_dma_start(out=z[:, t, :], out_offset=None, in_=z_rows,
                                            in_offset=bass.IndirectOffsetOnAxis(slot[:, t, 0:1].bitcast(I32), 0)
                                            ).then_inc(z_loaded, 16)
                for t in range(ST):
                    pool.indirect_dma_start(out=base[:, t, :], out_offset=None, in_=out_rows,
                                            in_offset=bass.IndirectOffsetOnAxis(slot[:, t, 0:1].bitcast(I32), 0)
                                            ).then_inc(base_loaded, 16)
                for t in range(ST):
                    wait_alone(pool, passed, y_done, 1 + b * ST + t + 1)
                    pool.indirect_dma_start(out=out_rows,
                                            out_offset=bass.IndirectOffsetOnAxis(slot[:, t, 0:1].bitcast(I32), 0),
                                            in_=y[:, t, :], in_offset=None).then_inc(y_stored, 16)
                wait_alone(pool, passed, y_stored, b * ST * 16 + ST * 16)

        @block.scalar
        def _(act):
            for n in range(PIECES):
                act.wait_ge(w_loaded[n % 2], 16 * (n // 2 + 1))
                act.activation(piece(n, w1_hi, w2_hi), raw[:, n % 2].rearrange("p k d -> p (k d)"),
                               ACT.Copy).then_inc(w_hi, 1)
            act.wait_ge(small_loaded, 48)
            with act.Fori(0, B) as b:
                for n in range(KT):
                    act.wait_ge(mid_done, USES + b * USES + n + 1)
                    act.activation(z_hi[:, n, :], ps[:, MB + n % 2, :], ACT.Copy,
                                   scale=gamma_col[:, n:n + 1]).then_inc(z_is_hi, 1)
                for m in range(MH):
                    act.wait_ge(mid_done, USES + b * USES + KT + m + 1)
                    act.wait_ge(g_is_lo, b * MH + m + 1)
                    act.activation(g[:, m % 2, :], ps[:, MB + m % 2, :], ACT.Gelu,
                                   bias=b1_col[:, m:m + 1]).then_inc(g_done, 1)

        @block.vector
        def _(dve):
            for n in range(PIECES):
                dve.wait_ge(w_hi, n + 1)
                dve.tensor_tensor(piece(n, w1_lo, w2_lo), raw[:, n % 2].rearrange("p k d -> p (k d)"),
                                  f32(piece(n, w1_hi, w2_hi)), ALU.subtract).then_inc(w_lo, 1)
            dve.wait_ge(small_loaded, 48)
            with dve.Fori(0, B) as b:
                for n in range(KT):
                    dve.wait_ge(z_is_hi, b * KT + n + 1)
                    dve.scalar_tensor_tensor(out=z_lo[:, n, :], in0=ps[:, MB + n % 2, :],
                                             scalar=gamma_col[:, n:n + 1], in1=f32(z_hi[:, n, :]),
                                             op0=ALU.mult, op1=ALU.subtract).then_inc(z_is_lo, 1)
                for m in range(MH):
                    r = m % GR
                    dve.wait_ge(g_done, 2 + b * MH + m + 1)
                    if m < GR:
                        dve.wait_ge(used, GR + b * MH)
                    else:
                        dve.wait_ge(used, b * MH + m + 1)
                    dve.tensor_copy(g_hi[:, r, :], g[:, m % 2, :]).then_inc(g_is_hi, 1)
                    dve.wait_ge(g_is_hi, b * MH + m + 1)
                    dve.tensor_tensor(g_lo[:, r, :], g[:, m % 2, :], f32(g_hi[:, r, :]),
                                      ALU.subtract).then_inc(g_is_lo, 1)
                dve.wait_ge(used, GR + b * MH + MH)
                for t in range(ST):
                    dve.tensor_tensor(y[:, t, :], ps[:, YB + t, :], b2_all[:, :], ALU.add).then_inc(b2_added, 1)
                dve.wait_ge(base_loaded, b * ST * 16 + ST * 16)
                for t in range(ST):
                    wait_alone(dve, passed, b2_added, ST + b * ST + t + 1)
                    dve.scalar_tensor_tensor(out=y[:, t, :], in0=y[:, t, :], scalar=slot[:, t, 1:2],
                                             in1=base[:, t, :], op0=ALU.mult, op1=ALU.add).then_inc(y_done, 1)

        @block.tensor
        def _(pe):
            pe.wait_ge(w_lo, PIECES)
            with pe.Fori(0, B) as b:
                pe.wait_ge(z_loaded, b * ST * 16 + ST * 16)
                for n in range(KT):
                    if n < 2:
                        pe.wait_ge(g_done, b * MH + 2)
                    else:
                        pe.wait_ge(z_is_lo, 2 + b * KT + n - 1)
                    for t in range(ST):
                        last = pe.transpose(ps[:, MB + n % 2, t * P:(t + 1) * P],
                                            z[:, t, n * P:(n + 1) * P], ident[:, :])
                    last.then_inc(mid_done, 1)
                pe.wait_ge(z_is_lo, 2 + b * KT + KT)
                pe.wait_ge(b2_added, b * ST + ST)
                for m in range(MH + 1):
                    if m < MH:
                        if m >= 2:
                            pe.wait_ge(g_done, b * MH + m + 1)
                        products(pe, ps[:, MB + m % 2, :],
                                 [(w[:, n, m * P:(m + 1) * P], zz[:, n, :])
                                  for w, zz in ((w1_hi, z_hi), (w1_lo, z_hi), (w1_hi, z_lo))
                                  for n in range(KT)]).then_inc(mid_done, 1)
                    if m >= 1:
                        v = m - 1
                        r = v % GR
                        pe.wait_ge(g_is_lo, 2 + b * MH + v + 1)
                        for t in range(ST):
                            for a, (gg, w) in enumerate(((g_hi, w2_hi), (g_lo, w2_hi), (g_hi, w2_lo))):
                                last = pe.matmul(ps[:, YB + t, :], gg[:, r, t * P:(t + 1) * P], w[:, v, :],
                                                 start=(v == 0 and a == 0), stop=(v == MH - 1 and a == 2),
                                                 skip_group_check=True)
                        last.then_inc(used, 1)


def xattn_ffn(nc, x, ctxT, mask, wq, wkv, wo, rt, gamma_l, w1_l, b1_l, w2_l, b2_l,
              gamma_h, w1_h, b1_h, w2_h, b2_h, out):
    with ExitStack() as ctx:
        def dram(name, shape, dt=F32):
            return nc.dram_tensor(name, shape, dt, kind="Internal").ap()

        ident = ctx.enter_context(nc.sbuf_tensor("ident", [P, P], F32))
        eps = ctx.enter_context(nc.sbuf_tensor("eps", [P, 1], F32))
        scores = ctx.enter_context(nc.sbuf_tensor("scores", [P, B * NT_B], F32))
        consts = dict(ident=ident, eps=eps)
        xnT = dram("xnT", [D, TOK])
        w_split = dram("w_split", [HALVES, 2, P, KT * 3 * HC])
        attT = dram("attT", [D, TOK])
        r_row = dram("r_row", [2, NB])
        z_rows = dram("z_rows", [TOK, D])
        score_row = dram("score_row", [TOK])
        slots = dram("slots", [TOK, 2])
        prepare(nc, x, wq, wkv, xnT, w_split, consts)
        attend(nc, ctxT, mask, xnT, w_split, attT, r_row, consts)
        light(nc, x, attT, wo, rt, gamma_l, w1_l, b1_l, w2_l, b2_l, z_rows, out, scores, consts)
        route(nc, scores, score_row, slots, consts)
        heavy(nc, z_rows, slots, gamma_h, w1_h, b1_h, w2_h, b2_h, out, consts)


def kernel(x, ctx_1024, mask_BxSxS2_bf1, L0_xattn_Wq, L0_xattn_Wkv, L0_xattn_Wo, L0_ffn_routing_token,
           L0_ffn_gamma_l, L0_ffn_w1_l, L0_ffn_b1_l, L0_ffn_w2_l, L0_ffn_b2_l, L0_ffn_gamma_h,
           L0_ffn_w1_h, L0_ffn_b1_h, L0_ffn_w2_h, L0_ffn_b2_h):
    import concourse.bacc as bacc
    from concourse.bass_utils import run_bass_kernel_spmd

    def columns(v):
        return np.ascontiguousarray(np.asarray(v).reshape(-1, P).T)

    def turned(w):
        return np.ascontiguousarray(np.asarray(w).T)

    arrays = {
        "x": np.asarray(x),
        "ctxT": np.ascontiguousarray(np.asarray(ctx_1024).transpose(0, 2, 1)),
        "mask": np.asarray(mask_BxSxS2_bf1).view(np.uint8),
        "wq": np.asarray(L0_xattn_Wq), "wkv": np.asarray(L0_xattn_Wkv), "wo": np.asarray(L0_xattn_Wo),
        "rt": np.asarray(L0_ffn_routing_token),
        "gamma_l": columns(L0_ffn_gamma_l), "w1_l": turned(L0_ffn_w1_l), "b1_l": columns(L0_ffn_b1_l),
        "w2_l": turned(L0_ffn_w2_l), "b2_l": np.asarray(L0_ffn_b2_l),
        "gamma_h": columns(L0_ffn_gamma_h), "w1_h": turned(L0_ffn_w1_h), "b1_h": columns(L0_ffn_b1_h),
        "w2_h": turned(L0_ffn_w2_h), "b2_h": np.asarray(L0_ffn_b2_h),
    }
    nc = bacc.Bacc("TRN2", target_bir_lowering=False, num_devices=1)
    aps = {n: nc.dram_tensor(n, a.shape, mybir.dt.from_np(a.dtype), kind="ExternalInput").ap()
           for n, a in arrays.items()}
    out = nc.dram_tensor("out", (B, N, D), F32, kind="ExternalOutput").ap()
    xattn_ffn(nc, out=out, **aps)
    r = run_bass_kernel_spmd(nc, [arrays], core_ids=[0])
    return r.results[0]["out"]
```

```python
from contextlib import ExitStack

import concourse.bass as bass
import numpy as np
from concourse import mybir

F32 = mybir.dt.float32
F32R = mybir.dt.float32r
BF16 = mybir.dt.bfloat16
U8 = mybir.dt.uint8
I32 = mybir.dt.int32
ALU = mybir.AluOpType
ACT = mybir.ActivationFunctionType
AX = mybir.AxisListType

P = 128
B, N, M, D = 4, 1024, 2048, 512
H, HD = 8, 64
KT = D // P
HALF = 4
HALVES = H // HALF
HC = HALF * HD
CH = 512
SCALE = HD ** -0.5
EPS = 1e-5
ITERS = 50
CHOSEN = 512
EFFECTIVE_K = min(CHOSEN * 9.0 / 8.0, N)
TOK = B * N
FL = 256
FH = 2048
BIG = 3.4028235e38


def f32(ap):
    return ap.bitcast(F32)


def rows_by_tile(ap, k):
    return ap.rearrange("(k p) n -> p k n", k=k)


def free_from_the_start(eng, *rings):
    for sem, slots in rings:
        eng.sem_inc(sem, slots)


def wait_alone(eng, passed, sem, value):
    eng.wait_ge(sem, value)
    eng.sem_inc(passed, 1)


def products(pe, out, pairs, last=True):
    for n, (w, m) in enumerate(pairs):
        ins = pe.matmul(out, w, m, start=(n == 0), stop=last and n == len(pairs) - 1,
                        skip_group_check=True)
    return ins


def prepare(nc, x, wq, wkv, xnT, w_split, consts):
    eps, ident = consts["eps"], consts["ident"]
    with ExitStack() as ctx:
        sb = lambda name, shape, dt=F32: ctx.enter_context(nc.sbuf_tensor(name, shape, dt))
        sem = lambda name: ctx.enter_context(nc.semaphore(name))
        xin = sb("a_xin", [P, 2, 4, D])
        xn = sb("a_xn", [P, 2, 4, D])
        xt = sb("a_xt", [P, 2, KT, CH])
        stats = sb("a_stats", [P, 4, 6])
        mv = sb("a_mv", [P, 4, 2])
        sd = sb("a_sd", [P, 4])
        rstd = sb("a_rstd", [P, 4])
        wraw = sb("a_wraw", [P, HALVES, KT, 3, HC])
        whi = sb("a_whi", [P, HALVES, KT, 3, HC], F32R)
        wlo = sb("a_wlo", [P, HALVES, KT, 3, HC], F32R)
        ps = ctx.enter_context(nc.psum_tensor("a_ps", [P, 8, CH], F32))

        x_loaded = [sem(f"a_x_loaded{i}") for i in range(2)]
        w_loaded = sem("a_w_loaded")
        w_hi = sem("a_w_hi")
        w_lo = sem("a_w_lo")
        w_stored = sem("a_w_stored")
        passed = sem("a_passed")
        stats_done = sem("a_stats_done")
        mv_done = sem("a_mv_done")
        sd_done = sem("a_sd_done")
        rstd_done = sem("a_rstd_done")
        normed = sem("a_normed")
        turned = sem("a_turned")
        copied = sem("a_copied")
        xt_stored = [sem(f"a_xt_stored{i}") for i in range(2)]
        ident_zero = sem("a_ident_zero")
        ident_ready = sem("a_ident_ready")
        eps_ready = sem("a_eps_ready")

        x_rows = x.rearrange("b n d -> (b n) d")
        block = ctx.enter_context(nc.Block())

        @block.gpsimd
        def _(pool):
            free_from_the_start(pool, (normed, 2), (turned, 2 * KT), (copied, 2 * KT),
                                (xt_stored[0], 16), (xt_stored[1], 16))
            pool.memset(ident[:, :], 0.0).then_inc(ident_zero, 1)
            pool.memset(eps[:, :], EPS).then_inc(eps_ready, 1)
            pool.wait_ge(ident_zero, 1)
            pool.affine_select(out=ident[:, :], in_=ident[:, :], compare_op=ALU.not_equal, fill=1.0,
                               base=0, pattern=[[-1, P]], channel_multiplier=1).then_inc(ident_ready, 1)

        @block.sync
        def _(sp):
            for h in range(HALVES):
                for n, w in enumerate((wq[:, h * HC:(h + 1) * HC], wkv[:, h * HC:(h + 1) * HC],
                                       wkv[:, D + h * HC:D + (h + 1) * HC])):
                    sp.dma_start(wraw[:, h, :, n, :], rows_by_tile(w, KT)).then_inc(w_loaded, 16)
            with sp.Fori(0, TOK // CH // 2) as i:
                for u in range(2):
                    c = i * 2 + u
                    sp.wait_ge(normed, c + 1)
                    sp.dma_start(xin[:, u, :, :], x_rows[bass.ds(c * CH, CH), :].rearrange(
                        "(t p) d -> p t d", p=P)).then_inc(x_loaded[u], 16)
                for u in range(2):
                    c = i * 2 + u
                    wait_alone(sp, passed, copied, 2 * KT + c * KT + KT)
                    sp.dma_start(rows_by_tile(xnT[:, bass.ds(c * CH, CH)], KT),
                                 xt[:, u, :, :]).then_inc(xt_stored[u], 16)
            sp.wait_ge(w_lo, HALVES)
            for h in range(HALVES):
                sp.dma_start(w_split[h, 0], f32(whi[:, h].rearrange("p k a n -> p (k a n)"))).then_inc(w_stored, 16)
                sp.dma_start(w_split[h, 1], f32(wlo[:, h].rearrange("p k a n -> p (k a n)"))).then_inc(w_stored, 16)
            sp.wait_ge(w_stored, 16 * 2 * HALVES)
            for u in range(2):
                sp.wait_ge(xt_stored[u], 16 + 16 * (TOK // CH // 2))

        @block.vector
        def _(dve):
            with dve.Fori(0, TOK // CH // 2) as i:
                for u in range(2):
                    c = i * 2 + u
                    dve.wait_ge(x_loaded[u], (i + 1) * 16)
                    for t in range(4):
                        last = dve.bn_stats(out=stats[:, t, :], in_=xin[:, u, t, :])
                    last.then_inc(stats_done, 1)
                    wait_alone(dve, passed, stats_done, c + 1)
                    for t in range(4):
                        last = dve.bn_aggr(out=mv[:, t, :], in_=stats[:, t, :])
                    last.then_inc(mv_done, 1)
                    dve.wait_ge(sd_done, c + 1)
                    dve.reciprocal(rstd[:, :], sd[:, :]).then_inc(rstd_done, 1)
                    dve.wait_ge(rstd_done, c + 1)
                    dve.wait_ge(turned, c * KT + KT)
                    for t in range(4):
                        last = dve.tensor_scalar(xn[:, u, t, :], xin[:, u, t, :], mv[:, t, 0:1],
                                                 rstd[:, t:t + 1], ALU.subtract, ALU.mult)
                    last.then_inc(normed, 1)
            dve.wait_ge(w_hi, HALVES)
            for h in range(HALVES):
                dve.tensor_tensor(wlo[:, h], wraw[:, h], f32(whi[:, h]), ALU.subtract).then_inc(w_lo, 1)

        @block.tensor
        def _(pe):
            pe.wait_ge(ident_ready, 1)
            with pe.Fori(0, TOK // CH // 2) as i:
                for u in range(2):
                    c = i * 2 + u
                    pe.wait_ge(normed, 2 + c + 1)
                    for k in range(KT):
                        if k == 0:
                            pe.wait_ge(copied, c * KT + KT)
                        for t in range(4):
                            last = pe.transpose(ps[:, 4 * u + k, t * P:(t + 1) * P],
                                                xn[:, u, t, k * P:(k + 1) * P], ident[:, :])
                        last.then_inc(turned, 1)

        @block.scalar
        def _(act):
            act.wait_ge(eps_ready, 1)
            act.wait_ge(w_loaded, 16 * 3 * HALVES)
            for h in range(HALVES):
                act.activation(whi[:, h], wraw[:, h], ACT.Copy).then_inc(w_hi, 1)
            with act.Fori(0, TOK // CH // 2) as i:
                for u in range(2):
                    c = i * 2 + u
                    act.wait_ge(mv_done, c + 1)
                    act.activation(sd[:, :], mv[:, :, 1], ACT.Sqrt, bias=eps[:, :]).then_inc(sd_done, 1)
                    for k in range(KT):
                        act.wait_ge(turned, 2 * KT + c * KT + k + 1)
                        if k == 0:
                            act.wait_ge(xt_stored[u], i * 16 + 16)
                        act.activation(xt[:, u, k, :], ps[:, 4 * u + k, :], ACT.Copy).then_inc(copied, 1)


NB = 256
BLOCKS = N // NB * HALF
NT = NB // P
STEPS = M // P // 2
CTX_CHUNKS, X_CHUNKS = M // CH, N // CH
CHUNKS = CTX_CHUNKS + X_CHUNKS
TILES = 4 * CTX_CHUNKS + 2 * X_CHUNKS
G = BLOCKS * STEPS
TBANKS = 3
RING = 4


def tiles_to(c):
    return 4 * min(c, CTX_CHUNKS) + 2 * max(c - CTX_CHUNKS, 0)


def attend(nc, ctxT, mask, xnT, w_split, attT, r_row, consts):
    ident = consts["ident"]
    with ExitStack() as ctx:
        def sb(name, shape, dt=F32, stack=ctx):
            return stack.enter_context(nc.sbuf_tensor(name, shape, dt))

        def sem(name):
            return ctx.enter_context(nc.semaphore("b_" + name))

        ks = sb("b_ks", [P, HALF, M], F32R)
        vs = sb("b_vs", [P, M // P, HALF, P], F32R)
        qhi = sb("b_qhi", [P, HALF, N], F32R)
        qlo = sb("b_qlo", [P, HALF, N], F32R)
        pthi = sb("b_pthi", [P, RING, 2 * NB], F32R)
        ptlo = sb("b_ptlo", [P, RING, 2 * NB], F32R)
        whi = sb("b_whi", [P, KT, 3, HC], F32R)
        wlo = sb("b_wlo", [P, KT, 3, HC], F32R)
        raw = sb("b_raw", [P, KT, CH])
        mask_in = sb("b_mask_in", [P, NT, M], U8)
        mask_add = sb("b_mask_add", [P, 2 * NT, M], BF16)
        lowest = sb("b_lowest", [P, 2 * NT, 2])
        sums = sb("b_sums", [P, 2 * NT, 2])
        total = sb("b_total", [P, NT])
        recip = sb("b_recip", [P, 2, NT])
        o_both = sb("b_o_both", [HD, 2, 2, NB])
        r_all = sb("b_r_all", [HD, 2, NB])
        o_sum = sb("b_o_sum", [HD, 2, NB])
        o_out = sb("b_o_out", [HD, 2, NB])
        with ExitStack() as first:
            probs = sb("b_probs", [P, 2 * NT, M], F32, first)
        with ExitStack() as second:
            xhi = sb("b_xhi", [P, 2, KT, CH], F32R, second)
            xlo = sb("b_xlo", [P, 2, KT, CH], F32R, second)
        ps = ctx.enter_context(nc.psum_tensor("b_ps", [P, 8, CH], F32))
        SB, TB, OB = 0, 4, 7

        const_ready = sem("const_ready")
        passed = sem("passed")
        w_loaded, raw_loaded = sem("w_loaded"), sem("raw_loaded")
        x_hi, x_lo = sem("x_hi"), sem("x_lo")
        tile_done = sem("tile_done")
        tile_hi, tile_lo = sem("tile_hi"), sem("tile_lo")
        scored = sem("scored")
        maxed = sem("maxed")
        exped = sem("exped")
        turned = sem("turned")
        pt_hi, pt_lo = sem("pt_hi"), sem("pt_lo")
        pv_done = sem("pv_done")
        totalled, inverted = sem("totalled"), sem("inverted")
        r_out = [sem(f"r_out{i}") for i in range(2)]
        r_in = [sem(f"r_in{i}") for i in range(2)]
        o_copied = sem("o_copied")
        o_summed = sem("o_summed")
        o_scaled = sem("o_scaled")
        o_stored = [sem(f"o_stored{i}") for i in range(2)]
        mask_loaded = [sem(f"mask_loaded{i}") for i in range(NT)]
        mask_made = sem("mask_made")
        block = ctx.enter_context(nc.Block())

        QK = 4 * BLOCKS

        def split_hi(act, it, c, tile):
            for n in range(4 if c < CTX_CHUNKS else 2):
                act.wait_ge(tile_done, 4 + it * TILES + tile + 1)
                bank = ps[:, SB + tile % 4, :]
                if c < CTX_CHUNKS and n < 2:
                    for a in range(2):
                        last = act.activation(ks[0:HD, 2 * n + a, c * CH:(c + 1) * CH],
                                              bank[a * HD:(a + 1) * HD, :], ACT.Copy)
                elif c < CTX_CHUNKS:
                    t = 4 * c + 2 * (n - 2)
                    last = act.activation(vs[:, t:t + 2, :, 0:HD],
                                          bank.rearrange("p (t h d) -> p t h d", t=2, h=HALF), ACT.Copy)
                else:
                    for a in range(2):
                        for twice in range(2):
                            col = (c - CTX_CHUNKS) * CH
                            last = act.activation(qhi[twice * HD:(twice + 1) * HD, 2 * n + a, col:col + CH],
                                                  bank[a * HD:(a + 1) * HD, :], ACT.Copy)
                last.then_inc(tile_hi, 1)
                tile += 1
            return tile

        def split_lo(dve, it, c, tile):
            for n in range(4 if c < CTX_CHUNKS else 2):
                dve.wait_ge(tile_hi, 4 + it * TILES + tile + 1)
                bank = ps[:, SB + tile % 4, :]
                if c < CTX_CHUNKS and n < 2:
                    for a in range(2):
                        cols = slice(c * CH, (c + 1) * CH)
                        last = dve.tensor_tensor(ks[HD:P, 2 * n + a, cols], bank[a * HD:(a + 1) * HD, :],
                                                 f32(ks[0:HD, 2 * n + a, cols]), ALU.subtract)
                elif c < CTX_CHUNKS:
                    t = 4 * c + 2 * (n - 2)
                    last = dve.tensor_tensor(vs[:, t:t + 2, :, HD:P],
                                             bank.rearrange("p (t h d) -> p t h d", t=2, h=HALF),
                                             f32(vs[:, t:t + 2, :, 0:HD]), ALU.subtract)
                else:
                    for a in range(2):
                        for twice in range(2):
                            cols = slice((c - CTX_CHUNKS) * CH, (c - CTX_CHUNKS + 1) * CH)
                            last = dve.tensor_tensor(qlo[twice * HD:(twice + 1) * HD, 2 * n + a, cols],
                                                     bank[a * HD:(a + 1) * HD, :],
                                                     f32(qhi[0:HD, 2 * n + a, cols]), ALU.subtract)
                last.then_inc(tile_lo, 1)
                tile += 1
            return tile

        @block.sync
        def _(sp):
            def load_chunk(b, it, c):
                sp.wait_ge(x_lo, it * CHUNKS + c + 1)
                if c < CTX_CHUNKS:
                    src = ctxT[bass.ds(b, 1), :, c * CH:(c + 1) * CH].rearrange("a (k p) m -> p (a k) m", p=P)
                else:
                    src = rows_by_tile(xnT[:, bass.ds(b * N + (c - CTX_CHUNKS) * CH, CH)], KT)
                sp.dma_start(raw[:, :, :], src).then_inc(raw_loaded, 16)

            def load_mask(b, it, nb, nt):
                wait_alone(sp, passed, mask_made, it * NT * 4 + (nb - 1) * NT + nt + 1 + NT)
                row = nb * NB + nt * P
                sp.dma_start(mask_in[:, nt, :], mask[bass.ds(b, 1), row:row + P, :].rearrange(
                    "a p m -> p (a m)")).then_inc(mask_loaded[nt], 16)

            with sp.Fori(0, B) as b:
                with sp.Fori(0, HALVES) as half:
                    it = b * HALVES + half
                    sp.wait_ge(tile_done, 4 + it * TILES)
                    sp.dma_start(f32(whi[:, :, :, :].rearrange("p k a n -> p (k a n)")),
                                 w_split[bass.ds(half, 1), 0].rearrange("a p n -> p (a n)")).then_inc(w_loaded, 16)
                    sp.dma_start(f32(wlo[:, :, :, :].rearrange("p k a n -> p (k a n)")),
                                 w_split[bass.ds(half, 1), 1].rearrange("a p n -> p (a n)")).then_inc(w_loaded, 16)
                    load_chunk(b, it, 0)
                    for nt in range(NT):
                        load_mask(b, it, 0, nt)
                    for c in range(1, CHUNKS):
                        load_chunk(b, it, c)
                    for j in range(BLOCKS):
                        if j // HALF < 3 and j % HALF < NT:
                            load_mask(b, it, j // HALF + 1, j % HALF)
                        sp.wait_ge(inverted, it * BLOCKS + j + 1)
                        sp.dma_start(r_row[j % 2].rearrange("(p t) -> p t", p=P),
                                     recip[:, j % 2, :]).then_inc(r_out[j % 2], 16)
                        sp.wait_ge(r_out[j % 2], 16 + it * 8 * 16 + j // 2 * 16 + 16)
                        sp.wait_ge(o_scaled, it * BLOCKS + j + 1)
                        sp.dma_start(r_all[:, j % 2, :], r_row[j % 2:j % 2 + 1, :].partition_broadcast(HD)
                                     ).then_inc(r_in[j % 2], 16)

        @block.gpsimd
        def _(pool):
            free_from_the_start(pool, (x_lo, 1), (tile_done, 4), (tile_hi, 4), (tile_lo, 4), (maxed, 2),
                                (turned, TBANKS), (pt_hi, TBANKS), (pt_lo, TBANKS), (pv_done, RING), (o_copied, 1),
                                (o_scaled, 2), (mask_made, NT), (r_out[0], 16), (r_out[1], 16))
            pool.sem_inc(const_ready, 1)

            def make_mask(it, nb, nt):
                pool.wait_ge(mask_loaded[nt], it * 4 * 16 + nb * 16 + 16)
                wait_alone(pool, passed, maxed, 2 + it * QK + max(nb - 1, 0) * HALF * 4)
                pool.tensor_scalar(mask_add[:, nb % 2 * NT + nt, :], mask_in[:, nt, :], -1.0, BIG,
                                   ALU.add, ALU.mult).then_inc(mask_made, 1)

            with pool.Fori(0, B) as b:
                with pool.Fori(0, HALVES) as half:
                    it = b * HALVES + half
                    for nt in range(NT):
                        make_mask(it, 0, nt)
                    for j in range(BLOCKS):
                        nb, h, s = j // HALF, j % HALF, j % 2
                        if nb < 3 and h < NT:
                            make_mask(it, nb + 1, h)
                        pool.wait_ge(o_copied, 1 + it * BLOCKS + j + 1)
                        pool.tensor_tensor(o_sum[:, s, :], o_both[:, s, 0, :], o_both[:, s, 1, :],
                                           ALU.add).then_inc(o_summed, 1)
                        pool.wait_ge(r_in[s], it * 8 * 16 + j // 2 * 16 + 16)
                        if j >= 2:
                            pool.wait_ge(o_stored[s], it * 8 * 16 + j // 2 * 16)
                        pool.wait_ge(o_summed, it * BLOCKS + j + 1)
                        pool.tensor_tensor(o_out[:, s, :].rearrange("d (t p) -> d t p", t=NT),
                                           o_sum[:, s, :].rearrange("d (t p) -> d t p", t=NT),
                                           r_all[:, s, :].rearrange("d (p t) -> d t p", t=NT),
                                           ALU.mult).then_inc(o_scaled, 1)
                        wait_alone(pool, passed, o_scaled, 2 + it * BLOCKS + j + 1)
                        pool.dma_start(attT[bass.ds(half * HC + h * HD, HD), bass.ds(b * N + nb * NB, NB)],
                                       o_out[:, s, :]).then_inc(o_stored[s], 16)
                    for s in range(2):
                        pool.wait_ge(o_stored[s], it * 8 * 16 + 8 * 16)

        @block.scalar
        def _(act):
            act.wait_ge(const_ready, 1)

            def exp(it, j, e):
                if not 0 <= j < BLOCKS:
                    return
                nt, c = e // 2, e % 2
                s = j % 2 * NT + nt
                if c == 0:
                    act.wait_ge(maxed, 2 + it * QK + 4 * j + 2 * nt + 2)
                piece = probs[:, s, c * 1024:(c + 1) * 1024]
                act.activation(piece, piece, ACT.Exp, bias=lowest[:, s, 1:2], scale=-1.0,
                               accum_out=sums[:, s, c:c + 1]).then_inc(exped, 1)

            def turned_hi(it, j, d):
                if not 0 <= j < BLOCKS:
                    return
                g = j * STEPS + d
                act.wait_ge(turned, TBANKS + it * G + g + 1)
                act.wait_ge(pv_done, it * G + g + 1)
                act.activation(pthi[:, g % RING, :], ps[:, TB + g % TBANKS, :], ACT.Copy).then_inc(pt_hi, 1)

            def copy_out(it, j):
                if not 0 <= j < BLOCKS:
                    return
                act.wait_ge(pv_done, RING + it * G + STEPS * (j + 1))
                act.wait_ge(o_scaled, it * BLOCKS + j + 1)
                for part in range(2):
                    last = act.activation(o_both[:, j % 2, part, :],
                                          ps[part * HD:(part + 1) * HD, OB, 0:NB], ACT.Copy)
                last.then_inc(o_copied, 1)

            with act.Fori(0, B) as b:
                with act.Fori(0, HALVES) as half:
                    it = b * HALVES + half
                    act.wait_ge(turned, TBANKS + it * G)
                    tile = 0
                    for c in range(CHUNKS):
                        act.wait_ge(raw_loaded, (it * CHUNKS + c + 1) * 16)
                        act.wait_ge(tile_done, 4 + it * TILES + (tiles_to(c - 1) if c >= 1 else -2))
                        act.activation(xhi[:, c % 2], raw[:, :, :], ACT.Copy).then_inc(x_hi, 1)
                        if c >= 1:
                            tile = split_hi(act, it, c - 1, tile)
                    tile = split_hi(act, it, CHUNKS - 1, tile)
                    for j in range(-1, BLOCKS + 1):
                        turned_hi(it, j, 1)
                        turned_hi(it, j, 2)
                        exp(it, j + 1, 0)
                        copy_out(it, j - 1)
                        turned_hi(it, j, 3)
                        exp(it, j + 1, 1)
                        for d in (4, 5, 6):
                            turned_hi(it, j, d)
                        exp(it, j + 1, 2)
                        turned_hi(it, j, 7)
                        exp(it, j + 1, 3)
                        turned_hi(it, j + 1, 0)

        @block.vector
        def _(dve):
            def mask_and_max(it, j, k):
                if not 0 <= j < BLOCKS:
                    return
                nb, h, nt, c = j // HALF, j % HALF, k // 2, k % 2
                s = j % 2 * NT + nt
                if h == 0 and c == 0:
                    dve.wait_ge(mask_made, NT + it * NT * 4 + nb * NT + nt + 1)
                if c == 1:
                    dve.wait_ge(maxed, 2 + it * QK + 4 * j + k)
                wait_alone(dve, passed, scored, it * QK + 4 * j + k + 1)
                dve.tensor_tensor_reduce(
                    out=probs[:, s, c * 1024:(c + 1) * 1024],
                    in0=ps[:, SB + 2 * (k % 2):SB + 2 * (k % 2) + 2, :].rearrange("p a n -> p (a n)"),
                    in1=mask_add[:, nb % 2 * NT + nt, c * 1024:(c + 1) * 1024], scale=-SCALE,
                    scalar=BIG if c == 0 else lowest[:, s, 0:1], op0=ALU.add, op1=ALU.min,
                    accum_out=lowest[:, s, c:c + 1]).then_inc(maxed, 1)

            def turned_lo(it, j, d):
                if not 0 <= j < BLOCKS:
                    return
                g = j * STEPS + d
                dve.wait_ge(pt_hi, TBANKS + it * G + g + 1)
                dve.tensor_tensor(ptlo[:, g % RING, :], ps[:, TB + g % TBANKS, :],
                                  f32(pthi[:, g % RING, :]), ALU.subtract).then_inc(pt_lo, 1)

            def invert(it, j):
                if not 0 <= j < BLOCKS:
                    return
                s = j % 2 * NT
                dve.wait_ge(exped, it * QK + 4 * j + 4)
                dve.tensor_tensor(total[:, :], sums[:, s:s + NT, 0], sums[:, s:s + NT, 1],
                                  ALU.add).then_inc(totalled, 1)
                dve.wait_ge(totalled, it * BLOCKS + j + 1)
                dve.wait_ge(r_out[j % 2], 16 + it * 8 * 16 + j // 2 * 16)
                dve.reciprocal(recip[:, j % 2, :], total[:, :]).then_inc(inverted, 1)

            with dve.Fori(0, B) as b:
                with dve.Fori(0, HALVES) as half:
                    it = b * HALVES + half
                    tile = 0
                    for c in range(CHUNKS):
                        dve.wait_ge(x_hi, it * CHUNKS + c + 1)
                        dve.tensor_tensor(xlo[:, c % 2], raw[:, :, :], f32(xhi[:, c % 2]),
                                          ALU.subtract).then_inc(x_lo, 1)
                        if c >= 1:
                            tile = split_lo(dve, it, c - 1, tile)
                    tile = split_lo(dve, it, CHUNKS - 1, tile)
                    for j in range(-2, BLOCKS):
                        turned_lo(it, j, 1)
                        turned_lo(it, j, 2)
                        mask_and_max(it, j + 1, 2)
                        turned_lo(it, j, 3)
                        mask_and_max(it, j + 1, 3)
                        invert(it, j)
                        for d in (4, 5, 6, 7):
                            turned_lo(it, j, d)
                        mask_and_max(it, j + 2, 0)
                        mask_and_max(it, j + 2, 1)
                        turned_lo(it, j + 1, 0)

        @block.tensor
        def _(pe):
            def project(it, c, tile):
                s = c % 2
                parts = ((whi, xhi), (wlo, xhi), (whi, xlo))
                pe.wait_ge(x_lo, 1 + it * CHUNKS + c + 1)
                for n in range(4 if c < CTX_CHUNKS else 2):
                    pe.wait_ge(tile_lo, it * TILES + tile + 1)
                    bank = ps[:, SB + tile % 4, :]
                    if n < 2:
                        a = 1 if c < CTX_CHUNKS else 0
                        last = products(pe, bank, [(w[:, k, a, n * P:(n + 1) * P], x[:, s, k, :])
                                                   for w, x in parts for k in range(KT)])
                    else:
                        for t in range(2):
                            col = (2 * (n - 2) + t) * P
                            last = products(pe, bank[:, t * HC:(t + 1) * HC],
                                            [(x[:, s, k, col:col + P], w[:, k, 2, :])
                                             for w, x in parts for k in range(KT)])
                    last.then_inc(tile_done, 1)
                    tile += 1
                return tile

            def score(it, j, k):
                if not 0 <= j < BLOCKS:
                    return
                nb, h, nt, c = j // HALF, j % HALF, k // 2, k % 2
                pe.wait_ge(maxed, it * QK + 4 * j + k + 1)
                row = nb * NB + nt * P
                for q in (qhi, qlo):
                    for m in range(2):
                        col = (2 * c + m) * CH
                        last = pe.matmul(ps[:, SB + 2 * (k % 2) + m, :], q[:, h, row:row + P],
                                         ks[:, h, col:col + CH], start=q is qhi, stop=q is qlo,
                                         skip_group_check=True)
                last.then_inc(scored, 1)

            def turn(it, j, d):
                if not 0 <= j < BLOCKS:
                    return
                g = j * STEPS + d
                if d == 0:
                    pe.wait_ge(exped, it * QK + 4 * j + 3)
                if d == STEPS // 2:
                    pe.wait_ge(exped, it * QK + 4 * j + 4)
                pe.wait_ge(pt_lo, it * G + g + 1)
                for m in range(2):
                    for nt in range(NT):
                        col = (2 * d + m) * P
                        last = pe.transpose(ps[:, TB + g % TBANKS, m * NB + nt * P:m * NB + (nt + 1) * P],
                                            probs[:, j % 2 * NT + nt, col:col + P], ident[:, :])
                last.then_inc(turned, 1)

            def weigh(it, j, d):
                if not 0 <= j < BLOCKS:
                    return
                v = j * STEPS + d
                pe.wait_ge(pt_lo, TBANKS + it * G + v + 1)
                if d == 0:
                    pe.wait_ge(o_copied, it * BLOCKS + j + 1)
                for m in range(2):
                    for pt in (pthi, ptlo):
                        last = pe.matmul(ps[:, OB, 0:NB], vs[:, 2 * d + m, j % HALF, :],
                                         pt[:, v % RING, m * NB:(m + 1) * NB],
                                         start=(d == 0 and m == 0 and pt is pthi),
                                         stop=(d == STEPS - 1 and m == 1 and pt is ptlo),
                                         skip_group_check=True)
                last.then_inc(pv_done, 1)

            with pe.Fori(0, B) as b:
                with pe.Fori(0, HALVES) as half:
                    it = b * HALVES + half
                    pe.wait_ge(w_loaded, it * 32 + 32)
                    tile = 0
                    for c in range(CHUNKS):
                        tile = project(it, c, tile)
                    pe.wait_ge(tile_lo, 4 + it * TILES + TILES)
                    for j in range(-2, BLOCKS + 1):
                        for d in (0, 1, 2):
                            turn(it, j, d)
                            weigh(it, j - 1, d + 5)
                        score(it, j + 1, 2)
                        score(it, j + 1, 3)
                        turn(it, j, 3)
                        turn(it, j, 4)
                        weigh(it, j, 0)
                        weigh(it, j, 1)
                        turn(it, j, 5)
                        weigh(it, j, 2)
                        turn(it, j, 6)
                        weigh(it, j, 3)
                        score(it, j + 2, 0)
                        turn(it, j, 7)
                        score(it, j + 2, 1)
                        weigh(it, j, 4)


LCHUNKS = TOK // CH
TILE = CH // P
ML = FL // P
MID = KT + ML


def light(nc, x, attT, wo, rt, gamma, w1, b1, w2, b2, z_rows, out, scores, consts):
    ident, eps = consts["ident"], consts["eps"]
    with ExitStack() as ctx:
        sb = lambda name, shape, dt=F32: ctx.enter_context(nc.sbuf_tensor("c_" + name, shape, dt))
        sem = lambda name: ctx.enter_context(nc.semaphore("c_" + name))
        wo_raw, wo_hi, wo_lo = (sb("wo" + n, [P, KT, D], dt) for n, dt in (("", F32), ("hi", F32R), ("lo", F32R)))
        w1_raw, w1_hi, w1_lo = (sb("w1" + n, [P, KT, FL], dt) for n, dt in (("", F32), ("hi", F32R), ("lo", F32R)))
        w2_raw, w2_hi, w2_lo = (sb("w2" + n, [P, ML, D], dt) for n, dt in (("", F32), ("hi", F32R), ("lo", F32R)))
        rt_all = sb("rt", [P, D])
        b2_all = sb("b2", [P, D])
        gamma_col = sb("gamma", [P, KT])
        b1_col = sb("b1", [P, ML])
        o_raw = sb("o_raw", [P, 2, KT, CH])
        o_hi, o_lo = sb("o_hi", [P, KT, CH], F32R), sb("o_lo", [P, KT, CH], F32R)
        x_in = sb("x_in", [P, 2, TILE, D])
        x1 = sb("x1", [P, 2, TILE, D])
        stats, mv = sb("stats", [P, TILE, 6]), sb("mv", [P, TILE, 2])
        sd, rstd = sb("sd", [P, TILE]), sb("rstd", [P, TILE])
        sq, nrm, nrm_min, rn = (sb(n, [P, TILE]) for n in ("sq", "nrm", "nrm_min", "rn"))
        s4 = sb("s4", [P, TILE])
        junk = sb("junk", [P, D])
        xn = sb("xn", [P, TILE, D])
        z = sb("z", [P, 2, TILE, D])
        z_hi, z_lo = sb("z_hi", [P, KT, CH], F32R), sb("z_lo", [P, KT, CH], F32R)
        g = sb("g", [P, ML, CH])
        g_hi, g_lo = sb("g_hi", [P, ML, CH], F32R), sb("g_lo", [P, ML, CH], F32R)
        y = sb("y", [P, TILE, D])
        ps = ctx.enter_context(nc.psum_tensor("c_ps", [P, 8, CH], F32))
        XB, MB, YB = 0, 4, 6

        passed = sem("passed")
        w_loaded, w_hi, w_lo = sem("w_loaded"), sem("w_hi"), sem("w_lo")
        o_loaded = [sem(f"o_loaded{u}") for u in range(2)]
        x_loaded = [sem(f"x_loaded{u}") for u in range(2)]
        o_is_hi, o_is_lo = sem("o_is_hi"), sem("o_is_lo")
        projected = sem("projected")
        x1_done, stats_done, mv_done, sd_done, rstd_done, xn_done = (
            sem(n) for n in ("x1_done", "stats_done", "mv_done", "sd_done", "rstd_done", "xn_done"))
        sq_done, junked, nrm_done, min_done, rn_done, z_done = (
            sem(n) for n in ("sq_done", "junked", "nrm_done", "min_done", "rn_done", "z_done"))
        z_stored = [sem(f"z_stored{u}") for u in range(2)]
        mid_done = sem("mid_done")
        z_is_hi, z_is_lo = sem("z_is_hi"), sem("z_is_lo")
        g_done, g_is_hi, g_is_lo = sem("g_done"), sem("g_is_hi"), sem("g_is_lo")
        b2_added = sem("b2_added")
        y_done, out_done = sem("y_done"), sem("out_done")
        out_stored = sem("out_stored")
        block = ctx.enter_context(nc.Block())
        x_rows = x.rearrange("b n d -> (b n) d")
        out_rows = out.rearrange("b n d -> (b n) d")
        weights = ((wo_raw, wo_hi, wo_lo), (w1_raw, w1_hi, w1_lo), (w2_raw, w2_hi, w2_lo))

        def steps(norm, split, last):
            pass

        def by_rows(ap, i, k):
            return ap[bass.ds((i * 2 + k) * CH, CH), :].rearrange("(t p) d -> p t d", p=P)

        @block.gpsimd
        def _(pool):
            free_from_the_start(pool, (projected, TILE), (x1_done, TILE), (mid_done, MID), (z_is_lo, KT),
                                (g_done, ML), (g_is_lo, ML), (y_done, TILE), (out_done, 2),
                                (z_stored[0], 16), (z_stored[1], 16), (out_stored, 16), (o_is_lo, 2))

            def add_b2(i, k):
                wait_alone(pool, passed, xn_done, i * 2 + k + 1)
                pool.tensor_tensor(x1[:, k % 2], x1[:, k % 2],
                                   b2_all[:, :].unsqueeze(1).broadcast_to([P, TILE, D]), ALU.add).then_inc(b2_added, 1)

            pool.wait_ge(w_loaded, 16 * 7)
            add_b2(0, 0)
            with pool.Fori(0, LCHUNKS // 2 - 1) as i:
                for k in range(2):
                    add_b2(i, k + 1)
            add_b2(0, LCHUNKS - 1)

        @block.sync
        def _(sp):
            def load(i, k):
                c, u = i * 2 + k, k % 2
                wait_alone(sp, passed, o_is_lo, c + 1)
                sp.dma_start(o_raw[:, u], rows_by_tile(attT[:, bass.ds(c * CH, CH)], KT)).then_inc(o_loaded[u], 16)
                if k >= 2:
                    wait_alone(sp, passed, x1_done, TILE + (c - 1) * TILE)
                sp.dma_start(x_in[:, u], by_rows(x_rows, i, k)).then_inc(x_loaded[u], 16)

            def store_z(i, k):
                c, u = i * 2 + k, k % 2
                wait_alone(sp, passed, z_done, c + 1)
                sp.dma_start(by_rows(z_rows, i, k), z[:, u]).then_inc(z_stored[u], 16)

            def store_out(i, k):
                c = i * 2 + k
                wait_alone(sp, passed, out_done, 2 + (c + 1) * TILE)
                sp.dma_start(by_rows(out_rows, i, k), y[:, :, :]).then_inc(out_stored, 16)

            for raw, w, kt in ((wo_raw, wo, KT), (w1_raw, w1, KT), (w2_raw, w2, ML)):
                sp.dma_start(raw[:, :, :], rows_by_tile(w, kt)).then_inc(w_loaded, 16)
            for all_, row in ((rt_all, rt), (b2_all, b2)):
                sp.dma_start(all_[:, :], row.rearrange("(a d) -> a d", a=1).partition_broadcast(P)
                             ).then_inc(w_loaded, 16)
            sp.dma_start(gamma_col[:, :], gamma).then_inc(w_loaded, 16)
            sp.dma_start(b1_col[:, :], b1).then_inc(w_loaded, 16)
            load(0, 0)
            load(0, 1)
            store_z(0, 0)
            with sp.Fori(0, LCHUNKS // 2 - 1) as i:
                for k in range(2):
                    load(i, k + 2)
                    store_z(i, k + 1)
                    store_out(i, k)
            store_z(0, LCHUNKS - 1)
            for k in (LCHUNKS - 2, LCHUNKS - 1):
                store_out(0, k)
            sp.wait_ge(out_stored, 16 + 16 * LCHUNKS)
            for u in range(2):
                sp.wait_ge(z_stored[u], 16 + 16 * LCHUNKS // 2)

        def in_order(eng, norm, light, split):
            split(0, 0)
            norm(0, 0)
            split(0, 1)
            with eng.Fori(0, LCHUNKS // 2 - 1) as i:
                for k in range(2):
                    norm(i, k + 1)
                    light(i, k)
                    split(i, k + 2)
            norm(0, LCHUNKS - 1)
            light(0, LCHUNKS - 2)
            light(0, LCHUNKS - 1)

        @block.scalar
        def _(act):
            act.wait_ge(w_loaded, 16 * 7)
            for raw, hi, lo in weights:
                act.activation(hi[:, :, :], raw[:, :, :], ACT.Copy).then_inc(w_hi, 1)

            def split(i, k):
                c, u = i * 2 + k, k % 2
                act.wait_ge(o_loaded[u], (i + k // 2 + 1) * 16)
                act.wait_ge(projected, TILE + c * TILE)
                act.activation(o_hi[:, :, :], o_raw[:, u], ACT.Copy).then_inc(o_is_hi, 1)

            def norm(i, k):
                c = i * 2 + k
                act.wait_ge(mv_done, c + 1)
                act.activation(sd[:, :], mv[:, :, 1], ACT.Sqrt, bias=eps[:, :]).then_inc(sd_done, 1)
                act.wait_ge(sq_done, c + 1)
                act.activation(nrm[:, :], sq[:, :], ACT.Sqrt).then_inc(nrm_done, 1)

            def light_branch(i, k):
                c = i * 2 + k
                for n in range(KT):
                    act.wait_ge(mid_done, MID + c * MID + n + 1)
                    act.activation(z_hi[:, n, :], ps[:, MB + n % 2, :], ACT.Copy,
                                   scale=gamma_col[:, n:n + 1]).then_inc(z_is_hi, 1)
                for m in range(ML):
                    act.wait_ge(mid_done, MID + c * MID + KT + m + 1)
                    act.wait_ge(g_is_lo, c * ML + ML)
                    act.activation(g[:, m, :], ps[:, MB + m % 2, :], ACT.Gelu,
                                   bias=b1_col[:, m:m + 1]).then_inc(g_done, 1)

            in_order(act, norm, light_branch, split)

        @block.vector
        def _(dve):
            for n, (raw, hi, lo) in enumerate(weights):
                dve.wait_ge(w_hi, n + 1)
                dve.tensor_tensor(lo[:, :, :], raw[:, :, :], f32(hi[:, :, :]), ALU.subtract).then_inc(w_lo, 1)

            def split(i, k):
                c, u = i * 2 + k, k % 2
                dve.wait_ge(o_is_hi, c + 1)
                dve.tensor_tensor(o_lo[:, :, :], o_raw[:, u], f32(o_hi[:, :, :]), ALU.subtract).then_inc(o_is_lo, 1)

            def norm(i, k):
                c, u = i * 2 + k, k % 2
                dve.wait_ge(x_loaded[u], (i + k // 2 + 1) * 16)
                for t in range(TILE):
                    dve.wait_ge(projected, TILE + c * TILE + t + 1)
                    dve.tensor_tensor(x1[:, u, t, :], ps[:, XB + t, :], x_in[:, u, t, :],
                                      ALU.add).then_inc(x1_done, 1)
                for t in range(TILE):
                    wait_alone(dve, passed, x1_done, TILE + c * TILE + t + 1)
                    last = dve.bn_stats(out=stats[:, t, :], in_=x1[:, u, t, :])
                last.then_inc(stats_done, 1)
                wait_alone(dve, passed, stats_done, c + 1)
                for t in range(TILE):
                    last = dve.bn_aggr(out=mv[:, t, :], in_=stats[:, t, :])
                last.then_inc(mv_done, 1)
                dve.wait_ge(sd_done, c + 1)
                dve.reciprocal(rstd[:, :], sd[:, :]).then_inc(rstd_done, 1)
                dve.wait_ge(rstd_done, c + 1)
                for t in range(TILE):
                    last = dve.tensor_scalar(xn[:, t, :], x1[:, u, t, :], mv[:, t, 0:1], rstd[:, t:t + 1],
                                             ALU.subtract, ALU.mult)
                last.then_inc(xn_done, 1)
                for t in range(TILE):
                    wait_alone(dve, passed, xn_done, c + 1)
                    if t == 0:
                        wait_alone(dve, passed, junked, c * 2 * TILE + 1)
                    for a, (other, total) in enumerate(((rt_all[:, :], s4), (xn[:, t, :], sq))):
                        if t + a > 0:
                            wait_alone(dve, passed, junked, 1 + (c * TILE + t) * 2 + a)
                        last = dve.tensor_tensor_reduce(out=junk[:, :], in0=xn[:, t, :], in1=other, scale=1.0,
                                                        scalar=0.0, op0=ALU.mult, op1=ALU.add,
                                                        accum_out=total[:, t:t + 1]).then_inc(junked, 1)
                dve.wait_ge(junked, 1 + (c + 1) * TILE * 2)
                dve.tensor_copy(scores[:, bass.ds(c * TILE, TILE)], s4[:, :]).then_inc(sq_done, 1)
                dve.wait_ge(nrm_done, c + 1)
                dve.tensor_scalar(nrm_min[:, :], nrm[:, :], 1e-12, None, ALU.max).then_inc(min_done, 1)
                dve.wait_ge(min_done, c + 1)
                dve.reciprocal(rn[:, :], nrm_min[:, :]).then_inc(rn_done, 1)
                dve.wait_ge(rn_done, c + 1)
                dve.wait_ge(z_stored[u], (i + k // 2 + 1) * 16)
                for t in range(TILE):
                    last = dve.tensor_scalar(z[:, u, t, :], xn[:, t, :], rn[:, t:t + 1], float(D) ** 0.5,
                                             ALU.mult, ALU.mult)
                last.then_inc(z_done, 1)

            def light_branch(i, k):
                c, u = i * 2 + k, k % 2
                for n in range(KT):
                    dve.wait_ge(z_is_hi, c * KT + n + 1)
                    dve.scalar_tensor_tensor(out=z_lo[:, n, :], in0=ps[:, MB + n % 2, :],
                                             scalar=gamma_col[:, n:n + 1], in1=f32(z_hi[:, n, :]),
                                             op0=ALU.mult, op1=ALU.subtract).then_inc(z_is_lo, 1)
                for m in range(ML):
                    dve.wait_ge(g_done, ML + c * ML + m + 1)
                    dve.wait_ge(y_done, TILE + c * TILE)
                    dve.tensor_copy(g_hi[:, m, :], g[:, m, :]).then_inc(g_is_hi, 1)
                    dve.wait_ge(g_is_hi, c * ML + m + 1)
                    dve.tensor_tensor(g_lo[:, m, :], g[:, m, :], f32(g_hi[:, m, :]),
                                      ALU.subtract).then_inc(g_is_lo, 1)
                dve.wait_ge(b2_added, c + 1)
                dve.wait_ge(out_stored, (c + 1) * 16)
                for t in range(TILE):
                    dve.wait_ge(y_done, TILE + c * TILE + t + 1)
                    dve.tensor_tensor(y[:, t, :], ps[:, YB + t % 2, :], x1[:, u, t, :],
                                      ALU.add).then_inc(out_done, 1)

            dve.memset(junk[:, :], 0.0).then_inc(junked, 1)
            in_order(dve, norm, light_branch, split)

        @block.tensor
        def _(pe):
            pe.wait_ge(w_lo, 3)

            def project(i, k):
                c = i * 2 + k
                pe.wait_ge(o_is_lo, 2 + c + 1)
                for t in range(TILE):
                    pe.wait_ge(x1_done, c * TILE + t + 1)
                    products(pe, ps[:, XB + t, :],
                             [(o[:, n, t * P:(t + 1) * P], w[:, n, :])
                              for o, w in ((o_hi, wo_hi), (o_lo, wo_hi), (o_hi, wo_lo))
                              for n in range(KT)]).then_inc(projected, 1)

            def light_branch(i, k):
                c, u = i * 2 + k, k % 2
                pe.wait_ge(z_done, c + 1)
                for n in range(KT):
                    if n < 2:
                        pe.wait_ge(g_done, c * ML + n + 1)
                    else:
                        pe.wait_ge(z_is_lo, KT + c * KT + n - 1)
                    for t in range(TILE):
                        last = pe.transpose(ps[:, MB + n % 2, t * P:(t + 1) * P],
                                            z[:, u, t, n * P:(n + 1) * P], ident[:, :])
                    last.then_inc(mid_done, 1)
                pe.wait_ge(z_is_lo, KT + c * KT + KT)
                for m in range(ML):
                    products(pe, ps[:, MB + m % 2, :],
                             [(w[:, n, m * P:(m + 1) * P], zz[:, n, :])
                              for w, zz in ((w1_hi, z_hi), (w1_lo, z_hi), (w1_hi, z_lo))
                              for n in range(KT)]).then_inc(mid_done, 1)
                pe.wait_ge(g_is_lo, ML + c * ML + ML)
                for t in range(TILE):
                    pe.wait_ge(out_done, c * TILE + t + 1)
                    products(pe, ps[:, YB + t % 2, :],
                             [(gg[:, m, t * P:(t + 1) * P], w[:, m, :])
                              for gg, w in ((g_hi, w2_hi), (g_lo, w2_hi), (g_hi, w2_lo))
                              for m in range(ML)]).then_inc(y_done, 1)

            in_order(pe, project, light_branch, lambda i, k: None)


NT_B = N // P


MH = FH // P
RAWS = 4


def weight_pieces(w1, w2, weights):
    w1_hi, w1_lo, w2_hi, w2_lo = weights
    return ([(w1[n * P:(n + 1) * P, :], w1_hi[:, n, :], w1_lo[:, n, :]) for n in range(KT)] +
            [(rows_by_tile(w2[n * CH:(n + 1) * CH, :], 4), w2_hi[:, 4 * n:4 * n + 4, :],
              w2_lo[:, 4 * n:4 * n + 4, :]) for n in range(FH // CH)])


def route(nc, scores, score_row, slots, w1, w2, weights):
    cols = B * NT_B
    with ExitStack() as ctx:
        sb = lambda name, shape, dt=F32: ctx.enter_context(nc.sbuf_tensor("d_" + name, shape, dt))
        sem = lambda name: ctx.enter_context(nc.semaphore("d_" + name))
        ones = sb("ones", [P, P])
        before = sb("before", [P, P])
        top1, top = sb("top1", [P, B]), sb("top", [P, B])
        neg_a = sb("neg_a", [P, B])
        shift = sb("shift", [P, B])
        zc, zs, e = (sb(n, [P, cols]) for n in ("zc", "zs", "e"))
        part, lg = sb("part", [P, B]), sb("lg", [P, B])
        sa = sb("sa", [P, cols])
        sel = sb("sel", [P, cols])
        one_minus = sb("one_minus", [P, cols])
        pay = sb("pay", [P, cols, 2])
        row = sb("row", [P, B, N])
        junk = sb("junk", [P, 3, N])
        raw = sb("raw", [P, RAWS, 4, CH])
        first_log = sb("first_log", [P, 1])
        counts = sb("counts", [P, 3, cols])
        rank1, rank = sb("rank1", [P, cols]), sb("rank", [P, cols])
        place = sb("place", [P, cols], I32)
        ps = ctx.enter_context(nc.psum_tensor("d_ps", [P, CH], F32))
        by_batch = lambda t: t[:, :].rearrange("p (b t) -> p b t", b=B)
        each = lambda t: t[:, :].unsqueeze(2).broadcast_to([P, B, NT_B])

        passed = sem("passed")
        ones_ready, before_zero, before_ready, ids_ready = (
            sem(n) for n in ("ones_ready", "before_zero", "before_ready", "ids_ready"))
        top_part, top_ready, start_ready = sem("top_part"), sem("top_ready"), sem("start_ready")
        cut, shifted, exped, parted, summed, logged, stepped = (
            sem(n) for n in ("cut", "shifted", "exped", "parted", "summed", "logged", "stepped"))
        sa_done, sa_min, sel_done, minus_done, weight_done = (
            sem(n) for n in ("sa_done", "sa_min", "sel_done", "minus_done", "weight_done"))
        row_out, row_in = sem("row_out"), [sem(f"row_in{b}") for b in range(B)]
        counted, rank1_done, rank_done, placed = (
            sem(n) for n in ("counted", "rank1_done", "rank_done", "placed"))
        scattered = sem("scattered")
        w_loaded = [sem(f"w_loaded{n}") for n in range(RAWS)]
        w_hi, w_lo = sem("w_hi"), sem("w_lo")
        block = ctx.enter_context(nc.Block())
        pieces = weight_pieces(w1, w2, weights)

        def raw_piece(n):
            place = raw[:, n % RAWS]
            return place.rearrange("p k d -> p (k d)") if n < KT else place

        def split_lo(dve, n):
            src, hi, lo = pieces[n]
            dve.wait_ge(w_hi, n + 1)
            dve.tensor_tensor(lo, raw_piece(n), f32(hi), ALU.subtract).then_inc(w_lo, 1)

        LOOPS = ITERS - 1
        FIRST_NEG_A = float(np.log(np.float32(N)) - np.log(np.float32(EFFECTIVE_K)))
        LOG_K = float(np.log(np.float32(EFFECTIVE_K)))

        @block.gpsimd
        def _(pool):
            pool.memset(ones[:, :], 1.0).then_inc(ones_ready, 1)
            pool.memset(before[:, :], 1.0).then_inc(before_zero, 1)
            pool.wait_ge(before_zero, 1)
            pool.affine_select(out=before[:, :], in_=before[:, :], compare_op=ALU.is_gt, fill=0.0, base=0,
                               pattern=[[-1, P]], channel_multiplier=1).then_inc(before_ready, 1)
            pool.iota(pay[:, :, 0].bitcast(I32), pattern=[[P, cols]], base=0,
                      channel_multiplier=1).then_inc(ids_ready, 1)
            pool.wait_ge(top_part, 1)
            pool.partition_all_reduce(top[:, :], top1[:, :], P, bass.bass_isa.ReduceOp.max).then_inc(top_ready, 1)
            pool.wait_ge(weight_done, 1)
            pool.wait_ge(ids_ready, 1)
            for n in range(cols):
                if n % NT_B == 0:
                    pool.wait_ge(placed, n // NT_B + 1)
                pool.indirect_dma_start(out=slots, out_offset=bass.IndirectOffsetOnAxis(place[:, n:n + 1], 0),
                                        in_=pay[:, n, :], in_offset=None).then_inc(scattered, 16)
            pool.wait_ge(scattered, 16 * cols)

        @block.scalar
        def _(act):
            act.wait_ge(ones_ready, 1)
            act.activation(first_log[:, :], ones[:, 0:1], ACT.Ln)
            with act.Fori(0, LOOPS) as i:
                act.wait_ge(shifted, i + 1)
                act.activation(e[:, :], zs[:, :], ACT.Exp).then_inc(exped, 1)
                act.wait_ge(summed, i + 1)
                act.activation(lg[:, :], ps[:, 0:B], ACT.Ln).then_inc(logged, 1)
            act.wait_ge(sa_min, 1)
            act.activation(sel[:, :], sa[:, :], ACT.Exp).then_inc(sel_done, 1)
            for n, (src, hi, lo) in enumerate(pieces):
                act.wait_ge(w_loaded[n % RAWS], 16 * (n // RAWS + 1))
                act.activation(hi, raw_piece(n), ACT.Copy).then_inc(w_hi, 1)

        @block.tensor
        def _(pe):
            pe.wait_ge(ones_ready, 1)
            with pe.Fori(0, LOOPS) as i:
                pe.wait_ge(parted, i + 1)
                pe.matmul(ps[:, 0:B], ones[:, :], part[:, :], start=True, stop=True).then_inc(summed, 1)

        @block.sync
        def _(sp):
            for n in range(RAWS):
                sp.dma_start(raw_piece(n), pieces[n][0]).then_inc(w_loaded[n], 16)
            sp.wait_ge(sel_done, 1)
            with nc.allow_non_contiguous_dma(reason="a column of scores to a row"):
                sp.dma_start(score_row.rearrange("(n p) -> p n", p=P), sel[:, :]).then_inc(row_out, 16)
            sp.wait_ge(row_out, 16)
            for b in range(B):
                sp.dma_start(row[:, b, :], score_row[b * N:(b + 1) * N].rearrange(
                    "(a n) -> a n", a=1).partition_broadcast(P)).then_inc(row_in[b], 16)
            for n in range(RAWS, len(pieces)):
                sp.wait_ge(w_lo, n - RAWS + 1)
                sp.dma_start(raw_piece(n), pieces[n][0]).then_inc(w_loaded[n % RAWS], 16)

        @block.vector
        def _(dve):
            dve.tensor_reduce(top1[:, :], by_batch(scores), AX.X, ALU.max).then_inc(top_part, 1)
            dve.memset(neg_a[:, :], FIRST_NEG_A).then_inc(stepped, 1)
            dve.wait_ge(top_ready, 1)
            with dve.Fori(0, LOOPS) as i:
                dve.wait_ge(stepped, i + 1)
                dve.tensor_tensor(by_batch(zc), by_batch(scores), each(neg_a), ALU.min).then_inc(cut, 1)
                dve.tensor_tensor(shift[:, :], top[:, :], neg_a[:, :], ALU.min).then_inc(cut, 1)
                dve.wait_ge(cut, 2 * i + 2)
                dve.tensor_tensor(by_batch(zs), by_batch(zc), each(shift), ALU.subtract).then_inc(shifted, 1)
                dve.wait_ge(exped, i + 1)
                dve.tensor_reduce(part[:, :], by_batch(e), AX.X, ALU.add).then_inc(parted, 1)
                dve.wait_ge(logged, i + 1)
                wait_alone(dve, passed, logged, i + 1)
                dve.scalar_tensor_tensor(out=neg_a[:, :], in0=lg[:, :], scalar=-LOG_K, in1=shift[:, :],
                                         op0=ALU.add, op1=ALU.add).then_inc(stepped, 1)
            dve.wait_ge(stepped, LOOPS + 1)
            dve.tensor_tensor(by_batch(zc), by_batch(scores), each(neg_a), ALU.subtract).then_inc(sa_done, 1)
            dve.wait_ge(sa_done, 1)
            dve.tensor_scalar(sa[:, :], zc[:, :], 0.0, None, ALU.min).then_inc(sa_min, 1)
            dve.wait_ge(sel_done, 1)
            dve.tensor_scalar(one_minus[:, :], sel[:, :], -1.0, 1.0, ALU.mult, ALU.add).then_inc(minus_done, 1)
            dve.wait_ge(minus_done, 1)
            dve.tensor_tensor(pay[:, :, 1], sel[:, :], one_minus[:, :], ALU.add).then_inc(weight_done, 1)
            for n in range(RAWS):
                split_lo(dve, n)
            dve.wait_ge(before_ready, 1)
            dve.memset(counts[:, :, :], 0.0).then_inc(counted, 1)
            done = 1
            for b in range(B):
                dve.wait_ge(row_in[b], 16)
                for t in range(NT_B):
                    n = b * NT_B + t
                    own = slice(t * P, (t + 1) * P)
                    mine = sel[:, n:n + 1]
                    dve.wait_ge(counted, done)
                    if t:
                        dve.tensor_scalar(junk[:, 0, 0:t * P], row[:, b, 0:t * P], mine, None, ALU.is_ge, ALU.add,
                                          accum_out=counts[:, 0, n:n + 1]).then_inc(counted, 1)
                        done += 1
                    dve.tensor_scalar(junk[:, 1, t * P:N], row[:, b, t * P:N], mine, None, ALU.is_gt, ALU.add,
                                      accum_out=counts[:, 1, n:n + 1]).then_inc(counted, 1)
                    dve.scalar_tensor_tensor(out=junk[:, 2, 0:P], in0=row[:, b, own], scalar=mine,
                                             in1=before[:, :], op0=ALU.is_equal, op1=ALU.mult,
                                             accum_out=counts[:, 2, n:n + 1]).then_inc(counted, 1)
                    done += 2
                own = slice(b * NT_B, (b + 1) * NT_B)
                dve.wait_ge(counted, done)
                dve.tensor_tensor(rank1[:, own], counts[:, 0, own], counts[:, 1, own], ALU.add).then_inc(rank1_done, 1)
                dve.wait_ge(rank1_done, b + 1)
                dve.tensor_tensor(rank[:, own], rank1[:, own], counts[:, 2, own], ALU.add).then_inc(rank_done, 1)
                dve.wait_ge(rank_done, b + 1)
                dve.tensor_scalar(place[:, own], rank[:, own], float(b * N), None, ALU.add).then_inc(placed, 1)
            for n in range(RAWS, len(pieces)):
                split_lo(dve, n)


ST = CHOSEN // P
USES = KT + MH
GR = 3


def heavy(nc, z_rows, slots, gamma, b1, b2, out, weights, consts):
    ident = consts["ident"]
    with ExitStack() as ctx:
        def sb(name, shape, dt=F32, stack=ctx):
            return stack.enter_context(nc.sbuf_tensor("e_" + name, shape, dt))

        sem = lambda name: ctx.enter_context(nc.semaphore("e_" + name))
        w1_hi, w1_lo, w2_hi, w2_lo = weights
        gamma_col, b1_col = sb("gamma", [P, KT]), sb("b1", [P, MH])
        b2_all = sb("b2", [P, D])
        slot = sb("slot", [P, B * ST, 2])
        z = sb("z", [P, 2 * ST, D])
        z_hi, z_lo = sb("z_hi", [P, KT, CH], F32R), sb("z_lo", [P, KT, CH], F32R)
        g = sb("g", [P, 2, CH])
        g_hi, g_lo = sb("g_hi", [P, GR, CH], F32R), sb("g_lo", [P, GR, CH], F32R)
        weight = sb("weight", [P, ST])
        rest = sb("rest", [P, ST, D])
        ps = ctx.enter_context(nc.psum_tensor("e_ps", [P, 8, CH], F32))
        YB, MB = 0, 4

        passed = sem("passed")
        small_loaded = sem("small_loaded")
        slot_loaded, rest_loaded = sem("slot_loaded"), sem("rest_loaded")
        z_loaded = [sem(f"z_loaded{b}") for b in range(B)]
        mid_done = sem("mid_done")
        z_is_hi, z_is_lo = sem("z_is_hi"), sem("z_is_lo")
        g_done, g_is_hi, g_is_lo = sem("g_done"), sem("g_is_hi"), sem("g_is_lo")
        used = sem("used")
        b2_added, y_done = sem("b2_added"), sem("y_done")
        y_stored = [sem(f"y_stored{t}") for t in range(ST)]
        weight_ready = sem("weight_ready")
        z_ready = sem("z_ready")
        block = ctx.enter_context(nc.Block())
        out_rows = out.rearrange("b n d -> (b n) d")

        @block.sync
        def _(sp):
            for b in range(B):
                sp.dma_start(slot[:, b * ST:(b + 1) * ST, :], slots[b * N:b * N + CHOSEN, :].rearrange(
                    "(t p) a -> p t a", p=P)).then_inc(slot_loaded, 16)
            sp.dma_start(gamma_col[:, :], gamma).then_inc(small_loaded, 16)
            sp.dma_start(b1_col[:, :], b1).then_inc(small_loaded, 16)
            sp.dma_start(b2_all[:, :], b2.rearrange("(a d) -> a d", a=1).partition_broadcast(P)
                         ).then_inc(small_loaded, 16)
            for b in range(B):
                sp.wait_ge(z_loaded[b], ST * 16)
                sp.sem_inc(z_ready, 1)

        @block.gpsimd
        def _(pool):
            def by_token(s):
                return bass.IndirectOffsetOnAxis(slot[:, s, 0:1].bitcast(I32), 0)

            free_from_the_start(pool, (mid_done, 0 + USES), (g_done, 2), (g_is_lo, 2), (used, GR),
                                (y_done, ST), (z_is_lo, 2))
            pool.wait_ge(slot_loaded, 16 * B)

            def load_z(b):
                for s in range(b * ST, (b + 1) * ST):
                    pool.indirect_dma_start(out=z[:, s % (2 * ST), :], out_offset=None, in_=z_rows,
                                            in_offset=by_token(s)).then_inc(z_loaded[b], 16)

            load_z(0)
            load_z(1)
            for b in range(B):
                for t in range(ST):
                    if b:
                        pool.wait_ge(y_stored[t], b * 16)
                    pool.indirect_dma_start(out=rest[:, t, :], out_offset=None, in_=out_rows,
                                            in_offset=by_token(b * ST + t)).then_inc(rest_loaded, 16)
                if b + 2 < B:
                    pool.wait_ge(mid_done, USES + b * USES + KT)
                    load_z(b + 2)
                for t in range(ST):
                    pool.wait_ge(y_done, ST + b * ST + t + 1)
                    pool.indirect_dma_start(out=out_rows, out_offset=by_token(b * ST + t),
                                            in_=rest[:, t, :], in_offset=None).then_inc(y_stored[t], 16)
            for t in range(ST):
                pool.wait_ge(y_stored[t], B * 16)

        @block.scalar
        def _(act):
            act.wait_ge(small_loaded, 48)
            with act.Fori(0, B) as b:
                for n in range(KT):
                    act.wait_ge(mid_done, USES + b * USES + n + 1)
                    act.activation(z_hi[:, n, :], ps[:, MB + n % 2, :], ACT.Copy,
                                   scale=gamma_col[:, n:n + 1]).then_inc(z_is_hi, 1)
                for m in range(MH):
                    act.wait_ge(mid_done, USES + b * USES + KT + m + 1)
                    act.wait_ge(g_is_lo, b * MH + m + 1)
                    act.activation(g[:, m % 2, :], ps[:, MB + m % 2, :], ACT.Gelu,
                                   bias=b1_col[:, m:m + 1]).then_inc(g_done, 1)

        @block.vector
        def _(dve):
            dve.wait_ge(small_loaded, 48)
            dve.wait_ge(slot_loaded, 16 * B)
            with dve.Fori(0, B) as b:
                dve.wait_ge(y_done, b * ST + ST)
                dve.tensor_copy(weight[:, :], slot[:, bass.ds(b * ST, ST), 1]).then_inc(weight_ready, 1)
                for n in range(KT):
                    dve.wait_ge(z_is_hi, b * KT + n + 1)
                    dve.scalar_tensor_tensor(out=z_lo[:, n, :], in0=ps[:, MB + n % 2, :],
                                             scalar=gamma_col[:, n:n + 1], in1=f32(z_hi[:, n, :]),
                                             op0=ALU.mult, op1=ALU.subtract).then_inc(z_is_lo, 1)
                for m in range(MH):
                    r = m % GR
                    dve.wait_ge(g_done, 2 + b * MH + m + 1)
                    if m < GR:
                        dve.wait_ge(used, GR + b * MH)
                    else:
                        dve.wait_ge(used, b * MH + m + 1)
                    dve.tensor_copy(g_hi[:, r, :], g[:, m % 2, :]).then_inc(g_is_hi, 1)
                    dve.wait_ge(g_is_hi, b * MH + m + 1)
                    dve.tensor_tensor(g_lo[:, r, :], g[:, m % 2, :], f32(g_hi[:, r, :]),
                                      ALU.subtract).then_inc(g_is_lo, 1)
                    if m >= MH - ST:
                        dve.wait_ge(weight_ready, b + 1)
                        t = m - (MH - ST)
                        wait_alone(dve, passed, rest_loaded, b * ST * 16 + ST * 16)
                        dve.scalar_tensor_tensor(out=rest[:, t, :], in0=b2_all[:, :],
                                                 scalar=weight[:, t:t + 1], in1=rest[:, t, :],
                                                 op0=ALU.mult, op1=ALU.add).then_inc(b2_added, 1)
                dve.wait_ge(b2_added, b * ST + ST)
                wait_alone(dve, passed, used, GR + b * MH + MH)
                for t in range(ST):
                    dve.scalar_tensor_tensor(out=rest[:, t, :], in0=ps[:, YB + t, :],
                                             scalar=weight[:, t:t + 1], in1=rest[:, t, :],
                                             op0=ALU.mult, op1=ALU.add).then_inc(y_done, 1)

        @block.tensor
        def _(pe):
            with pe.Fori(0, B // 2) as pair:
                for u in range(2):
                    b = pair * 2 + u
                    pe.wait_ge(z_ready, b + 1)
                    for n in range(KT):
                        if n < 2:
                            pe.wait_ge(g_done, b * MH + 2)
                        else:
                            pe.wait_ge(z_is_lo, 2 + b * KT + n - 1)
                        for t in range(ST):
                            last = pe.transpose(ps[:, MB + n % 2, t * P:(t + 1) * P],
                                                z[:, u * ST + t, n * P:(n + 1) * P], ident[:, :])
                        last.then_inc(mid_done, 1)
                    pe.wait_ge(z_is_lo, 2 + b * KT + KT)
                    pe.wait_ge(y_done, b * ST + ST)
                    for m in range(MH + 1):
                        if m < MH:
                            if m >= 2:
                                pe.wait_ge(g_done, b * MH + m + 1)
                            products(pe, ps[:, MB + m % 2, :],
                                     [(w[:, n, m * P:(m + 1) * P], zz[:, n, :])
                                      for w, zz in ((w1_hi, z_hi), (w1_lo, z_hi), (w1_hi, z_lo))
                                      for n in range(KT)]).then_inc(mid_done, 1)
                        if m >= 1:
                            v = m - 1
                            r = v % GR
                            pe.wait_ge(g_is_lo, 2 + b * MH + v + 1)
                            for t in range(ST):
                                for a, (gg, w) in enumerate(((g_hi, w2_hi), (g_lo, w2_hi), (g_hi, w2_lo))):
                                    last = pe.matmul(ps[:, YB + t, :], gg[:, r, t * P:(t + 1) * P], w[:, v, :],
                                                     start=(v == 0 and a == 0), stop=(v == MH - 1 and a == 2),
                                                     skip_group_check=True)
                            last.then_inc(used, 1)


def xattn_ffn(nc, x, ctxT, mask, wq, wkv, wo, rt, gamma_l, w1_l, b1_l, w2_l, b2_l,
              gamma_h, w1_h, b1_h, w2_h, b2_h, out):
    with ExitStack() as ctx:
        def dram(name, shape, dt=F32):
            return nc.dram_tensor(name, shape, dt, kind="Internal").ap()

        ident = ctx.enter_context(nc.sbuf_tensor("ident", [P, P], F32))
        eps = ctx.enter_context(nc.sbuf_tensor("eps", [P, 1], F32))
        scores = ctx.enter_context(nc.sbuf_tensor("scores", [P, B * NT_B], F32))
        consts = dict(ident=ident, eps=eps)
        xnT = dram("xnT", [D, TOK])
        w_split = dram("w_split", [HALVES, 2, P, KT * 3 * HC])
        attT = dram("attT", [D, TOK])
        r_row = dram("r_row", [2, NB])
        z_rows = dram("z_rows", [TOK, D])
        score_row = dram("score_row", [TOK])
        slots = dram("slots", [TOK, 2])
        prepare(nc, x, wq, wkv, xnT, w_split, consts)
        attend(nc, ctxT, mask, xnT, w_split, attT, r_row, consts)
        light(nc, x, attT, wo, rt, gamma_l, w1_l, b1_l, w2_l, b2_l, z_rows, out, scores, consts)
        weights = [ctx.enter_context(nc.sbuf_tensor(name, shape, F32R)) for name, shape in (
            ("w1_hi", [P, KT, FH]), ("w1_lo", [P, KT, FH]), ("w2_hi", [P, MH, D]), ("w2_lo", [P, MH, D]))]
        route(nc, scores, score_row, slots, w1_h, w2_h, weights)
        heavy(nc, z_rows, slots, gamma_h, b1_h, b2_h, out, weights, consts)


def kernel(x, ctx_1024, mask_BxSxS2_bf1, L0_xattn_Wq, L0_xattn_Wkv, L0_xattn_Wo, L0_ffn_routing_token,
           L0_ffn_gamma_l, L0_ffn_w1_l, L0_ffn_b1_l, L0_ffn_w2_l, L0_ffn_b2_l, L0_ffn_gamma_h,
           L0_ffn_w1_h, L0_ffn_b1_h, L0_ffn_w2_h, L0_ffn_b2_h):
    import concourse.bacc as bacc
    from concourse.bass_utils import run_bass_kernel_spmd

    def columns(v):
        return np.ascontiguousarray(np.asarray(v).reshape(-1, P).T)

    def turned(w):
        return np.ascontiguousarray(np.asarray(w).T)

    arrays = {
        "x": np.asarray(x),
        "ctxT": np.ascontiguousarray(np.asarray(ctx_1024).transpose(0, 2, 1)),
        "mask": np.asarray(mask_BxSxS2_bf1).view(np.uint8),
        "wq": np.asarray(L0_xattn_Wq), "wkv": np.asarray(L0_xattn_Wkv), "wo": np.asarray(L0_xattn_Wo),
        "rt": np.asarray(L0_ffn_routing_token),
        "gamma_l": columns(L0_ffn_gamma_l), "w1_l": turned(L0_ffn_w1_l), "b1_l": columns(L0_ffn_b1_l),
        "w2_l": turned(L0_ffn_w2_l), "b2_l": np.asarray(L0_ffn_b2_l),
        "gamma_h": columns(L0_ffn_gamma_h), "w1_h": turned(L0_ffn_w1_h), "b1_h": columns(L0_ffn_b1_h),
        "w2_h": turned(L0_ffn_w2_h), "b2_h": np.asarray(L0_ffn_b2_h),
    }
    nc = bacc.Bacc("TRN2", target_bir_lowering=False, num_devices=1)
    aps = {n: nc.dram_tensor(n, a.shape, mybir.dt.from_np(a.dtype), kind="ExternalInput").ap()
           for n, a in arrays.items()}
    out = nc.dram_tensor("out", (B, N, D), F32, kind="ExternalOutput").ap()
    xattn_ffn(nc, out=out, **aps)
    r = run_bass_kernel_spmd(nc, [arrays], core_ids=[0])
    return r.results[0]["out"]
```

```python
from contextlib import ExitStack

import concourse.bass as bass
import numpy as np
from concourse import mybir

F32 = mybir.dt.float32
F32R = mybir.dt.float32r
BF16 = mybir.dt.bfloat16
U8 = mybir.dt.uint8
I32 = mybir.dt.int32
ALU = mybir.AluOpType
ACT = mybir.ActivationFunctionType
AX = mybir.AxisListType

P = 128
B, N, M, D = 4, 1024, 2048, 512
H, HD = 8, 64
KT = D // P
HALF = 4
HALVES = H // HALF
HC = HALF * HD
CH = 512
SCALE = HD ** -0.5
EPS = 1e-5
ITERS = 50
CHOSEN = 512
EFFECTIVE_K = min(CHOSEN * 9.0 / 8.0, N)
TOK = B * N
FL = 256
FH = 2048
BIG = 3.4028235e38


def f32(ap):
    return ap.bitcast(F32)


def rows_by_tile(ap, k):
    return ap.rearrange("(k p) n -> p k n", k=k)


def free_from_the_start(eng, *rings):
    for sem, slots in rings:
        eng.sem_inc(sem, slots)


def wait_alone(eng, passed, sem, value):
    eng.wait_ge(sem, value)
    eng.sem_inc(passed, 1)


def products(pe, out, pairs, last=True):
    for n, (w, m) in enumerate(pairs):
        ins = pe.matmul(out, w, m, start=(n == 0), stop=last and n == len(pairs) - 1,
                        skip_group_check=True)
    return ins


def prepare(nc, x, wq, wkv, ctxT, xnT, w_split, first_w, first_raw, consts):
    eps, ident = consts["eps"], consts["ident"]
    with ExitStack() as ctx:
        sb = lambda name, shape, dt=F32: ctx.enter_context(nc.sbuf_tensor(name, shape, dt))
        sem = lambda name: ctx.enter_context(nc.semaphore(name))
        xin = sb("a_xin", [P, 2, 4, D])
        xn = sb("a_xn", [P, 2, 4, D])
        xt = sb("a_xt", [P, 2, KT, CH])
        stats = sb("a_stats", [P, 4, 6])
        mv = sb("a_mv", [P, 4, 2])
        sd = sb("a_sd", [P, 4])
        rstd = sb("a_rstd", [P, 4])
        wraw = sb("a_wraw", [P, HALVES, KT, 3, HC])
        whi = [first_w[0], sb("a_whi", [P, KT, 3, HC], F32R)]
        wlo = [first_w[1], sb("a_wlo", [P, KT, 3, HC], F32R)]
        ps = ctx.enter_context(nc.psum_tensor("a_ps", [P, 8, CH], F32))

        x_loaded = [sem(f"a_x_loaded{i}") for i in range(2)]
        w_loaded = [sem(f"a_w_loaded{h}") for h in range(HALVES)]
        w_hi = sem("a_w_hi")
        w_lo = sem("a_w_lo")
        w_stored = sem("a_w_stored")
        raw_loaded = sem("a_raw_loaded")
        passed = sem("a_passed")
        stats_done = sem("a_stats_done")
        mv_done = sem("a_mv_done")
        sd_done = sem("a_sd_done")
        rstd_done = sem("a_rstd_done")
        normed = sem("a_normed")
        turned = sem("a_turned")
        copied = sem("a_copied")
        xt_stored = [sem(f"a_xt_stored{i}") for i in range(2)]
        ident_zero = sem("a_ident_zero")
        ident_ready = sem("a_ident_ready")
        eps_ready = sem("a_eps_ready")

        x_rows = x.rearrange("b n d -> (b n) d")
        block = ctx.enter_context(nc.Block())

        @block.gpsimd
        def _(pool):
            free_from_the_start(pool, (normed, 2), (turned, 2 * KT), (copied, 2 * KT),
                                (xt_stored[0], 16), (xt_stored[1], 16))
            pool.memset(ident[:, :], 0.0).then_inc(ident_zero, 1)
            pool.memset(eps[:, :], EPS).then_inc(eps_ready, 1)
            pool.wait_ge(ident_zero, 1)
            pool.affine_select(out=ident[:, :], in_=ident[:, :], compare_op=ALU.not_equal, fill=1.0,
                               base=0, pattern=[[-1, P]], channel_multiplier=1).then_inc(ident_ready, 1)

        @block.sync
        def _(sp):
            for h in range(HALVES):
                for n, w in enumerate((wq[:, h * HC:(h + 1) * HC], wkv[:, h * HC:(h + 1) * HC],
                                       wkv[:, D + h * HC:D + (h + 1) * HC])):
                    sp.dma_start(wraw[:, h, :, n, :], rows_by_tile(w, KT)).then_inc(w_loaded[h], 16)
            with sp.Fori(0, TOK // CH // 2) as i:
                for u in range(2):
                    c = i * 2 + u
                    sp.wait_ge(normed, c + 1)
                    sp.dma_start(xin[:, u, :, :], x_rows[bass.ds(c * CH, CH), :].rearrange(
                        "(t p) d -> p t d", p=P)).then_inc(x_loaded[u], 16)
            sp.dma_start(first_raw[:, :, :], rows_by_tile(ctxT[0, :, 0:CH], KT)).then_inc(raw_loaded, 16)
            sp.wait_ge(raw_loaded, 16)
            sp.wait_ge(w_stored, 16 * 2 * HALVES)
            for u in range(2):
                sp.wait_ge(xt_stored[u], 16 + 16 * (TOK // CH // 2))

        @block.vector
        def _(dve):
            for h in range(HALVES):
                dve.wait_ge(w_hi, h + 1)
                dve.tensor_tensor(wlo[h][:, :, :, :], wraw[:, h], f32(whi[h][:, :, :, :]),
                                  ALU.subtract).then_inc(w_lo, 1)
            with dve.Fori(0, TOK // CH // 2) as i:
                for u in range(2):
                    c = i * 2 + u
                    dve.wait_ge(x_loaded[u], (i + 1) * 16)
                    for t in range(4):
                        last = dve.bn_stats(out=stats[:, t, :], in_=xin[:, u, t, :])
                    last.then_inc(stats_done, 1)
                    wait_alone(dve, passed, stats_done, c + 1)
                    for t in range(4):
                        last = dve.bn_aggr(out=mv[:, t, :], in_=stats[:, t, :])
                    last.then_inc(mv_done, 1)
                    dve.wait_ge(sd_done, c + 1)
                    dve.reciprocal(rstd[:, :], sd[:, :]).then_inc(rstd_done, 1)
                    dve.wait_ge(rstd_done, c + 1)
                    dve.wait_ge(turned, c * KT + KT)
                    for t in range(4):
                        last = dve.tensor_scalar(xn[:, u, t, :], xin[:, u, t, :], mv[:, t, 0:1],
                                                 rstd[:, t:t + 1], ALU.subtract, ALU.mult)
                    last.then_inc(normed, 1)

        @block.tensor
        def _(pe):
            pe.wait_ge(ident_ready, 1)
            with pe.Fori(0, TOK // CH // 2) as i:
                for u in range(2):
                    c = i * 2 + u
                    pe.wait_ge(normed, 2 + c + 1)
                    for k in range(KT):
                        if k == 0:
                            pe.wait_ge(copied, c * KT + KT)
                        for t in range(4):
                            last = pe.transpose(ps[:, 4 * u + k, t * P:(t + 1) * P],
                                                xn[:, u, t, k * P:(k + 1) * P], ident[:, :])
                        last.then_inc(turned, 1)

        @block.scalar
        def _(act):
            act.wait_ge(eps_ready, 1)
            for h in range(HALVES):
                act.wait_ge(w_loaded[h], 16 * 3)
                act.activation(whi[h][:, :, :, :], wraw[:, h], ACT.Copy).then_inc(w_hi, 1)
            for h in range(HALVES):
                act.wait_ge(w_hi, h + 1)
                act.dma_start(w_split[h, 0], f32(whi[h][:, :, :, :].rearrange("p k a n -> p (k a n)"))
                              ).then_inc(w_stored, 16)
                act.wait_ge(w_lo, h + 1)
                act.dma_start(w_split[h, 1], f32(wlo[h][:, :, :, :].rearrange("p k a n -> p (k a n)"))
                              ).then_inc(w_stored, 16)
            with act.Fori(0, TOK // CH // 2) as i:
                for u in range(2):
                    c = i * 2 + u
                    act.wait_ge(mv_done, c + 1)
                    act.activation(sd[:, :], mv[:, :, 1], ACT.Sqrt, bias=eps[:, :]).then_inc(sd_done, 1)
                    for k in range(KT):
                        act.wait_ge(turned, 2 * KT + c * KT + k + 1)
                        if k == 0:
                            act.wait_ge(xt_stored[u], i * 16 + 16)
                        act.activation(xt[:, u, k, :], ps[:, 4 * u + k, :], ACT.Copy).then_inc(copied, 1)
                    wait_alone(act, passed, copied, 2 * KT + c * KT + KT)
                    act.dma_start(rows_by_tile(xnT[:, bass.ds(c * CH, CH)], KT),
                                  xt[:, u, :, :]).then_inc(xt_stored[u], 16)


NB = 256
BLOCKS = N // NB * HALF
NT = NB // P
STEPS = M // P // 2
CTX_CHUNKS, X_CHUNKS = M // CH, N // CH
CHUNKS = CTX_CHUNKS + X_CHUNKS
TILES = 4 * CTX_CHUNKS + 2 * X_CHUNKS
G = BLOCKS * STEPS
TBANKS = 3
RING = 4


ORDER = ((True, 0), (True, 1), (False, 0), (True, 2), (False, 1), (True, 3))
RAW_SLOT = (0, 0, 1, 2, 0, 1)


def tiles_to(c):
    return sum(4 if of_context else 2 for of_context, _ in ORDER[:c])


def loads_of(it, c):
    per_round = RAW_SLOT.count(RAW_SLOT[c])
    return (it * per_round + RAW_SLOT[:c + 1].count(RAW_SLOT[c])) * 16


def attend(nc, ctxT, mask, xnT, w_split, first_w, raw_0, attT, r_row, consts):
    ident = consts["ident"]
    with ExitStack() as ctx:
        def sb(name, shape, dt=F32, stack=ctx):
            return stack.enter_context(nc.sbuf_tensor(name, shape, dt))

        def sem(name):
            return ctx.enter_context(nc.semaphore("b_" + name))

        ks = sb("b_ks", [P, HALF, M], F32R)
        vs = sb("b_vs", [P, M // P, HALF, P], F32R)
        qhi = sb("b_qhi", [P, HALF, N], F32R)
        qlo = sb("b_qlo", [P, HALF, N], F32R)
        whi, wlo = first_w
        mask_in = sb("b_mask_in", [P, NT, M], U8)
        mask_add = sb("b_mask_add", [P, 2 * NT, M], BF16)
        lowest = sb("b_lowest", [P, 2 * NT, 2])
        sums = sb("b_sums", [P, 2 * NT, 2])
        total = sb("b_total", [P, NT])
        recip = sb("b_recip", [P, 2, NT])
        o_both = sb("b_o_both", [HD, 2, 2, NB])
        r_all = sb("b_r_all", [HD, 2, NB])
        o_sum = sb("b_o_sum", [HD, 2, NB])
        o_out = sb("b_o_out", [HD, 2, NB])
        with ExitStack() as first:
            pthi = sb("b_pthi", [P, RING, 2 * NB], F32R, first)
            ptlo = sb("b_ptlo", [P, RING, 2 * NB], F32R, first)
            probs = sb("b_probs", [P, 2 * NT, M], F32, first)
        with ExitStack() as second:
            raw_1 = sb("b_raw_1", [P, KT, CH], F32, second)
            raw_2 = sb("b_raw_2", [P, KT, CH], F32, second)
            xs = sb("b_xs", [P, 2, 2, KT, CH], F32R, second)
        raws = (raw_0, raw_1, raw_2)
        ps = ctx.enter_context(nc.psum_tensor("b_ps", [P, 8, CH], F32))
        SB, TB, OB = 0, 4, 7

        const_ready = sem("const_ready")
        passed = sem("passed")
        w_loaded = sem("w_loaded")
        raw_loaded = [sem(f"raw_loaded{n}") for n in range(3)]
        x_hi, x_lo = sem("x_hi"), sem("x_lo")
        tile_done = sem("tile_done")
        tile_hi, tile_lo = sem("tile_hi"), sem("tile_lo")
        scored = sem("scored")
        maxed = sem("maxed")
        exped = sem("exped")
        turned = sem("turned")
        pt_hi, pt_lo = sem("pt_hi"), sem("pt_lo")
        pv_done = sem("pv_done")
        totalled, inverted = sem("totalled"), sem("inverted")
        r_out = [sem(f"r_out{i}") for i in range(2)]
        r_in = [sem(f"r_in{i}") for i in range(2)]
        o_copied = sem("o_copied")
        o_summed = sem("o_summed")
        o_scaled = sem("o_scaled")
        o_stored = [sem(f"o_stored{i}") for i in range(2)]
        mask_loaded = [sem(f"mask_loaded{i}") for i in range(NT)]
        mask_made = sem("mask_made")
        block = ctx.enter_context(nc.Block())

        QK = 4 * BLOCKS

        def chunk_hi(act, it, c, pieces):
            for n in pieces:
                if n == 0:
                    act.wait_ge(raw_loaded[RAW_SLOT[c]], loads_of(it, c))
                    if c >= 2:
                        act.wait_ge(tile_done, 4 + it * TILES + tiles_to(c - 1))
                    if c == 1:
                        act.wait_ge(turned, TBANKS + it * G)
                act.activation(xs[:, c % 2, 0, n], raws[RAW_SLOT[c]][:, n, :], ACT.Copy).then_inc(x_hi, 1)

        def chunk_lo(dve, it, c, pieces):
            for n in pieces:
                dve.wait_ge(x_hi, (it * CHUNKS + c) * KT + n + 1)
                last = dve.tensor_tensor(xs[:, c % 2, 1, n], raws[RAW_SLOT[c]][:, n, :],
                                         f32(xs[:, c % 2, 0, n]), ALU.subtract)
                if n == KT - 1:
                    last.then_inc(x_lo, 1)

        def tiles_of(c):
            return [(tiles_to(c) + n, ps[:, TB + (tiles_to(c) + n) % 4, :], n)
                    for n in range(4 if ORDER[c][0] else 2)]

        def split_hi(act, it, c):
            for tile, bank, n in tiles_of(c):
                act.wait_ge(tile_done, 4 + it * TILES + tile + 1)
                of_context, col = ORDER[c][0], ORDER[c][1] * CH
                if not of_context:
                    for a in range(2):
                        for twice in range(2):
                            last = act.activation(qhi[twice * HD:(twice + 1) * HD, 2 * n + a, col:col + CH],
                                                  bank[a * HD:(a + 1) * HD, :], ACT.Copy)
                elif n < 2:
                    for a in range(2):
                        last = act.activation(ks[0:HD, 2 * n + a, col:col + CH],
                                              bank[a * HD:(a + 1) * HD, :], ACT.Copy)
                else:
                    t = col // P + 2 * (n - 2)
                    last = act.activation(vs[:, t:t + 2, :, 0:HD],
                                          bank.rearrange("p (t h d) -> p t h d", t=2, h=HALF), ACT.Copy)
                last.then_inc(tile_hi, 1)

        def split_lo(dve, it, c, first=0, end=4):
            for tile, bank, n in tiles_of(c)[first:end]:
                dve.wait_ge(tile_hi, 4 + it * TILES + tile + 1)
                of_context, col = ORDER[c][0], ORDER[c][1] * CH
                cols = slice(col, col + CH)
                if not of_context:
                    for a in range(2):
                        for twice in range(2):
                            last = dve.tensor_tensor(qlo[twice * HD:(twice + 1) * HD, 2 * n + a, cols],
                                                     bank[a * HD:(a + 1) * HD, :],
                                                     f32(qhi[0:HD, 2 * n + a, cols]), ALU.subtract)
                elif n < 2:
                    for a in range(2):
                        last = dve.tensor_tensor(ks[HD:P, 2 * n + a, cols], bank[a * HD:(a + 1) * HD, :],
                                                 f32(ks[0:HD, 2 * n + a, cols]), ALU.subtract)
                else:
                    t = col // P + 2 * (n - 2)
                    last = dve.tensor_tensor(vs[:, t:t + 2, :, HD:P],
                                             bank.rearrange("p (t h d) -> p t h d", t=2, h=HALF),
                                             f32(vs[:, t:t + 2, :, 0:HD]), ALU.subtract)
                last.then_inc(tile_lo, 1)

        @block.sync
        def _(sp):
            def load_chunk(b, it, c):
                if c in (2, 3):
                    wait_alone(sp, passed, pv_done, RING + it * G)
                else:
                    before = {0: -1, 1: 1, 4: 2, 5: 3}[c]
                    wait_alone(sp, passed, x_lo, 1 + it * CHUNKS + before)
                of_context, n = ORDER[c]
                if of_context:
                    src = ctxT[bass.ds(b, 1), :, n * CH:(n + 1) * CH].rearrange("a (k p) m -> p (a k) m", p=P)
                else:
                    src = rows_by_tile(xnT[:, bass.ds(b * N + n * CH, CH)], KT)
                sp.dma_start(raws[RAW_SLOT[c]][:, :, :], src).then_inc(raw_loaded[RAW_SLOT[c]], 16)

            def load_mask(b, it, nb, nt):
                wait_alone(sp, passed, mask_made, it * NT * 4 + (nb - 1) * NT + nt + 1 + NT)
                row = nb * NB + nt * P
                sp.dma_start(mask_in[:, nt, :], mask[bass.ds(b, 1), row:row + P, :].rearrange(
                    "a p m -> p (a m)")).then_inc(mask_loaded[nt], 16)

            def load_weights(half):
                for weights, part in ((whi, 0), (wlo, 1)):
                    sp.dma_start(f32(weights[:, :, :, :].rearrange("p k a n -> p (k a n)")),
                                 w_split[bass.ds(half, 1), part].rearrange("a p n -> p (a n)")
                                 ).then_inc(w_loaded, 16)

            sp.wait_ge(x_lo, 2)
            sp.dma_start(raw_0[:, :, :], rows_by_tile(ctxT[0, :, CH:2 * CH], KT)).then_inc(raw_loaded[0], 16)
            with sp.Fori(0, B) as b:
                with sp.Fori(0, HALVES) as half:
                    it = b * HALVES + half
                    next_b = (b + half) & (B - 1)
                    for nt in range(NT):
                        load_mask(b, it, 0, nt)
                    for c in range(2, CHUNKS):
                        load_chunk(b, it, c)
                    for j in range(BLOCKS):
                        if j // HALF < 3 and j % HALF < NT:
                            load_mask(b, it, j // HALF + 1, j % HALF)
                        if j == 2:
                            load_chunk(next_b, it + 1, 0)
                            wait_alone(sp, passed, tile_done, 4 + it * TILES + TILES)
                            load_weights(1 - half)
                        sp.wait_ge(inverted, it * BLOCKS + j + 1)
                        sp.dma_start(r_row[j % 2].rearrange("(p t) -> p t", p=P),
                                     recip[:, j % 2, :]).then_inc(r_out[j % 2], 16)
                        if j == BLOCKS - 1:
                            load_chunk(next_b, it + 1, 1)
                        sp.wait_ge(r_out[j % 2], 16 + it * 8 * 16 + j // 2 * 16 + 16)
                        sp.wait_ge(o_scaled, it * BLOCKS + j + 1)
                        sp.dma_start(r_all[:, j % 2, :], r_row[j % 2:j % 2 + 1, :].partition_broadcast(HD)
                                     ).then_inc(r_in[j % 2], 16)
            sp.wait_ge(w_loaded, (B * HALVES + 1) * 32)
            sp.wait_ge(raw_loaded[0], loads_of(B * HALVES, 1))

        @block.gpsimd
        def _(pool):
            free_from_the_start(pool, (x_lo, 1), (tile_done, 4), (tile_hi, 4), (tile_lo, 4), (maxed, 2),
                                (turned, TBANKS), (pt_hi, TBANKS), (pt_lo, TBANKS), (pv_done, RING), (o_copied, 1),
                                (o_scaled, 2), (mask_made, NT), (r_out[0], 16), (r_out[1], 16), (w_loaded, 32),
                                (raw_loaded[0], 16))
            pool.sem_inc(const_ready, 1)

            def make_mask(it, nb, nt):
                pool.wait_ge(mask_loaded[nt], it * 4 * 16 + nb * 16 + 16)
                wait_alone(pool, passed, maxed, 2 + it * QK + max(nb - 1, 0) * HALF * 4)
                pool.tensor_scalar(mask_add[:, nb % 2 * NT + nt, :], mask_in[:, nt, :], -1.0, BIG,
                                   ALU.add, ALU.mult).then_inc(mask_made, 1)

            with pool.Fori(0, B) as b:
                with pool.Fori(0, HALVES) as half:
                    it = b * HALVES + half
                    for nt in range(NT):
                        make_mask(it, 0, nt)
                    for j in range(BLOCKS):
                        nb, h, s = j // HALF, j % HALF, j % 2
                        if nb < 3 and h < NT:
                            make_mask(it, nb + 1, h)
                        pool.wait_ge(o_copied, 1 + it * BLOCKS + j + 1)
                        pool.tensor_tensor(o_sum[:, s, :], o_both[:, s, 0, :], o_both[:, s, 1, :],
                                           ALU.add).then_inc(o_summed, 1)
                        pool.wait_ge(r_in[s], it * 8 * 16 + j // 2 * 16 + 16)
                        if j >= 2:
                            pool.wait_ge(o_stored[s], it * 8 * 16 + j // 2 * 16)
                        pool.wait_ge(o_summed, it * BLOCKS + j + 1)
                        pool.tensor_tensor(o_out[:, s, :].rearrange("d (t p) -> d t p", t=NT),
                                           o_sum[:, s, :].rearrange("d (t p) -> d t p", t=NT),
                                           r_all[:, s, :].rearrange("d (p t) -> d t p", t=NT),
                                           ALU.mult).then_inc(o_scaled, 1)
                        wait_alone(pool, passed, o_scaled, 2 + it * BLOCKS + j + 1)
                        pool.dma_start(attT[bass.ds(half * HC + h * HD, HD), bass.ds(b * N + nb * NB, NB)],
                                       o_out[:, s, :]).then_inc(o_stored[s], 16)
                    for s in range(2):
                        pool.wait_ge(o_stored[s], it * 8 * 16 + 8 * 16)

        @block.scalar
        def _(act):
            act.wait_ge(const_ready, 1)

            def exp(it, j, e):
                if not 0 <= j < BLOCKS:
                    return
                nt, c = e // 2, e % 2
                s = j % 2 * NT + nt
                if c == 0:
                    act.wait_ge(maxed, 2 + it * QK + 4 * j + 2 * nt + 2)
                piece = probs[:, s, c * 1024:(c + 1) * 1024]
                act.activation(piece, piece, ACT.Exp, bias=lowest[:, s, 1:2], scale=-1.0,
                               accum_out=sums[:, s, c:c + 1]).then_inc(exped, 1)

            def turned_hi(it, j, d):
                if not 0 <= j < BLOCKS:
                    return
                g = j * STEPS + d
                act.wait_ge(turned, TBANKS + it * G + g + 1)
                act.wait_ge(pv_done, it * G + g + 1)
                act.activation(pthi[:, g % RING, :], ps[:, TB + g % TBANKS, :], ACT.Copy).then_inc(pt_hi, 1)

            def copy_out(it, j):
                if not 0 <= j < BLOCKS:
                    return
                act.wait_ge(pv_done, RING + it * G + STEPS * (j + 1))
                act.wait_ge(o_scaled, it * BLOCKS + j + 1)
                for part in range(2):
                    last = act.activation(o_both[:, j % 2, part, :],
                                          ps[part * HD:(part + 1) * HD, OB, 0:NB], ACT.Copy)
                last.then_inc(o_copied, 1)

            chunk_hi(act, 0, 0, range(KT))
            with act.Fori(0, B) as b:
                with act.Fori(0, HALVES) as half:
                    it = b * HALVES + half
                    for c in range(CHUNKS):
                        if c + 1 < CHUNKS:
                            chunk_hi(act, it, c + 1, range(KT))
                        split_hi(act, it, c)
                    for j in range(-1, BLOCKS + 1):
                        turned_hi(it, j, 1)
                        turned_hi(it, j, 2)
                        exp(it, j + 1, 0)
                        copy_out(it, j - 1)
                        turned_hi(it, j, 3)
                        exp(it, j + 1, 1)
                        if j == BLOCKS - 1:
                            act.wait_ge(turned, TBANKS + it * G + (BLOCKS - 1) * STEPS)
                        for d in (4, 5, 6):
                            turned_hi(it, j, d)
                            if j == BLOCKS - 1:
                                chunk_hi(act, it + 1, 0, {4: (0,), 5: (1,), 6: (2, 3)}[d])
                        exp(it, j + 1, 2)
                        turned_hi(it, j, 7)
                        exp(it, j + 1, 3)
                        turned_hi(it, j + 1, 0)

        @block.vector
        def _(dve):
            def mask_and_max(it, j, k):
                if not 0 <= j < BLOCKS:
                    return
                nb, h, nt, c = j // HALF, j % HALF, k // 2, k % 2
                s = j % 2 * NT + nt
                if h == 0 and c == 0:
                    dve.wait_ge(mask_made, NT + it * NT * 4 + nb * NT + nt + 1)
                if c == 1:
                    dve.wait_ge(maxed, 2 + it * QK + 4 * j + k)
                wait_alone(dve, passed, scored, it * QK + 4 * j + k + 1)
                dve.tensor_tensor_reduce(
                    out=probs[:, s, c * 1024:(c + 1) * 1024],
                    in0=ps[:, SB + 2 * (k % 2):SB + 2 * (k % 2) + 2, :].rearrange("p a n -> p (a n)"),
                    in1=mask_add[:, nb % 2 * NT + nt, c * 1024:(c + 1) * 1024], scale=-SCALE,
                    scalar=BIG if c == 0 else lowest[:, s, 0:1], op0=ALU.add, op1=ALU.min,
                    accum_out=lowest[:, s, c:c + 1]).then_inc(maxed, 1)

            def turned_lo(it, j, d):
                if not 0 <= j < BLOCKS:
                    return
                g = j * STEPS + d
                dve.wait_ge(pt_hi, TBANKS + it * G + g + 1)
                dve.tensor_tensor(ptlo[:, g % RING, :], ps[:, TB + g % TBANKS, :],
                                  f32(pthi[:, g % RING, :]), ALU.subtract).then_inc(pt_lo, 1)

            def invert(it, j):
                if not 0 <= j < BLOCKS:
                    return
                s = j % 2 * NT
                dve.wait_ge(exped, it * QK + 4 * j + 4)
                dve.tensor_tensor(total[:, :], sums[:, s:s + NT, 0], sums[:, s:s + NT, 1],
                                  ALU.add).then_inc(totalled, 1)
                dve.wait_ge(totalled, it * BLOCKS + j + 1)
                dve.wait_ge(r_out[j % 2], 16 + it * 8 * 16 + j // 2 * 16)
                dve.reciprocal(recip[:, j % 2, :], total[:, :]).then_inc(inverted, 1)

            chunk_lo(dve, 0, 0, range(KT))
            with dve.Fori(0, B) as b:
                with dve.Fori(0, HALVES) as half:
                    it = b * HALVES + half
                    for c in range(CHUNKS - 1):
                        chunk_lo(dve, it, c + 1, range(KT))
                        split_lo(dve, it, c)
                    split_lo(dve, it, CHUNKS - 1, 0, 3)
                    mask_and_max(it, 0, 0)
                    mask_and_max(it, 0, 1)
                    split_lo(dve, it, CHUNKS - 1, 3, 4)
                    for j in range(-1, BLOCKS):
                        turned_lo(it, j, 1)
                        turned_lo(it, j, 2)
                        mask_and_max(it, j + 1, 2)
                        turned_lo(it, j, 3)
                        mask_and_max(it, j + 1, 3)
                        invert(it, j)
                        for d in (4, 5, 6, 7):
                            turned_lo(it, j, d)
                            if j == BLOCKS - 1:
                                chunk_lo(dve, it + 1, 0, (d - 4,))
                        mask_and_max(it, j + 2, 0)
                        mask_and_max(it, j + 2, 1)
                        turned_lo(it, j + 1, 0)

        @block.tensor
        def _(pe):
            def project(it, c, first=0, end=4):
                s = c % 2
                parts = ((whi, 0), (wlo, 0), (whi, 1))
                pe.wait_ge(x_lo, 1 + it * CHUNKS + c + 1)
                for tile, bank, n in tiles_of(c)[first:end]:
                    if tile == 3:
                        pe.wait_ge(o_copied, 1 + it * BLOCKS)
                    pe.wait_ge(tile_lo, it * TILES + tile + 1)
                    if n < 2:
                        a = 1 if ORDER[c][0] else 0
                        last = products(pe, bank, [(w[:, k, a, n * P:(n + 1) * P], xs[:, s, x, k, :])
                                                   for w, x in parts for k in range(KT)])
                    else:
                        for t in range(2):
                            col = (2 * (n - 2) + t) * P
                            last = products(pe, bank[:, t * HC:(t + 1) * HC],
                                            [(xs[:, s, x, k, col:col + P], w[:, k, 2, :])
                                             for w, x in parts for k in range(KT)])
                    last.then_inc(tile_done, 1)

            def score(it, j, k):
                if not 0 <= j < BLOCKS:
                    return
                nb, h, nt, c = j // HALF, j % HALF, k // 2, k % 2
                pe.wait_ge(maxed, it * QK + 4 * j + k + 1)
                row = nb * NB + nt * P
                for q in (qhi, qlo):
                    for m in range(2):
                        col = (2 * c + m) * CH
                        last = pe.matmul(ps[:, SB + 2 * (k % 2) + m, :], q[:, h, row:row + P],
                                         ks[:, h, col:col + CH], start=q is qhi, stop=q is qlo,
                                         skip_group_check=True)
                last.then_inc(scored, 1)

            def turn(it, j, d):
                if not 0 <= j < BLOCKS:
                    return
                g = j * STEPS + d
                if d == 0:
                    pe.wait_ge(exped, it * QK + 4 * j + 3)
                if d == STEPS // 2:
                    pe.wait_ge(exped, it * QK + 4 * j + 4)
                pe.wait_ge(pt_lo, it * G + g + 1)
                for m in range(2):
                    for nt in range(NT):
                        col = (2 * d + m) * P
                        last = pe.transpose(ps[:, TB + g % TBANKS, m * NB + nt * P:m * NB + (nt + 1) * P],
                                            probs[:, j % 2 * NT + nt, col:col + P], ident[:, :])
                last.then_inc(turned, 1)

            def weigh(it, j, d):
                if not 0 <= j < BLOCKS:
                    return
                v = j * STEPS + d
                pe.wait_ge(pt_lo, TBANKS + it * G + v + 1)
                if d == 0:
                    pe.wait_ge(o_copied, it * BLOCKS + j + 1)
                for m in range(2):
                    for pt in (pthi, ptlo):
                        last = pe.matmul(ps[:, OB, 0:NB], vs[:, 2 * d + m, j % HALF, :],
                                         pt[:, v % RING, m * NB:(m + 1) * NB],
                                         start=(d == 0 and m == 0 and pt is pthi),
                                         stop=(d == STEPS - 1 and m == 1 and pt is ptlo),
                                         skip_group_check=True)
                last.then_inc(pv_done, 1)

            with pe.Fori(0, B) as b:
                with pe.Fori(0, HALVES) as half:
                    it = b * HALVES + half
                    pe.wait_ge(w_loaded, it * 32 + 32)
                    pe.wait_ge(pt_lo, TBANKS + it * G)
                    for c in range(CHUNKS - 1):
                        project(it, c)
                    project(it, CHUNKS - 1, 0, 3)
                    pe.wait_ge(tile_lo, 4 + it * TILES + TILES - 2)
                    score(it, 0, 0)
                    score(it, 0, 1)
                    project(it, CHUNKS - 1, 3, 4)
                    for j in range(-1, BLOCKS + 1):
                        if j == 0:
                            pe.wait_ge(tile_lo, 4 + it * TILES + TILES)
                        for d in (0, 1, 2):
                            turn(it, j, d)
                            weigh(it, j - 1, d + 5)
                        score(it, j + 1, 2)
                        score(it, j + 1, 3)
                        turn(it, j, 3)
                        turn(it, j, 4)
                        weigh(it, j, 0)
                        weigh(it, j, 1)
                        turn(it, j, 5)
                        weigh(it, j, 2)
                        turn(it, j, 6)
                        weigh(it, j, 3)
                        score(it, j + 2, 0)
                        turn(it, j, 7)
                        score(it, j + 2, 1)
                        weigh(it, j, 4)


LCHUNKS = TOK // CH
TILE = CH // P
ML = FL // P
MID = KT + ML


def light(nc, x, attT, wo, rt, gamma, w1, b1, w2, b2, z_rows, out, scores, consts):
    ident, eps = consts["ident"], consts["eps"]
    with ExitStack() as ctx:
        sb = lambda name, shape, dt=F32: ctx.enter_context(nc.sbuf_tensor("c_" + name, shape, dt))
        sem = lambda name: ctx.enter_context(nc.semaphore("c_" + name))
        wo_raw, wo_hi, wo_lo = (sb("wo" + n, [P, KT, D], dt) for n, dt in (("", F32), ("hi", F32R), ("lo", F32R)))
        w1_raw, w1_hi, w1_lo = (sb("w1" + n, [P, KT, FL], dt) for n, dt in (("", F32), ("hi", F32R), ("lo", F32R)))
        w2_raw, w2_hi, w2_lo = (sb("w2" + n, [P, ML, D], dt) for n, dt in (("", F32), ("hi", F32R), ("lo", F32R)))
        rt_all = sb("rt", [P, D])
        b2_all = sb("b2", [P, D])
        gamma_col = sb("gamma", [P, KT])
        b1_col = sb("b1", [P, ML])
        o_raw = sb("o_raw", [P, 2, KT, CH])
        o_hi, o_lo = sb("o_hi", [P, 2, KT, CH], F32R), sb("o_lo", [P, 2, KT, CH], F32R)
        x_in = sb("x_in", [P, 2, TILE, D])
        x1 = sb("x1", [P, 2, TILE, D])
        stats, mv = sb("stats", [P, TILE, 6]), sb("mv", [P, TILE, 2])
        sd, rstd = sb("sd", [P, TILE]), sb("rstd", [P, TILE])
        sq, nrm, nrm_min, rn = (sb(n, [P, TILE]) for n in ("sq", "nrm", "nrm_min", "rn"))
        s4 = sb("s4", [P, TILE])
        junk = sb("junk", [P, D])
        xn = sb("xn", [P, TILE, D])
        z = sb("z", [P, 2, TILE, D])
        z_hi, z_lo = sb("z_hi", [P, KT, CH], F32R), sb("z_lo", [P, KT, CH], F32R)
        g = sb("g", [P, ML, CH])
        g_hi, g_lo = sb("g_hi", [P, ML, CH], F32R), sb("g_lo", [P, ML, CH], F32R)
        y = sb("y", [P, TILE, D])
        ps = ctx.enter_context(nc.psum_tensor("c_ps", [P, 8, CH], F32))
        XB, MB, YB = 0, 4, 6

        passed = sem("passed")
        w_loaded = [sem(f"w_loaded{n}") for n in range(3)]
        small_loaded, w_hi, w_lo = sem("small_loaded"), sem("w_hi"), sem("w_lo")
        o_loaded = [sem(f"o_loaded{u}") for u in range(2)]
        x_loaded = [sem(f"x_loaded{u}") for u in range(2)]
        o_is_hi, o_is_lo = sem("o_is_hi"), sem("o_is_lo")
        projected = sem("projected")
        x1_done, stats_done, mv_done, sd_done, rstd_done, xn_done = (
            sem(n) for n in ("x1_done", "stats_done", "mv_done", "sd_done", "rstd_done", "xn_done"))
        sq_done, junked, nrm_done, min_done, rn_done, z_done = (
            sem(n) for n in ("sq_done", "junked", "nrm_done", "min_done", "rn_done", "z_done"))
        z_stored = [sem(f"z_stored{u}") for u in range(2)]
        mid_done = sem("mid_done")
        z_is_hi, z_is_lo = sem("z_is_hi"), sem("z_is_lo")
        g_done, g_is_hi, g_is_lo = sem("g_done"), sem("g_is_hi"), sem("g_is_lo")
        b2_added = sem("b2_added")
        y_done, out_done = sem("y_done"), sem("out_done")
        out_stored = sem("out_stored")
        block = ctx.enter_context(nc.Block())
        x_rows = x.rearrange("b n d -> (b n) d")
        out_rows = out.rearrange("b n d -> (b n) d")
        weights = ((wo_raw, wo_hi, wo_lo), (w1_raw, w1_hi, w1_lo), (w2_raw, w2_hi, w2_lo))

        def exists(i, k):
            return not isinstance(i, int) or 0 <= k < LCHUNKS

        def run(eng, step, after_first=None):
            for k in (-3, -2, -1):
                step(0, k)
                if k == -3 and after_first:
                    after_first()
            with eng.Fori(0, LCHUNKS // 2 - 1) as i:
                for k in range(2):
                    step(i, k)
            for k in (LCHUNKS - 2, LCHUNKS - 1):
                step(0, k)

        def by_rows(ap, i, k):
            return ap[bass.ds((i * 2 + k) * CH, CH), :].rearrange("(t p) d -> p t d", p=P)

        @block.gpsimd
        def _(pool):
            free_from_the_start(pool, (projected, 2 * TILE), (x1_done, TILE), (mid_done, MID), (z_is_lo, KT),
                                (g_done, ML), (g_is_lo, ML), (y_done, TILE), (out_done, 2),
                                (z_stored[0], 16), (z_stored[1], 16), (out_stored, 16), (o_is_lo, 2))
            pool.wait_ge(small_loaded, 16 * 4)

            def step(i, k):
                if exists(i, k + 1):
                    wait_alone(pool, passed, xn_done, i * 2 + k + 2)
                    x1_rows = x1[:, (k + 1) % 2]
                    pool.tensor_tensor(x1_rows, x1_rows, b2_all[:, :].unsqueeze(1).broadcast_to([P, TILE, D]),
                                       ALU.add).then_inc(b2_added, 1)

            run(pool, step)

        @block.sync
        def _(sp):
            def load_o(i, k):
                c, u = i * 2 + k, k % 2
                wait_alone(sp, passed, o_is_lo, c + 1)
                sp.dma_start(o_raw[:, u], rows_by_tile(attT[:, bass.ds((c & (LCHUNKS - 1)) * CH, CH)], KT)
                             ).then_inc(o_loaded[u], 16)

            def load_x(i, k):
                c, u = i * 2 + k, k % 2
                if k >= 2:
                    wait_alone(sp, passed, x1_done, TILE + (c - 1) * TILE)
                sp.dma_start(x_in[:, u], by_rows(x_rows, i, k)).then_inc(x_loaded[u], 16)

            def store_z(i, k):
                c, u = i * 2 + k, k % 2
                wait_alone(sp, passed, z_done, c + 1)
                sp.dma_start(by_rows(z_rows, i, k), z[:, u]).then_inc(z_stored[u], 16)

            def store_out(i, k):
                c = i * 2 + k
                wait_alone(sp, passed, out_done, 2 + (c + 1) * TILE)
                sp.dma_start(by_rows(out_rows, i, k), y[:, :, :]).then_inc(out_stored, 16)

            def step(i, k):
                if exists(i, k + 4):
                    load_o(i, k + 4)
                if exists(i, k + 2) and k > -2:
                    load_x(i, k + 2)
                if exists(i, k + 1):
                    store_z(i, k + 1)
                if exists(i, k):
                    store_out(i, k)

            for n, (raw, w, kt) in enumerate(((wo_raw, wo, KT), (w1_raw, w1, KT), (w2_raw, w2, ML))):
                sp.dma_start(raw[:, :, :], rows_by_tile(w, kt)).then_inc(w_loaded[n], 16)
                if n == 0:
                    load_o(0, 0)
                    load_x(0, 0)
            for all_, row in ((rt_all, rt), (b2_all, b2)):
                sp.dma_start(all_[:, :], row.rearrange("(a d) -> a d", a=1).partition_broadcast(P)
                             ).then_inc(small_loaded, 16)
            sp.dma_start(gamma_col[:, :], gamma).then_inc(small_loaded, 16)
            sp.dma_start(b1_col[:, :], b1).then_inc(small_loaded, 16)
            run(sp, step)
            for u in range(2):
                sp.wait_ge(o_loaded[u], (LCHUNKS // 2 + 1) * 16)
                sp.wait_ge(z_stored[u], 16 + 16 * LCHUNKS // 2)
            sp.wait_ge(out_stored, 16 + 16 * LCHUNKS)

        @block.scalar
        def _(act):
            def weights_hi(which):
                for n in which:
                    raw, hi, lo = weights[n]
                    act.wait_ge(w_loaded[n], 16)
                    act.activation(hi[:, :, :], raw[:, :, :], ACT.Copy).then_inc(w_hi, 1)

            def rest():
                weights_hi((1, 2))
                act.wait_ge(small_loaded, 16 * 4)

            def split_hi(i, k):
                if exists(i, k):
                    c, u = i * 2 + k, k % 2
                    act.wait_ge(o_loaded[u], (i + k // 2 + 1) * 16)
                    act.wait_ge(projected, TILE + c * TILE)
                    act.activation(o_hi[:, u], o_raw[:, u], ACT.Copy).then_inc(o_is_hi, 1)

            def deviation(i, k):
                if exists(i, k):
                    act.wait_ge(mv_done, i * 2 + k + 1)
                    act.activation(sd[:, :], mv[:, :, 1], ACT.Sqrt, bias=eps[:, :]).then_inc(sd_done, 1)

            def squares(i, k, tiles):
                if exists(i, k):
                    c, u = i * 2 + k, k % 2
                    if tiles[0] == 0:
                        act.wait_ge(xn_done, c + 1)
                        act.wait_ge(z_stored[u], (i + k // 2 + 1) * 16)
                    for t in tiles:
                        act.activation(z[:, u, t, :], xn[:, t, :], ACT.Square,
                                       accum_out=sq[:, t:t + 1]).then_inc(sq_done, 1)

            def norms(i, k):
                if exists(i, k):
                    act.wait_ge(sq_done, (i * 2 + k + 1) * TILE)
                    act.activation(nrm[:, :], sq[:, :], ACT.Sqrt).then_inc(nrm_done, 1)

            def scale_z(i, k):
                if exists(i, k):
                    act.wait_ge(rn_done, i * 2 + k + 1)
                    for t in range(TILE):
                        last = act.activation(z[:, k % 2, t, :], xn[:, t, :], ACT.Copy, scale=rn[:, t:t + 1])
                    last.then_inc(z_done, 1)

            def turned_hi(i, k):
                if exists(i, k):
                    c = i * 2 + k
                    for n in range(KT):
                        act.wait_ge(mid_done, MID + c * MID + n + 1)
                        act.activation(z_hi[:, n, :], ps[:, MB + n % 2, :], ACT.Copy,
                                       scale=gamma_col[:, n:n + 1]).then_inc(z_is_hi, 1)

            def hidden(i, k, m):
                if exists(i, k):
                    c = i * 2 + k
                    act.wait_ge(mid_done, MID + c * MID + KT + m + 1)
                    act.wait_ge(g_is_lo, c * ML + ML)
                    act.activation(g[:, m, :], ps[:, MB + m % 2, :], ACT.Gelu,
                                   bias=b1_col[:, m:m + 1]).then_inc(g_done, 1)
                    act.wait_ge(y_done, TILE + c * TILE)
                    act.wait_ge(g_done, ML + c * ML + m + 1)
                    act.activation(g_hi[:, m, :], g[:, m, :], ACT.Copy).then_inc(g_is_hi, 1)

            def step(i, k):
                turned_hi(i, k)
                split_hi(i, k + 3)
                deviation(i, k + 1)
                for m in range(ML):
                    hidden(i, k, m)
                    squares(i, k + 1, range(TILE * m // ML, TILE * (m + 1) // ML))
                norms(i, k + 1)
                scale_z(i, k + 1)

            weights_hi((0,))
            run(act, step, rest)

        @block.vector
        def _(dve):
            def weights_lo(which):
                for n in which:
                    raw, hi, lo = weights[n]
                    dve.wait_ge(w_hi, n + 1)
                    dve.tensor_tensor(lo[:, :, :], raw[:, :, :], f32(hi[:, :, :]), ALU.subtract).then_inc(w_lo, 1)

            def rest():
                weights_lo((1, 2))
                dve.wait_ge(small_loaded, 16 * 4)

            dve.memset(junk[:, :], 0.0).then_inc(junked, 1)

            def add_x(i, k, tiles):
                if exists(i, k):
                    c, u = i * 2 + k, k % 2
                    if tiles[0] == 0:
                        dve.wait_ge(x_loaded[u], (i + k // 2 + 1) * 16)
                    if tiles[0] == 0 and k >= 1:
                        dve.wait_ge(out_done, 2 + (c - 1) * TILE)
                    for t in tiles:
                        dve.wait_ge(projected, 2 * TILE + c * TILE + t + 1)
                        dve.tensor_tensor(x1[:, u, t, :], ps[:, XB + t, :], x_in[:, u, t, :],
                                          ALU.add).then_inc(x1_done, 1)

            def turned_lo(i, k, tiles):
                if exists(i, k):
                    c = i * 2 + k
                    for n in tiles:
                        dve.wait_ge(z_is_hi, c * KT + n + 1)
                        dve.scalar_tensor_tensor(out=z_lo[:, n, :], in0=ps[:, MB + n % 2, :],
                                                 scalar=gamma_col[:, n:n + 1], in1=f32(z_hi[:, n, :]),
                                                 op0=ALU.mult, op1=ALU.subtract).then_inc(z_is_lo, 1)

            def statistics(i, k):
                if exists(i, k):
                    c, u = i * 2 + k, k % 2
                    wait_alone(dve, passed, x1_done, TILE + c * TILE + TILE)
                    for t in range(TILE):
                        last = dve.bn_stats(out=stats[:, t, :], in_=x1[:, u, t, :])
                    last.then_inc(stats_done, 1)
                    wait_alone(dve, passed, stats_done, c + 1)
                    for t in range(TILE):
                        last = dve.bn_aggr(out=mv[:, t, :], in_=stats[:, t, :])
                    last.then_inc(mv_done, 1)

            def normalize(i, k):
                if exists(i, k):
                    c, u = i * 2 + k, k % 2
                    dve.wait_ge(sd_done, c + 1)
                    dve.reciprocal(rstd[:, :], sd[:, :]).then_inc(rstd_done, 1)
                    if k >= 1:
                        dve.wait_ge(z_done, c)
                    dve.wait_ge(rstd_done, c + 1)
                    for t in range(TILE):
                        last = dve.tensor_scalar(xn[:, t, :], x1[:, u, t, :], mv[:, t, 0:1], rstd[:, t:t + 1],
                                                 ALU.subtract, ALU.mult)
                    last.then_inc(xn_done, 1)

            def split_lo(i, k):
                if exists(i, k):
                    c, u = i * 2 + k, k % 2
                    dve.wait_ge(o_is_hi, c + 1)
                    dve.tensor_tensor(o_lo[:, u], o_raw[:, u], f32(o_hi[:, u]), ALU.subtract).then_inc(o_is_lo, 1)

            def hidden_lo(i, k):
                if exists(i, k):
                    c = i * 2 + k
                    for m in range(ML):
                        dve.wait_ge(g_is_hi, c * ML + m + 1)
                        dve.tensor_tensor(g_lo[:, m, :], g[:, m, :], f32(g_hi[:, m, :]),
                                          ALU.subtract).then_inc(g_is_lo, 1)

            def route_scores(i, k):
                if exists(i, k):
                    c = i * 2 + k
                    wait_alone(dve, passed, xn_done, c + 1)
                    for t in range(TILE):
                        wait_alone(dve, passed, junked, 1 + c * TILE + t)
                        dve.tensor_tensor_reduce(out=junk[:, :], in0=xn[:, t, :], in1=rt_all[:, :], scale=1.0,
                                                 scalar=0.0, op0=ALU.mult, op1=ALU.add,
                                                 accum_out=s4[:, t:t + 1]).then_inc(junked, 1)
                    dve.wait_ge(junked, 1 + (c + 1) * TILE)
                    dve.tensor_copy(scores[:, bass.ds(c * TILE, TILE)], s4[:, :])

            def inverse_norms(i, k):
                if exists(i, k):
                    c = i * 2 + k
                    dve.wait_ge(nrm_done, c + 1)
                    dve.tensor_scalar(nrm_min[:, :], nrm[:, :], 1e-12, float(D) ** -0.5,
                                      ALU.max, ALU.mult).then_inc(min_done, 1)
                    dve.wait_ge(min_done, c + 1)
                    dve.reciprocal(rn[:, :], nrm_min[:, :]).then_inc(rn_done, 1)

            def add_y(i, k):
                if exists(i, k):
                    c, u = i * 2 + k, k % 2
                    dve.wait_ge(b2_added, c + 1)
                    dve.wait_ge(out_stored, (c + 1) * 16)
                    for t in range(TILE):
                        dve.wait_ge(y_done, TILE + c * TILE + t + 1)
                        dve.tensor_tensor(y[:, t, :], ps[:, YB + t % 2, :], x1[:, u, t, :],
                                          ALU.add).then_inc(out_done, 1)

            def step(i, k):
                add_x(i, k + 1, (0,))
                turned_lo(i, k, (0, 1))
                add_x(i, k + 1, (1, 2, 3))
                turned_lo(i, k, (2, 3))
                statistics(i, k + 1)
                normalize(i, k + 1)
                split_lo(i, k + 3)
                hidden_lo(i, k)
                route_scores(i, k + 1)
                inverse_norms(i, k + 1)
                add_y(i, k)

            weights_lo((0,))
            run(dve, step, rest)

        @block.tensor
        def _(pe):
            pe.wait_ge(w_lo, 1)

            def project(i, k, tiles):
                if exists(i, k):
                    c, u = i * 2 + k, k % 2
                    if tiles[0] == 0:
                        pe.wait_ge(o_is_lo, 2 + c + 1)
                    for t in tiles:
                        pe.wait_ge(x1_done, c * TILE + t + 1)
                        products(pe, ps[:, XB + t, :],
                                 [(o[:, u, n, t * P:(t + 1) * P], w[:, n, :])
                                  for o, w in ((o_hi, wo_hi), (o_lo, wo_hi), (o_hi, wo_lo))
                                  for n in range(KT)]).then_inc(projected, 1)

            def turn(i, k, tiles):
                if exists(i, k):
                    c, u = i * 2 + k, k % 2
                    if tiles[0] == 0:
                        pe.wait_ge(z_done, c + 1)
                    for n in tiles:
                        if n < 2:
                            pe.wait_ge(g_done, c * ML + n + 1)
                        else:
                            pe.wait_ge(z_is_lo, KT + c * KT + n - 1)
                        for t in range(TILE):
                            last = pe.transpose(ps[:, MB + n % 2, t * P:(t + 1) * P],
                                                z[:, u, t, n * P:(n + 1) * P], ident[:, :])
                        last.then_inc(mid_done, 1)

            def hidden(i, k):
                if exists(i, k):
                    pe.wait_ge(z_is_lo, KT + (i * 2 + k) * KT + KT)
                    for m in range(ML):
                        products(pe, ps[:, MB + m % 2, :],
                                 [(w[:, n, m * P:(m + 1) * P], zz[:, n, :])
                                  for w, zz in ((w1_hi, z_hi), (w1_lo, z_hi), (w1_hi, z_lo))
                                  for n in range(KT)]).then_inc(mid_done, 1)

            def result(i, k):
                if exists(i, k):
                    c = i * 2 + k
                    pe.wait_ge(g_is_lo, ML + c * ML + ML)
                    for t in range(TILE):
                        pe.wait_ge(out_done, c * TILE + t + 1)
                        products(pe, ps[:, YB + t % 2, :],
                                 [(gg[:, m, t * P:(t + 1) * P], w[:, m, :])
                                  for gg, w in ((g_hi, w2_hi), (g_lo, w2_hi), (g_hi, w2_lo))
                                  for m in range(ML)]).then_inc(y_done, 1)

            def step(i, k):
                if k == -1:
                    pe.wait_ge(w_lo, 3)
                turn(i, k, (0, 1))
                project(i, k + 2, (0,))
                turn(i, k, (2, 3))
                project(i, k + 2, (1,))
                hidden(i, k)
                project(i, k + 2, (2, 3))
                result(i, k)

            run(pe, step)


NT_B = N // P


MH = FH // P
RAWS = 4


def weight_pieces(w1, w2, weights):
    w1_hi, w1_lo, w2_hi, w2_lo = weights
    return ([(w1[n * P:(n + 1) * P, :], w1_hi[:, n, :], w1_lo[:, n, :]) for n in range(KT)] +
            [(rows_by_tile(w2[n * CH:(n + 1) * CH, :], 4), w2_hi[:, 4 * n:4 * n + 4, :],
              w2_lo[:, 4 * n:4 * n + 4, :]) for n in range(FH // CH)])


def rank_tiles(dve, ranks, junk, row, b, tiles, counted, done):
    sel, before, counts = ranks["sel"], ranks["before"], ranks["counts"]
    for t in tiles:
        n = b * NT_B + t
        own = slice(t * P, (t + 1) * P)
        mine = sel[:, n:n + 1]
        dve.wait_ge(counted, done)
        if t:
            dve.tensor_scalar(junk[:, 0:t * P], row[:, 0:t * P], mine, None, ALU.is_ge, ALU.add,
                              accum_out=counts[:, 0, n:n + 1]).then_inc(counted, 1)
            done += 1
        dve.tensor_scalar(junk[:, t * P:N], row[:, t * P:N], mine, None, ALU.is_gt, ALU.add,
                          accum_out=counts[:, 1, n:n + 1]).then_inc(counted, 1)
        dve.scalar_tensor_tensor(out=junk[:, N:N + P], in0=row[:, own], scalar=mine,
                                 in1=before[:, :], op0=ALU.is_equal, op1=ALU.mult,
                                 accum_out=counts[:, 2, n:n + 1]).then_inc(counted, 1)
        done += 2
    return done


def place_tokens(dve, ranks, b, counted, done, added, placed):
    counts, rank1, rank, place = (ranks[n] for n in ("counts", "rank1", "rank", "place"))
    own = slice(b * NT_B, (b + 1) * NT_B)
    dve.wait_ge(counted, done)
    dve.tensor_tensor(rank1[:, own], counts[:, 0, own], counts[:, 1, own], ALU.add).then_inc(added, 1)
    first = max(b - 1, 0) * 2
    dve.wait_ge(added, first + 1)
    dve.tensor_tensor(rank[:, own], rank1[:, own], counts[:, 2, own], ALU.add).then_inc(added, 1)
    dve.wait_ge(added, first + 2)
    dve.tensor_scalar(place[:, own], rank[:, own], float(b * N), None, ALU.add).then_inc(placed, 1)


def scatter_tokens(pool, ranks, slots, b, scattered):
    for n in range(b * NT_B, (b + 1) * NT_B):
        pool.indirect_dma_start(out=slots, out_offset=bass.IndirectOffsetOnAxis(ranks["place"][:, n:n + 1], 0),
                                in_=ranks["pay"][:, n, :], in_offset=None).then_inc(scattered, 16)


def route(nc, scores, score_row, slots, w1, w2, weights, ranks):
    cols = B * NT_B
    with ExitStack() as ctx:
        sb = lambda name, shape, dt=F32: ctx.enter_context(nc.sbuf_tensor("d_" + name, shape, dt))
        sem = lambda name: ctx.enter_context(nc.semaphore("d_" + name))
        ones = sb("ones", [P, P])
        before, sel, pay, counts = (ranks[n] for n in ("before", "sel", "pay", "counts"))
        top1, top = sb("top1", [P, B]), sb("top", [P, B])
        neg_a = sb("neg_a", [P, B])
        shift = sb("shift", [P, B])
        zc, zs, e = (sb(n, [P, cols]) for n in ("zc", "zs", "e"))
        part, lg = sb("part", [P, B]), sb("lg", [P, B])
        sa = sb("sa", [P, cols])
        one_minus = sb("one_minus", [P, cols])
        row = sb("row", [P, N])
        junk = sb("junk", [P, N + P])
        raw = sb("raw", [P, RAWS, 4, CH])
        ps = ctx.enter_context(nc.psum_tensor("d_ps", [P, CH], F32))
        by_batch = lambda t: t[:, :].rearrange("p (b t) -> p b t", b=B)
        each = lambda t: t[:, :].unsqueeze(2).broadcast_to([P, B, NT_B])

        passed = sem("passed")
        ones_ready, before_zero, before_ready, ids_ready = (
            sem(n) for n in ("ones_ready", "before_zero", "before_ready", "ids_ready"))
        top_part, top_ready, start_ready = sem("top_part"), sem("top_ready"), sem("start_ready")
        cut, shifted, exped, parted, summed, logged, stepped = (
            sem(n) for n in ("cut", "shifted", "exped", "parted", "summed", "logged", "stepped"))
        sa_done, sa_min, sel_done, minus_done, weight_done = (
            sem(n) for n in ("sa_done", "sa_min", "sel_done", "minus_done", "weight_done"))
        row_out, row_in = sem("row_out"), sem("row_in")
        counted, added, placed = (sem(n) for n in ("counted", "added", "placed"))
        scattered = sem("scattered")
        w_loaded = [sem(f"w_loaded{n}") for n in range(RAWS)]
        w_hi, w_lo = sem("w_hi"), sem("w_lo")
        block = ctx.enter_context(nc.Block())
        pieces = weight_pieces(w1, w2, weights)

        def raw_piece(n):
            place = raw[:, n % RAWS]
            return place.rearrange("p k d -> p (k d)") if n < KT else place

        def split_lo(dve, n):
            src, hi, lo = pieces[n]
            dve.wait_ge(w_hi, n + 1)
            dve.tensor_tensor(lo, raw_piece(n), f32(hi), ALU.subtract).then_inc(w_lo, 1)

        LOOPS, UNROLL = ITERS - 1, 7
        FIRST_NEG_A = float(np.log(np.float32(N)) - np.log(np.float32(EFFECTIVE_K)))

        @block.gpsimd
        def _(pool):
            pool.memset(ones[:, :], 1.0).then_inc(ones_ready, 1)
            pool.memset(before[:, :], 1.0).then_inc(before_zero, 1)
            pool.wait_ge(before_zero, 1)
            pool.affine_select(out=before[:, :], in_=before[:, :], compare_op=ALU.is_gt, fill=0.0, base=0,
                               pattern=[[-1, P]], channel_multiplier=1).then_inc(before_ready, 1)
            pool.iota(pay[:, :, 0].bitcast(I32), pattern=[[P, cols]], base=0,
                      channel_multiplier=1).then_inc(ids_ready, 1)
            pool.wait_ge(top_part, 1)
            pool.partition_all_reduce(top[:, :], top1[:, :], P, bass.bass_isa.ReduceOp.max).then_inc(top_ready, 1)
            pool.wait_ge(weight_done, 1)
            pool.wait_ge(ids_ready, 1)
            pool.wait_ge(placed, 1)
            scatter_tokens(pool, ranks, slots, 0, scattered)
            pool.wait_ge(scattered, 16 * NT_B)

        @block.scalar
        def _(act):
            nc.scalar.preload_act_table_set("natural_log_exp_and_others")
            with act.Fori(0, LOOPS // UNROLL) as loop:
                for u in range(UNROLL):
                    i = loop * UNROLL + u
                    act.wait_ge(shifted, i + 1)
                    act.activation(e[:, :], zs[:, :], ACT.Exp).then_inc(exped, 1)
                    act.wait_ge(summed, i + 1)
                    act.activation(lg[:, :], ps[:, 0:B], ACT.Ln, scale=1.0 / EFFECTIVE_K).then_inc(logged, 1)
            act.wait_ge(sa_min, 1)
            act.activation(sel[:, :], sa[:, :], ACT.Exp).then_inc(sel_done, 1)
            for n, (src, hi, lo) in enumerate(pieces):
                act.wait_ge(w_loaded[n % RAWS], 16 * (n // RAWS + 1))
                act.activation(hi, raw_piece(n), ACT.Copy).then_inc(w_hi, 1)

        @block.tensor
        def _(pe):
            pe.wait_ge(ones_ready, 1)
            with pe.Fori(0, LOOPS // UNROLL) as loop:
                for u in range(UNROLL):
                    pe.wait_ge(parted, loop * UNROLL + u + 1)
                    pe.matmul(ps[:, 0:B], ones[:, :], part[:, :], start=True, stop=True).then_inc(summed, 1)

        @block.sync
        def _(sp):
            for n in range(RAWS):
                sp.dma_start(raw_piece(n), pieces[n][0]).then_inc(w_loaded[n], 16)
            sp.wait_ge(sel_done, 1)
            with nc.allow_non_contiguous_dma(reason="a column of scores to a row"):
                sp.dma_start(score_row.rearrange("(n p) -> p n", p=P), sel[:, :]).then_inc(row_out, 16)
            sp.wait_ge(row_out, 16)
            sp.dma_start(row[:, :], score_row[0:N].rearrange("(a n) -> a n", a=1).partition_broadcast(P)
                         ).then_inc(row_in, 16)
            for n in range(RAWS, len(pieces)):
                sp.wait_ge(w_lo, n - RAWS + 1)
                sp.dma_start(raw_piece(n), pieces[n][0]).then_inc(w_loaded[n % RAWS], 16)

        @block.vector
        def _(dve):
            dve.tensor_reduce(top1[:, :], by_batch(scores), AX.X, ALU.max).then_inc(top_part, 1)
            dve.memset(neg_a[:, :], FIRST_NEG_A).then_inc(stepped, 1)
            dve.wait_ge(top_ready, 1)
            with dve.Fori(0, LOOPS // UNROLL) as loop:
                for u in range(UNROLL):
                    i = loop * UNROLL + u
                    dve.wait_ge(stepped, i + 1)
                    dve.tensor_tensor(by_batch(zc), by_batch(scores), each(neg_a), ALU.min).then_inc(cut, 1)
                    dve.tensor_tensor(shift[:, :], top[:, :], neg_a[:, :], ALU.min).then_inc(cut, 1)
                    dve.wait_ge(cut, 2 * i + 2)
                    dve.tensor_tensor(by_batch(zs), by_batch(zc), each(shift), ALU.subtract).then_inc(shifted, 1)
                    dve.wait_ge(exped, i + 1)
                    dve.tensor_reduce(part[:, :], by_batch(e), AX.X, ALU.add).then_inc(parted, 1)
                    dve.wait_ge(logged, i + 1)
                    dve.tensor_tensor(neg_a[:, :], lg[:, :], shift[:, :], ALU.add).then_inc(stepped, 1)
            dve.wait_ge(stepped, LOOPS + 1)
            dve.tensor_tensor(by_batch(zc), by_batch(scores), each(neg_a), ALU.subtract).then_inc(sa_done, 1)
            dve.wait_ge(sa_done, 1)
            dve.tensor_scalar(sa[:, :], zc[:, :], 0.0, None, ALU.min).then_inc(sa_min, 1)
            dve.wait_ge(sel_done, 1)
            dve.tensor_scalar(one_minus[:, :], sel[:, :], -1.0, 1.0, ALU.mult, ALU.add).then_inc(minus_done, 1)
            dve.wait_ge(minus_done, 1)
            dve.tensor_tensor(pay[:, :, 1], sel[:, :], one_minus[:, :], ALU.add).then_inc(weight_done, 1)
            for n in range(RAWS):
                split_lo(dve, n)
            dve.wait_ge(before_ready, 1)
            dve.memset(counts[:, :, :], 0.0).then_inc(counted, 1)
            dve.wait_ge(row_in, 16)
            done = rank_tiles(dve, ranks, junk, row, 0, range(NT_B), counted, 1)
            place_tokens(dve, ranks, 0, counted, done, added, placed)
            for n in range(RAWS, len(pieces)):
                split_lo(dve, n)


ST = CHOSEN // P
USES = KT + MH
GR = 3


def heavy(nc, z_rows, score_row, slots, gamma, b1, b2, out, weights, ranks, consts):
    ident = consts["ident"]
    with ExitStack() as ctx:
        def sb(name, shape, dt=F32, stack=ctx):
            return stack.enter_context(nc.sbuf_tensor("e_" + name, shape, dt))

        sem = lambda name: ctx.enter_context(nc.semaphore("e_" + name))
        w1_hi, w1_lo, w2_hi, w2_lo = weights
        gamma_col, b1_col = sb("gamma", [P, KT]), sb("b1", [P, MH])
        b2_all = sb("b2", [P, D])
        slot = sb("slot", [P, B * ST, 2])
        z = sb("z", [P, 2 * ST, D])
        z_hi, z_lo = sb("z_hi", [P, KT, CH], F32R), sb("z_lo", [P, KT, CH], F32R)
        g = sb("g", [P, 2, CH])
        g_hi, g_lo = sb("g_hi", [P, GR, CH], F32R), sb("g_lo", [P, GR, CH], F32R)
        weight = sb("weight", [P, ST])
        with ExitStack() as first:
            rows = sb("rows", [P, B - 1, N], F32, first)
        rest = sb("rest", [P, ST, D])
        sb("rows_end", [P, (B - 1) * N - ST * D])
        junk = sb("junk", [P, N + P])
        ps = ctx.enter_context(nc.psum_tensor("e_ps", [P, 8, CH], F32))
        YB, MB = 0, 4

        passed = sem("passed")
        small_loaded = sem("small_loaded")
        slot_loaded, rest_loaded = sem("slot_loaded"), sem("rest_loaded")
        z_loaded = [sem(f"z_loaded{b}") for b in range(B)]
        mid_done = sem("mid_done")
        z_is_hi, z_is_lo = sem("z_is_hi"), sem("z_is_lo")
        g_done, g_is_hi, g_is_lo = sem("g_done"), sem("g_is_hi"), sem("g_is_lo")
        used = sem("used")
        b2_added, y_done = sem("b2_added"), sem("y_done")
        y_stored = [sem(f"y_stored{t}") for t in range(ST)]
        weight_ready = sem("weight_ready")
        rows_loaded, counted, added, placed = (sem(n) for n in ("rows_loaded", "counted", "added", "placed"))
        scattered = [sem(f"scattered{b}") for b in range(B)]
        z_ready = sem("z_ready")
        block = ctx.enter_context(nc.Block())
        out_rows = out.rearrange("b n d -> (b n) d")

        @block.sync
        def _(sp):
            def load_slots(b):
                sp.dma_start(slot[:, b * ST:(b + 1) * ST, :], slots[b * N:b * N + CHOSEN, :].rearrange(
                    "(t p) a -> p t a", p=P)).then_inc(slot_loaded, 16)

            load_slots(0)
            sp.dma_start(rows[:, :, :].rearrange("p b n -> p (b n)"),
                         score_row[N:B * N].rearrange("(a n) -> a n", a=1).partition_broadcast(P)
                         ).then_inc(rows_loaded, 16)
            sp.dma_start(gamma_col[:, :], gamma).then_inc(small_loaded, 16)
            sp.dma_start(b1_col[:, :], b1).then_inc(small_loaded, 16)
            sp.dma_start(b2_all[:, :], b2.rearrange("(a d) -> a d", a=1).partition_broadcast(P)
                         ).then_inc(small_loaded, 16)
            for b in range(B):
                sp.wait_ge(z_loaded[b], ST * 16)
                sp.sem_inc(z_ready, 1)
                if b == 0:
                    for other in range(1, B):
                        sp.wait_ge(scattered[other], 16 * NT_B)
                        sp.wait_ge(slot_loaded, 16 * other)
                        load_slots(other)

        @block.gpsimd
        def _(pool):
            def by_token(s):
                return bass.IndirectOffsetOnAxis(slot[:, s, 0:1].bitcast(I32), 0)

            free_from_the_start(pool, (mid_done, USES), (g_done, 2), (g_is_lo, 2), (used, GR),
                                (y_done, ST), (z_is_lo, 2))

            def load_z(b):
                pool.wait_ge(slot_loaded, 16 * (b + 1))
                for s in range(b * ST, (b + 1) * ST):
                    pool.indirect_dma_start(out=z[:, s % (2 * ST), :], out_offset=None, in_=z_rows,
                                            in_offset=by_token(s)).then_inc(z_loaded[b], 16)

            load_z(0)
            for b in range(1, B):
                pool.wait_ge(placed, b)
                scatter_tokens(pool, ranks, slots, b, scattered[b])
            load_z(1)
            for b in range(B):
                for t in range(ST):
                    if b:
                        pool.wait_ge(y_stored[t], b * 16)
                    pool.indirect_dma_start(out=rest[:, t, :], out_offset=None, in_=out_rows,
                                            in_offset=by_token(b * ST + t)).then_inc(rest_loaded, 16)
                if b + 2 < B:
                    pool.wait_ge(mid_done, USES + b * USES + KT)
                    load_z(b + 2)
                for t in range(ST):
                    pool.wait_ge(y_done, ST + b * ST + t + 1)
                    pool.indirect_dma_start(out=out_rows, out_offset=by_token(b * ST + t),
                                            in_=rest[:, t, :], in_offset=None).then_inc(y_stored[t], 16)
            for t in range(ST):
                pool.wait_ge(y_stored[t], B * 16)

        @block.scalar
        def _(act):
            act.wait_ge(small_loaded, 48)
            with act.Fori(0, B) as b:
                for n in range(KT):
                    act.wait_ge(mid_done, USES + b * USES + n + 1)
                    act.activation(z_hi[:, n, :], ps[:, MB + n % 2, :], ACT.Copy,
                                   scale=gamma_col[:, n:n + 1]).then_inc(z_is_hi, 1)
                for m in range(MH):
                    act.wait_ge(mid_done, USES + b * USES + KT + m + 1)
                    act.wait_ge(g_is_lo, b * MH + m + 1)
                    act.activation(g[:, m % 2, :], ps[:, MB + m % 2, :], ACT.Gelu,
                                   bias=b1_col[:, m:m + 1]).then_inc(g_done, 1)

        @block.vector
        def _(dve):
            dve.wait_ge(small_loaded, 48)
            dve.wait_ge(rows_loaded, 16)

            def batch(b, beside=None):
                dve.wait_ge(slot_loaded, 16 * b + 16)
                dve.wait_ge(y_done, b * ST + ST)
                dve.tensor_copy(weight[:, :], slot[:, bass.ds(b * ST, ST), 1]).then_inc(weight_ready, 1)
                for n in range(KT):
                    dve.wait_ge(z_is_hi, b * KT + n + 1)
                    dve.scalar_tensor_tensor(out=z_lo[:, n, :], in0=ps[:, MB + n % 2, :],
                                             scalar=gamma_col[:, n:n + 1], in1=f32(z_hi[:, n, :]),
                                             op0=ALU.mult, op1=ALU.subtract).then_inc(z_is_lo, 1)
                for m in range(MH):
                    r = m % GR
                    dve.wait_ge(g_done, 2 + b * MH + m + 1)
                    if m < GR:
                        dve.wait_ge(used, GR + b * MH)
                    else:
                        dve.wait_ge(used, b * MH + m + 1)
                    dve.tensor_copy(g_hi[:, r, :], g[:, m % 2, :]).then_inc(g_is_hi, 1)
                    dve.wait_ge(g_is_hi, b * MH + m + 1)
                    dve.tensor_tensor(g_lo[:, r, :], g[:, m % 2, :], f32(g_hi[:, r, :]),
                                      ALU.subtract).then_inc(g_is_lo, 1)
                    if beside:
                        beside(m)
                wait_alone(dve, passed, weight_ready, b + 1)
                wait_alone(dve, passed, rest_loaded, b * ST * 16 + ST * 16)
                for t in range(ST):
                    dve.scalar_tensor_tensor(out=rest[:, t, :], in0=b2_all[:, :], scalar=weight[:, t:t + 1],
                                             in1=rest[:, t, :], op0=ALU.mult, op1=ALU.add).then_inc(b2_added, 1)
                dve.wait_ge(b2_added, b * ST + ST)
                wait_alone(dve, passed, used, GR + b * MH + MH)
                for t in range(ST):
                    dve.scalar_tensor_tensor(out=rest[:, t, :], in0=ps[:, YB + t, :],
                                             scalar=weight[:, t:t + 1], in1=rest[:, t, :],
                                             op0=ALU.mult, op1=ALU.add).then_inc(y_done, 1)

            done = 0

            def rank_others(m):
                nonlocal done
                for tile in range(2 * m, min(2 * m + 2, (B - 1) * NT_B)):
                    b, t = tile // NT_B + 1, tile % NT_B
                    if tile == 0:
                        dve.memset(junk[:, :], 0.0).then_inc(counted, 1)
                        done = 1
                    done = rank_tiles(dve, ranks, junk, rows[:, b - 1, :], b, [t], counted, done)
                    if t == NT_B - 1:
                        place_tokens(dve, ranks, b, counted, done, added, placed)

            batch(0, rank_others)
            with dve.Fori(0, B - 1) as i:
                batch(i + 1)

        @block.tensor
        def _(pe):
            with pe.Fori(0, B // 2) as pair:
                for u in range(2):
                    b = pair * 2 + u
                    pe.wait_ge(z_ready, b + 1)
                    for n in range(KT):
                        if n < 2:
                            pe.wait_ge(g_done, b * MH + 2)
                        else:
                            pe.wait_ge(z_is_lo, 2 + b * KT + n - 1)
                        for t in range(ST):
                            last = pe.transpose(ps[:, MB + n % 2, t * P:(t + 1) * P],
                                                z[:, u * ST + t, n * P:(n + 1) * P], ident[:, :])
                        last.then_inc(mid_done, 1)
                    pe.wait_ge(z_is_lo, 2 + b * KT + KT)
                    pe.wait_ge(y_done, b * ST + ST)
                    for m in range(MH + 1):
                        if m < MH:
                            if m >= 2:
                                pe.wait_ge(g_done, b * MH + m + 1)
                            products(pe, ps[:, MB + m % 2, :],
                                     [(w[:, n, m * P:(m + 1) * P], zz[:, n, :])
                                      for w, zz in ((w1_hi, z_hi), (w1_lo, z_hi), (w1_hi, z_lo))
                                      for n in range(KT)]).then_inc(mid_done, 1)
                        if m >= 1:
                            v = m - 1
                            r = v % GR
                            pe.wait_ge(g_is_lo, 2 + b * MH + v + 1)
                            for t in range(ST):
                                for a, (gg, w) in enumerate(((g_hi, w2_hi), (g_lo, w2_hi), (g_hi, w2_lo))):
                                    last = pe.matmul(ps[:, YB + t, :], gg[:, r, t * P:(t + 1) * P], w[:, v, :],
                                                     start=(v == 0 and a == 0), stop=(v == MH - 1 and a == 2),
                                                     skip_group_check=True)
                            last.then_inc(used, 1)


def xattn_ffn(nc, x, ctxT, mask, wq, wkv, wo, rt, gamma_l, w1_l, b1_l, w2_l, b2_l,
              gamma_h, w1_h, b1_h, w2_h, b2_h, out):
    with ExitStack() as ctx:
        def dram(name, shape, dt=F32):
            return nc.dram_tensor(name, shape, dt, kind="Internal").ap()

        ident = ctx.enter_context(nc.sbuf_tensor("ident", [P, P], F32))
        eps = ctx.enter_context(nc.sbuf_tensor("eps", [P, 1], F32))
        scores = ctx.enter_context(nc.sbuf_tensor("scores", [P, B * NT_B], F32))
        consts = dict(ident=ident, eps=eps)
        xnT = dram("xnT", [D, TOK])
        w_split = dram("w_split", [HALVES, 2, P, KT * 3 * HC])
        attT = dram("attT", [D, TOK])
        r_row = dram("r_row", [2, NB])
        z_rows = dram("z_rows", [TOK, D])
        score_row = dram("score_row", [TOK])
        slots = dram("slots", [TOK, 2])
        with ExitStack() as heads:
            first_w = [heads.enter_context(nc.sbuf_tensor(name, [P, KT, 3, HC], F32R))
                       for name in ("w_hi_heads", "w_lo_heads")]
            first_raw = heads.enter_context(nc.sbuf_tensor("raw_0", [P, KT, CH], F32))
            prepare(nc, x, wq, wkv, ctxT, xnT, w_split, first_w, first_raw, consts)
            attend(nc, ctxT, mask, xnT, w_split, first_w, first_raw, attT, r_row, consts)
        light(nc, x, attT, wo, rt, gamma_l, w1_l, b1_l, w2_l, b2_l, z_rows, out, scores, consts)
        weights = [ctx.enter_context(nc.sbuf_tensor(name, shape, F32R)) for name, shape in (
            ("w1_hi", [P, KT, FH]), ("w1_lo", [P, KT, FH]), ("w2_hi", [P, MH, D]), ("w2_lo", [P, MH, D]))]
        ranks = {name: ctx.enter_context(nc.sbuf_tensor(name, shape, dt)) for name, shape, dt in (
            ("before", [P, P], F32),
            ("sel", [P, B * NT_B], F32),
            ("pay", [P, B * NT_B, 2], F32),
            ("counts", [P, 3, B * NT_B], F32),
            ("rank1", [P, B * NT_B], F32), ("rank", [P, B * NT_B], F32),
            ("place", [P, B * NT_B], I32))}
        route(nc, scores, score_row, slots, w1_h, w2_h, weights, ranks)
        heavy(nc, z_rows, score_row, slots, gamma_h, b1_h, b2_h, out, weights, ranks, consts)


def kernel(x, ctx_1024, mask_BxSxS2_bf1, L0_xattn_Wq, L0_xattn_Wkv, L0_xattn_Wo, L0_ffn_routing_token,
           L0_ffn_gamma_l, L0_ffn_w1_l, L0_ffn_b1_l, L0_ffn_w2_l, L0_ffn_b2_l, L0_ffn_gamma_h,
           L0_ffn_w1_h, L0_ffn_b1_h, L0_ffn_w2_h, L0_ffn_b2_h):
    import concourse.bacc as bacc
    from concourse.bass_utils import run_bass_kernel_spmd

    def columns(v):
        return np.ascontiguousarray(np.asarray(v).reshape(-1, P).T)

    def turned(w):
        return np.ascontiguousarray(np.asarray(w).T)

    arrays = {
        "x": np.asarray(x),
        "ctxT": np.ascontiguousarray(np.asarray(ctx_1024).transpose(0, 2, 1)),
        "mask": np.asarray(mask_BxSxS2_bf1).view(np.uint8),
        "wq": np.asarray(L0_xattn_Wq), "wkv": np.asarray(L0_xattn_Wkv), "wo": np.asarray(L0_xattn_Wo),
        "rt": np.asarray(L0_ffn_routing_token),
        "gamma_l": columns(L0_ffn_gamma_l), "w1_l": turned(L0_ffn_w1_l), "b1_l": columns(L0_ffn_b1_l),
        "w2_l": turned(L0_ffn_w2_l), "b2_l": np.asarray(L0_ffn_b2_l),
        "gamma_h": columns(L0_ffn_gamma_h), "w1_h": turned(L0_ffn_w1_h), "b1_h": columns(L0_ffn_b1_h),
        "w2_h": turned(L0_ffn_w2_h), "b2_h": np.asarray(L0_ffn_b2_h),
    }
    nc = bacc.Bacc("TRN2", target_bir_lowering=False, num_devices=1)
    aps = {n: nc.dram_tensor(n, a.shape, mybir.dt.from_np(a.dtype), kind="ExternalInput").ap()
           for n, a in arrays.items()}
    out = nc.dram_tensor("out", (B, N, D), F32, kind="ExternalOutput").ap()
    xattn_ffn(nc, out=out, **aps)
    r = run_bass_kernel_spmd(nc, [arrays], core_ids=[0])
    return r.results[0]["out"]
```
